# Optimizing a Trainium2 kernel written in Bass

```python
import numpy as np
import jax
import jax.numpy as jnp

def _softmax(x, axis=-1):
    return jax.nn.softmax(x, axis=axis)

def _gelu(x):
    return jax.nn.gelu(x, approximate=True)

def _silu(x):
    return jax.nn.silu(x)

def _sigmoid(x):
    return jax.nn.sigmoid(x)

def _layernorm(x, axis=-1, eps=1e-05):
    m = jnp.mean(x, axis=axis, keepdims=True)
    v = jnp.var(x, axis=axis, keepdims=True)
    return (x - m) / jnp.sqrt(v + eps)

def _scatter_add(tgt, idx, src, axis=0):
    return tgt.at[idx].add(src)

def _segment_sum(src, seg, n):
    return jax.ops.segment_sum(src, seg, n)
kernel_name = 'mk_xattn_ffn_d1_seqx_r2_7a6f9c'

def setup_inputs(seed: int=0):
    np.random.seed(seed)
    _w = jnp.asarray

    def _rec_inputs():
        import jax
        import jax.numpy as jnp
        _rk = jax.random.key(seed)
        x = -0.0003929 + 0.9999 * jax.random.normal(jax.random.fold_in(_rk, 1), (8, 1024, 512), jnp.float32)
        _lenS = 1024 - jax.random.randint(jax.random.fold_in(_rk, 7), (8,), 0, max(1, 1024 // 4) + 1, jnp.int32)
        _lenS2 = 1601 - jax.random.randint(jax.random.fold_in(_rk, 8), (8,), 0, max(1, 1601 // 4) + 1, jnp.int32)
        _ctx_2048P = jax.random.normal(jax.random.fold_in(_rk, 11), (8, 16, 1024), jnp.float32)
        _ctx_2048c = jax.random.dirichlet(jax.random.fold_in(_rk, 511), 0.3 * jnp.ones((16,), jnp.float32), (8, 1601))
        _ctx_2048t = jnp.einsum('bsk,bkd->bsd', _ctx_2048c, _ctx_2048P)
        _ctx_2048t = _ctx_2048t * jax.lax.rsqrt(jnp.mean(jnp.square(_ctx_2048t)) + 1e-12) * 0.953939
        ctx_2048 = 4.13588e-05 + 0.999923 * (_ctx_2048t + 0.3 * jax.random.normal(jax.random.fold_in(_rk, 611), (8, 1601, 1024), jnp.float32))
        _validS = jnp.arange(1024)[None, :] < _lenS[:, None]
        _validS2 = jnp.arange(1601)[None, :] < _lenS2[:, None]
        _causal = jnp.tril(jnp.ones((1024, 1024), dtype=bool))
        mask_BxS2_if0 = jnp.where(jnp.ones((8, 1601), dtype=bool), 4, 0).astype(jnp.int32)
        return (x, ctx_2048, mask_BxS2_if0)
    x, ctx_2048, mask_BxS2_if0 = _rec_inputs()

    def _L0_xattn_setup():
        import jax, jax.numpy as jnp
        import numpy as np
        B, L, P = (4, 2048, 512)
        D_MODEL = 512
        D_GLOBAL = 1024
        HEADDIM = 32
        EPSILON = 0.001
        RMS_EPS = 1e-05

        def rmsnorm(x, g, eps=RMS_EPS):
            var = jnp.mean(jnp.square(x), axis=-1, keepdims=True)
            return x * jax.lax.rsqrt(var + eps) * g

        def _hnet_depool(h, h_patch_full, patch_lens):
            h_patch = h_patch_full[..., :D_MODEL]
            bsz, plen = (h_patch.shape[0], h_patch.shape[1])
            seqlen = h.shape[1]
            logp = jnp.full((bsz, plen), -EPSILON, dtype=jnp.float32)
            bidx = jnp.cumsum(patch_lens, axis=1) - 1
            boundary_mask = jnp.zeros((bsz, seqlen), dtype=jnp.int32)
            boundary_mask = boundary_mask.at[jnp.arange(bsz)[:, None], bidx].set(1)
            dt = (-jnp.log(-jnp.expm1(logp))).astype(h_patch.dtype)
            x = h_patch / dt[..., None]
            n_heads = D_MODEL // HEADDIM
            A = -jnp.ones((n_heads,), dtype=jnp.float32)
            bcoef = jnp.exp(logp).astype(h_patch.dtype)
            x4 = x.reshape(bsz, plen, n_heads, HEADDIM)
            a = jnp.exp(dt[:, :, None] * A[None, None, :])
            u = (dt * bcoef)[:, :, None, None] * x4
            a_b = jnp.broadcast_to(a[..., None], u.shape)

            def comb(lft, rgt):
                aL, uL = lft
                aR, uR = rgt
                return (aL * aR, uL * aR + uR)
            _, s = jax.lax.associative_scan(comb, (a_b, u), axis=1)
            depool = s.reshape(bsz, plen, D_MODEL)
            plug = jnp.clip(jnp.cumsum(boundary_mask, axis=1) - 1, 0, plen - 1)
            depool_out = depool[jnp.arange(bsz)[:, None], plug]
            return depool_out + h
        key = jax.random.key(seed)
        k1, k2, k3, k4 = jax.random.split(key, 4)
        embeds = jax.random.normal(k1, (B, L, D_MODEL), dtype=jnp.float32)
        patch_embeds = jax.random.normal(k2, (B, P, D_GLOBAL), dtype=jnp.float32)
        patch_lens = jnp.full((B, P), L // P, dtype=jnp.int64)
        W_in = jax.random.normal(k3, (D_MODEL, D_MODEL), dtype=jnp.float32) * 0.02
        b_in = jnp.zeros((D_MODEL,), dtype=jnp.float32)
        g_res = jnp.ones((D_MODEL,), dtype=jnp.float32)
        g_init = jnp.ones((D_GLOBAL,), dtype=jnp.float32)
        return {'embeds': embeds, 'patch_embeds': patch_embeds, 'patch_lens': patch_lens, 'W_in': W_in, 'b_in': b_in, 'g_res': g_res, 'g_init': g_init}
    _L0_xattn_all = _L0_xattn_setup()
    _L0_xattn_in = {k: v for k, v in _L0_xattn_all.items() if k in ('W_in', 'b_in', 'g_res', 'g_init')}
    del _L0_xattn_all

    def _L0_ffn_setup():
        import jax, jax.numpy as jnp
        import numpy as np
        from jax import lax
        H, DK, DV, N_EXP, CHUNK = (8, 64, 64, 4, 64)
        LORA, GATE_LR = (64, 16)
        NORMALIZER = 16.0
        EPS = 1e-05

        def chunk_gla(q, k, v, gk, C=CHUNK):
            L, h, dk = q.shape
            dv = v.shape[-1]
            nc = L // C
            qc, kc, vc, gc = (t.reshape(nc, C, h, -1) for t in (q, k, v, gk))
            g = jnp.cumsum(gc, axis=1)
            g_last = g[:, -1]
            qg = qc * jnp.exp(g)
            kg = kc * jnp.exp(-g)
            A = jnp.einsum('cthd,cshd->chts', qg, kg)
            A = A * jnp.tril(jnp.ones((C, C), q.dtype))
            o_intra = jnp.einsum('chts,cshe->cthe', A, vc)
            k_out = kc * jnp.exp(g_last[:, None] - g)
            chunk_kv = jnp.einsum('cthd,cthe->chde', k_out, vc)
            decay = jnp.exp(g_last)

            def step(S, inp):
                kv, dec, qg_c = inp
                o_inter = jnp.einsum('thd,hde->the', qg_c, S)
                return (S * dec[..., None] + kv, o_inter)
            S0 = jnp.zeros((h, dk, dv), q.dtype)
            _, o_inter = lax.scan(step, S0, (chunk_kv, decay, qg))
            return (o_intra + o_inter).reshape(L, h, dv)
        key = jax.random.key(seed)
        ks = jax.random.split(key, 20)
        B, L, Dh = (1, 2048, 512)
        KD, VD = (H * DK, H * DV)
        w = lambda i, shape: jax.random.normal(ks[i], shape, jnp.float32) * 0.02
        return {'x': jax.random.normal(ks[0], (B, L, Dh), jnp.float32), 'Wq': w(1, (Dh, KD)), 'Wk': w(2, (Dh, KD)), 'Wv': w(3, (Dh, VD)), 'Wqa': w(4, (Dh, LORA)), 'Wqb': w(5, (LORA, KD)), 'Wka': w(6, (Dh, LORA)), 'Wkb': w(7, (LORA, KD)), 'Wg1a': w(8, (Dh, GATE_LR)), 'Wg1b': w(9, (GATE_LR, KD)), 'bg1': jnp.zeros((KD,), jnp.float32), 'Wg2a': w(10, (Dh, GATE_LR)), 'Wg2b': w(11, (GATE_LR, KD)), 'bg2': jnp.zeros((KD,), jnp.float32), 'We': w(12, (Dh, N_EXP)), 'Wga': w(13, (Dh, LORA)), 'Wgb': w(14, (LORA, VD)), 'norm_w': jnp.ones((DV,), jnp.float32), 'Wo': w(15, (VD, Dh))}
    _L0_ffn_all = _L0_ffn_setup()
    _L0_ffn_in = {k: v for k, v in _L0_ffn_all.items() if k in ('Wq', 'Wk', 'Wv', 'Wqa', 'Wqb', 'Wka', 'Wkb', 'Wg1a', 'Wg1b', 'bg1', 'Wg2a', 'Wg2b', 'bg2', 'We', 'Wga', 'Wgb', 'norm_w', 'Wo')}
    del _L0_ffn_all
    return {'x': x, 'ctx_2048': ctx_2048, 'mask_BxS2_if0': mask_BxS2_if0, 'L0_xattn_W_in': _L0_xattn_in['W_in'], 'L0_xattn_b_in': _L0_xattn_in['b_in'], 'L0_xattn_g_res': _L0_xattn_in['g_res'], 'L0_xattn_g_init': _L0_xattn_in['g_init'], 'L0_ffn_Wq': _L0_ffn_in['Wq'], 'L0_ffn_Wk': _L0_ffn_in['Wk'], 'L0_ffn_Wv': _L0_ffn_in['Wv'], 'L0_ffn_Wqa': _L0_ffn_in['Wqa'], 'L0_ffn_Wqb': _L0_ffn_in['Wqb'], 'L0_ffn_Wka': _L0_ffn_in['Wka'], 'L0_ffn_Wkb': _L0_ffn_in['Wkb'], 'L0_ffn_Wg1a': _L0_ffn_in['Wg1a'], 'L0_ffn_Wg1b': _L0_ffn_in['Wg1b'], 'L0_ffn_bg1': _L0_ffn_in['bg1'], 'L0_ffn_Wg2a': _L0_ffn_in['Wg2a'], 'L0_ffn_Wg2b': _L0_ffn_in['Wg2b'], 'L0_ffn_bg2': _L0_ffn_in['bg2'], 'L0_ffn_We': _L0_ffn_in['We'], 'L0_ffn_Wga': _L0_ffn_in['Wga'], 'L0_ffn_Wgb': _L0_ffn_in['Wgb'], 'L0_ffn_norm_w': _L0_ffn_in['norm_w'], 'L0_ffn_Wo': _L0_ffn_in['Wo']}

def reference(x, ctx_2048, mask_BxS2_if0, L0_xattn_W_in, L0_xattn_b_in, L0_xattn_g_res, L0_xattn_g_init, L0_ffn_Wq, L0_ffn_Wk, L0_ffn_Wv, L0_ffn_Wqa, L0_ffn_Wqb, L0_ffn_Wka, L0_ffn_Wkb, L0_ffn_Wg1a, L0_ffn_Wg1b, L0_ffn_bg1, L0_ffn_Wg2a, L0_ffn_Wg2b, L0_ffn_bg2, L0_ffn_We, L0_ffn_Wga, L0_ffn_Wgb, L0_ffn_norm_w, L0_ffn_Wo):
    import jax
    import jax.numpy as jnp

    def _L0_xattn_ref(embeds, patch_embeds, patch_lens, W_in, b_in, g_res, g_init):
        import jax, jax.numpy as jnp
        import numpy as np
        B, L, P = (4, 2048, 512)
        D_MODEL = 512
        D_GLOBAL = 1024
        HEADDIM = 32
        EPSILON = 0.001
        RMS_EPS = 1e-05

        def rmsnorm(x, g, eps=RMS_EPS):
            var = jnp.mean(jnp.square(x), axis=-1, keepdims=True)
            return x * jax.lax.rsqrt(var + eps) * g

        def _hnet_depool(h, h_patch_full, patch_lens):
            h_patch = h_patch_full[..., :D_MODEL]
            bsz, plen = (h_patch.shape[0], h_patch.shape[1])
            seqlen = h.shape[1]
            logp = jnp.full((bsz, plen), -EPSILON, dtype=jnp.float32)
            bidx = jnp.cumsum(patch_lens, axis=1) - 1
            boundary_mask = jnp.zeros((bsz, seqlen), dtype=jnp.int32)
            boundary_mask = boundary_mask.at[jnp.arange(bsz)[:, None], bidx].set(1)
            dt = (-jnp.log(-jnp.expm1(logp))).astype(h_patch.dtype)
            x = h_patch / dt[..., None]
            n_heads = D_MODEL // HEADDIM
            A = -jnp.ones((n_heads,), dtype=jnp.float32)
            bcoef = jnp.exp(logp).astype(h_patch.dtype)
            x4 = x.reshape(bsz, plen, n_heads, HEADDIM)
            a = jnp.exp(dt[:, :, None] * A[None, None, :])
            u = (dt * bcoef)[:, :, None, None] * x4
            a_b = jnp.broadcast_to(a[..., None], u.shape)

            def comb(lft, rgt):
                aL, uL = lft
                aR, uR = rgt
                return (aL * aR, uL * aR + uR)
            _, s = jax.lax.associative_scan(comb, (a_b, u), axis=1)
            depool = s.reshape(bsz, plen, D_MODEL)
            plug = jnp.clip(jnp.cumsum(boundary_mask, axis=1) - 1, 0, plen - 1)
            depool_out = depool[jnp.arange(bsz)[:, None], plug]
            return depool_out + h
        h = rmsnorm(embeds, g_res)
        h = jnp.einsum('bld,ed->ble', h, W_in) + b_in
        h_patch = rmsnorm(patch_embeds, g_init)
        return _hnet_depool(h, h_patch, patch_lens)

    def _L0_ffn_ref(x, Wq, Wk, Wv, Wqa, Wqb, Wka, Wkb, Wg1a, Wg1b, bg1, Wg2a, Wg2b, bg2, We, Wga, Wgb, norm_w, Wo):
        import jax, jax.numpy as jnp
        import numpy as np
        from jax import lax
        H, DK, DV, N_EXP, CHUNK = (8, 64, 64, 4, 64)
        LORA, GATE_LR = (64, 16)
        NORMALIZER = 16.0
        EPS = 1e-05

        def chunk_gla(q, k, v, gk, C=CHUNK):
            L, h, dk = q.shape
            dv = v.shape[-1]
            nc = L // C
            qc, kc, vc, gc = (t.reshape(nc, C, h, -1) for t in (q, k, v, gk))
            g = jnp.cumsum(gc, axis=1)
            g_last = g[:, -1]
            qg = qc * jnp.exp(g)
            kg = kc * jnp.exp(-g)
            A = jnp.einsum('cthd,cshd->chts', qg, kg)
            A = A * jnp.tril(jnp.ones((C, C), q.dtype))
            o_intra = jnp.einsum('chts,cshe->cthe', A, vc)
            k_out = kc * jnp.exp(g_last[:, None] - g)
            chunk_kv = jnp.einsum('cthd,cthe->chde', k_out, vc)
            decay = jnp.exp(g_last)

            def step(S, inp):
                kv, dec, qg_c = inp
                o_inter = jnp.einsum('thd,hde->the', qg_c, S)
                return (S * dec[..., None] + kv, o_inter)
            S0 = jnp.zeros((h, dk, dv), q.dtype)
            _, o_inter = lax.scan(step, S0, (chunk_kv, decay, qg))
            return (o_intra + o_inter).reshape(L, h, dv)
        B, L, Dh = x.shape
        scale = DK ** (-0.5)
        q1 = (x @ Wq).reshape(B, L, H, DK) * scale
        k1 = (x @ Wk).reshape(B, L, H, DK)
        v = (x @ Wv).reshape(B, L, H, DV)
        q2 = (x @ Wqa @ Wqb).reshape(B, L, H, DK) * scale
        k2 = jax.nn.softmax((x @ Wka @ Wkb).reshape(B, L, H, DK), axis=-1)
        gk1 = (jax.nn.log_sigmoid(x @ Wg1a @ Wg1b + bg1) / NORMALIZER).reshape(B, L, H, DK)
        gk2 = (jax.nn.log_sigmoid(x @ Wg2a @ Wg2b + bg2) / NORMALIZER).reshape(B, L, H, DK)
        e = jax.nn.softmax(x @ We, axis=-1)
        _, idx = lax.top_k(e, 1)
        mask = jax.nn.one_hot(idx, N_EXP, dtype=x.dtype).sum(-2)
        rw = e * mask
        fac = jnp.swapaxes(rw, 1, 2)[:, :, :, None, None]
        mfac = jnp.swapaxes(mask, 1, 2)[:, :, :, None, None]
        q_e = q2[:, None] * fac
        k_e = k2[:, None] * fac
        gk_e = gk2[:, None] * mfac
        gla_b = jax.vmap(chunk_gla)
        o_dense = gla_b(q1, k1, v, gk1)
        gla_be = jax.vmap(jax.vmap(chunk_gla, in_axes=(0, 0, None, 0)))
        o_sparse = gla_be(q_e, k_e, v, gk_e).sum(axis=1)
        o = o_dense + o_sparse
        g = (x @ Wga @ Wgb).reshape(B, L, H, DV)
        o = o * lax.rsqrt(jnp.mean(o * o, axis=-1, keepdims=True) + EPS) * norm_w
        o = o * (g * jax.nn.sigmoid(g))
        return o.reshape(B, L, H * DV) @ Wo
    x = x + _L0_xattn_ref(_layernorm(x, axis=-1), ctx_2048, mask_BxS2_if0, L0_xattn_W_in, L0_xattn_b_in, L0_xattn_g_res, L0_xattn_g_init)
    x = x + _L0_ffn_ref(_layernorm(x, axis=-1), L0_ffn_Wq, L0_ffn_Wk, L0_ffn_Wv, L0_ffn_Wqa, L0_ffn_Wqb, L0_ffn_Wka, L0_ffn_Wkb, L0_ffn_Wg1a, L0_ffn_Wg1b, L0_ffn_bg1, L0_ffn_Wg2a, L0_ffn_Wg2b, L0_ffn_bg2, L0_ffn_We, L0_ffn_Wga, L0_ffn_Wgb, L0_ffn_norm_w, L0_ffn_Wo)
    return x

_drawn_inputs = setup_inputs


def setup_inputs(seed=0):
    import zlib

    import numpy as np

    out = dict(_drawn_inputs(seed))
    spreads = {'L0_xattn_b_in': (0.0, 0.1),
     'L0_xattn_g_res': (1.0, 0.2),
     'L0_xattn_g_init': (1.0, 0.2),
     'L0_ffn_bg1': (0.0, 0.8),
     'L0_ffn_bg2': (0.0, 0.8),
     'L0_ffn_norm_w': (1.0, 0.6)}
    factors = {'L0_ffn_Wq': 5.019,
     'L0_ffn_Wk': 4.981,
     'L0_ffn_Wv': 5.046,
     'L0_ffn_Wqa': 8.0,
     'L0_ffn_Wqb': 8.0,
     'L0_ffn_Wka': 8.0,
     'L0_ffn_Wkb': 8.0,
     'L0_ffn_Wg1a': 8.0,
     'L0_ffn_Wg1b': 8.0,
     'L0_ffn_Wg2a': 8.0,
     'L0_ffn_Wg2b': 8.0,
     'L0_ffn_We': 8.0,
     'L0_ffn_Wga': 5.009,
     'L0_ffn_Wgb': 5.026,
     'L0_ffn_Wo': 5.047}
    for name, (base, spread) in spreads.items():
        noise = np.random.default_rng([zlib.crc32(name.encode()), seed]).standard_normal(out[name].shape)
        drawn = base * np.exp(spread * noise) if base else spread * noise
        out[name] = jnp.asarray(drawn.astype(out[name].dtype))
    for name, factor in factors.items():
        out[name] = (out[name] * factor).astype(out[name].dtype)
    return out
```

```python
import math
from contextlib import ExitStack

import concourse.bass as bass
from concourse import mybir

ALU = mybir.AluOpType
ACT = mybir.ActivationFunctionType
AX = mybir.AxisListType
F32 = mybir.dt.float32
BF16 = mybir.dt.bfloat16
I32 = mybir.dt.int32

LOOP_FROM, UNROLL = 4, 2
P = 128
D = 512
KC = D // P
H, DK = 8, 64
PAIRS = H // 2
NE = 4
SLOTS = 1 + NE
LORA, GLR = 64, 16
LN_EPS = 1e-5
RMS_EPS = 1e-5
NORMALIZER = 16.0
SCALE = DK ** -0.5
LOGP = -0.001
B_COEF = math.exp(LOGP)
SMALL = 5 + 5 + 5 + 2
LN_A = math.log(-math.expm1(LOGP))


def xattn_ffn(nc, x, ctx_in, lens, w_in, b_in, g_res, g_init, wq, wk, wv, wqa, wqb, wka, wkb,
              wg1a, wg1b, bg1, wg2a, wg2b, bg2, we, wga, wgb, norm_w, wo, out):
    B, S, _ = x.shape
    PLEN, DG = ctx_in.shape[1], ctx_in.shape[2]
    TB = S // P
    NT = B * TB
    LC = -(-PLEN // P)
    LCF = PLEN // P
    TAIL = PLEN - LCF * P
    NCOL = B * LC
    x_rows = x.rearrange("b s d -> (b s) d")
    out_rows = out.rearrange("b s d -> (b s) d")
    ctx_rows = ctx_in.rearrange("b p d -> (b p) d")

    stack = ExitStack()
    with stack:
        def sb(name, shape, dt=F32):
            return stack.enter_context(nc.sbuf_tensor(name, shape, dt))

        def sem(name):
            return stack.enter_context(nc.semaphore(name))

        bank = [stack.enter_context(nc.psum_tensor(f"bank{i}", [P, D], F32)) for i in range(8)]

        ident = sb("ident", [P, P])
        triu = sb("triu", [P, P])
        triu_b = sb("triu_b", [P, P], BF16)
        ones = sb("ones", [P, P])
        ones_b = sb("ones_b", [P, P], BF16)
        cum_mat = sb("cum_mat", [P, P])
        half_z = sb("half_z", [P, 2])
        sel_e = sb("sel_e", [NE, NE, P], BF16)
        rank = sb("rank", [P, NE])
        minus_half = sb("minus_half", [P, H])
        row_no = sb("row_no", [P, 1])
        carry_bias = sb("carry_bias", [P, 1])
        last_row = sb("last_row", [P, 1])
        bias_rows = sb("bias_rows", [P, 1])
        keep = sb("keep", [P, NT + UNROLL])
        w_in_s = sb("w_in_s", [P, KC, D])
        wq_s = sb("wq_s", [P, KC, D])
        wk_s = sb("wk_s", [P, KC, D])
        wv_s = sb("wv_s", [P, KC, D])
        wo_s = sb("wo_s", [P, KC, D])
        w_low = sb("w_low", [P, KC, 2 * P])
        we_s = sb("we_s", [P, KC, NE])
        w_up = sb("w_up", [P, 2, D])
        g_res_s = sb("g_res_s", [P, KC])
        b_in_s = sb("b_in_s", [P, D])
        g_init_s = sb("g_init_s", [P, D])
        norm_s = sb("norm_s", [P, DK])
        bound = sb("bound", [P, NT + UNROLL])
        started = sb("started", [P, NT + UNROLL])
        unstarted = sb("unstarted", [P, NT + UNROLL])
        first_row = sb("first_row", [1, NT], I32)

        lens_rows = sb("lens_rows", [P, P], I32)

        xs = sb("xs", [P, 2, D])
        ctx = sb("ctx", [P, 2, DG])
        stat = sb("stat", [P, 6])
        stat2 = sb("stat2", [P, 6])
        mv = sb("mv", [P, 2])
        mv2 = sb("mv2", [P, 2])
        var_a = sb("var_a", [P, 2])
        rs_a = sb("rs_a", [P, 2])
        ctx_ss = sb("ctx_ss", [P, 1])
        var2 = sb("var2", [P, 1])
        idle = sb("idle", [P, 1])
        rs2 = sb("rs2", [P, 1])
        xhat = sb("xhat", [P, D])
        xhat_t = sb("xhat_t", [P, KC, P])
        tri_bound = sb("tri_bound", [P, P], BF16)
        ctx_bin = sb("ctx_bin", [P, DG], BF16)
        dist = sb("dist", [P, P])
        dist_p = sb("dist_p", [P, P])
        decay_w = sb("decay_w", [P, P])
        carry_y = sb("carry_y", [P, P])
        in_past = sb("in_past", [P, P])
        w_depool = sb("w_depool", [P, P])
        w_carry = sb("w_carry", [P, P])
        depool = sb("depool", [P, 2, D])
        x_plus_b = sb("x_plus_b", [P, D])
        dep_g = sb("dep_g", [P, D])
        resid = sb("resid", [P, D])
        x1 = sb("x1", [P, 2, D])
        xn = sb("xn", [P, D])
        xn_t = sb("xn_t", [P, 2, KC, P])
        x1_late = sb("x1_late", [P, 2, D])
        low = sb("low", [P, 2 * P])
        l_max = sb("l_max", [P, 1])
        l_sub = sb("l_sub", [P, NE])
        l_exp = sb("l_exp", [P, NE])
        l_sum = sb("l_sum", [P, 1])
        l_rank = sb("l_rank", [P, NE])
        l_best = sb("l_best", [P, 1])
        onehot = sb("onehot", [P, NE])
        fac = sb("fac", [P, 1])
        fac_q = sb("fac_q", [P, 1])
        onehot_t = sb("onehot_t", [NE, P], BF16)
        mask2 = sb("mask2", [P, 2, P])
        cum_mat2 = sb("cum_mat2", [P, P])
        z2_half = sb("z2_half", [P, 2, NE])
        mask_row = sb("mask_row", [P, NE, P])
        q1 = sb("q1", [P, D])
        k1 = sb("k1", [P, D])
        q2 = sb("q2", [P, D])
        v = sb("v", [P, 2, D])
        v_e = sb("v_e", [P, NE, D])
        gate_l = sb("gate_l", [P, 3, D])
        g_norm = sb("g_norm", [P, D])
        sig = sb("sig", [P, D])
        g_silu = sb("g_silu", [P, 2, D])
        k2_max = sb("k2_max", [P, H])
        k2_exp = sb("k2_exp", [P, D])
        k2_sum = sb("k2_sum", [P, H])
        k2_rec = sb("k2_rec", [P, H])
        k2_fac = sb("k2_fac", [P, H])
        e1p = sb("e1p", [P, D])
        e1m = sb("e1m", [P, D])
        e2p = sb("e2p", [P, D])
        e2m = sb("e2m", [P, D])
        dec = sb("dec", [P, 2, 2, PAIRS, SLOTS])
        dec_first = sb("dec_first", [P, 2, PAIRS, SLOTS])
        kt1 = sb("kt1", [P, 2, D])
        kt2 = sb("kt2", [P, 2, D])
        q1_t = sb("q1_t", [P, PAIRS, P])
        k1_t = sb("k1_t", [P, PAIRS, P])
        q2_t = sb("q2_t", [P, PAIRS, P])
        k2_t = sb("k2_t", [P, PAIRS, P])
        q2_te = sb("q2_te", [P, NE, PAIRS, P])
        att1 = sb("att1", [P, 2, PAIRS, P])
        att2 = sb("att2", [P, 2, PAIRS, P])
        state = sb("state", [P, PAIRS, SLOTS, DK])
        o = sb("o", [P, D])
        o_sq = sb("o_sq", [P, D])
        o_ss = sb("o_ss", [P, H])
        o_var = sb("o_var", [P, H])
        o_rs = sb("o_rs", [P, H])
        o_n = sb("o_n", [P, D])
        o_t = sb("o_t", [P, KC, P])
        res = sb("res", [P, 2, D])
        lens_i = lens_rows[0:NCOL, :]
        lens_i32 = lens_i
        lens_f = q2_te[0:NCOL, 0, 1, :]
        lens_t = q2_te[:, 0, 2, 0:NCOL]
        totals = q2_te[:, 0, 3, 0:NCOL].rearrange("p (b c) -> p b c", b=B)
        offs = q2_te[:, 1, 0, 0:NCOL].rearrange("p (b c) -> p b c", b=B)
        ends = q2_te[:, 1, 1, 0:NCOL].rearrange("p (b c) -> p b c", b=B)
        wrapped = q2_te[:, 1, 2, 0:NCOL]
        hi_no = q2_te[:, 1, 3, 0:NCOL]
        w_in_rows = ctx[:, :, :].rearrange("p a n -> p (a n)").rearrange("p (c n) -> p c n", c=KC)
        lo_no = q2_te[:, 2, 0, 0:NCOL]
        thr = q2_te[:, 2, 1, 0:TB + 1]
        col_no = q2_te[:, 2, 2, :]
        row_start = q2_te[:, 2, 3, 0:NT].rearrange("p (b t) -> p b t", b=B)
        before = q2_te[:, 3, 0, 0:NT].rearrange("p (b t) -> p b t", b=B)
        tile_tot = q2_te[:, 3, 1, 0:NT].rearrange("p (b t) -> p b t", b=B)
        row_first = q2_te[:, 3, 2, 0:NT].rearrange("p (b t) -> p b t", b=B)
        reached = v_e[:, 0:2, :].bitcast(BF16).rearrange("p a n -> p (a n)")[:, 0:NCOL * (TB + 1)]\
            .rearrange("p (c j) -> p c j", j=TB + 1)
        hi_hot = v_e[:, 2:4, :].bitcast(BF16).rearrange("p a n -> p (a n)")[:, 0:NCOL * TB]\
            .rearrange("p (c j) -> p c j", j=TB)
        lo_hot = [att1[:, :, :, :].bitcast(BF16).rearrange("p j a n -> p (j a n)")[:, 0:LC * P],
                  gate_l[:, :, :].bitcast(BF16).rearrange("p a n -> p (a n)")[:, 0:LC * P]]
        lo_hot = [h.rearrange("p (c n) -> p c n", n=P) for h in lo_hot]

        s = {n: sem(n) for n in """
            consts_made consts_selected weights_in lens_in small_in lens_float lens_turned lens_summed
            prologue_step g_scaled counts_ready w_in_turned hot_ready hot_used totals_ready tables_ready
            x_stats x_mean x_var a_rs xhat_made xhat_turned xhat_t_made
            ctx_sq ctx_var tri_made cum_made dist_made dist_pos decay_made carry_made past_made dep_w_made
            dep_made dep_copied xb_made dep_scaled resid_made w_made x1_made x1_stats x1_mean x1_var x1_rs
            xn_made xn_turned xn_t_made x1_moved
            low_made low_copied l_max_made l_read l_sub_made l_rank_made l_best_made onehot_made l_exp_made fac_made facq_made
            q1_made k1_made v_made q1_copied k1_copied v_copied
            q2_made k2_made q2_copied k2_maxed k2_subbed k2_exped k2_summed k2_reced k2_faced
            g_normed sig_made silu_made
            hot_turned hot_t_made same_made same_used z2_made masks_made masks_copied
            gt1_made gt2_made dec_made gt1_exped gt2_exped dec_exped dec_kept
            qt1_made qt2_made k2d_made kt1_made kt2_made
            q1_turned k1_turned q2_turned k2_turned q1_t_made k1_t_made q2_t_made k2_t_made q2_te_made
            a1_made a2_made a1e_masked a1o_masked a2e_masked a2o_masked att_summed state_first o_made oe_copied o_copied o_sq_made kv0_made kv1_made kvd_made kv0_added kv1_added
            state_added state_made o_summed o_var_made o_rs_made o_gated_made o_n_made
            o_turned o_t_made y_made res_made
            """.split()}

        z_made = [sem(f"z_made{j}") for j in range(3)]
        z_min = [sem(f"z_min{j}") for j in range(3)]
        z_exp = [sem(f"z_exp{j}") for j in range(3)]
        z_ln = [sem(f"z_ln{j}") for j in range(3)]
        l_made = [sem(f"l_made{j}") for j in range(3)]

        x_in = [sem(f"x_in{j}") for j in range(2)]
        ctx_loaded = [sem(f"ctx_loaded{j}") for j in range(2)]
        res_out = [sem(f"res_out{j}") for j in range(2)]

        def moved(eng, semaphores, tile, par):
            if not isinstance(tile, int) or tile >= 0:
                eng.wait_ge(semaphores[par], (tile - par) * 8 + 16)

        def at(eng, semaphore, tile):
            if isinstance(tile, int):
                if tile < 0:
                    return
                tile = min(tile, NT - 1)
            eng.wait_ge(semaphore, tile + 1)

        def heads(a):
            return a.rearrange("p (h d) -> p h d", h=H)

        def over_heads(col):
            return col.unsqueeze(2).to_broadcast([P, H, DK])


        def run(eng, step):
            for i in range(LOOP_FROM):
                step(i, i % UNROLL)
            with eng.Fori(LOOP_FROM, NT, UNROLL) as i:
                for u in range(UNROLL):
                    step(i + u, u)
            for i in range(NT, NT + 2):
                step(i, i % UNROLL)

        def live(tile):
            return not isinstance(tile, int) or 0 <= tile < NT

        block = stack.enter_context(nc.Block())

        @block.sync
        def _(sp):
            sp.wait_ge(s["consts_made"], 1)
            for b in range(B):
                sp.dma_start(lens_i[b * LCF:(b + 1) * LCF, :],
                             lens[b, 0:LCF * P].rearrange("(c k) -> c k", k=P)).then_inc(s["lens_in"], 16)
            sp.dma_start(lens_i[B * LCF:NCOL, 0:TAIL], lens[:, LCF * P:PLEN]).then_inc(s["lens_in"], 16)
            for dst, src in ((w_in_rows, w_in), (wq_s, wq), (wk_s, wk), (wv_s, wv), (wo_s, wo)):
                sp.dma_start(dst[:, :, :], src.rearrange("(c p) n -> p c n", p=P)).then_inc(s["weights_in"], 16)

            def load_x(t, par):
                at(sp, s["xb_made"], t - 2)
                at(sp, s["xhat_made"], t - 2)
                sp.dma_start(xs[:, par, :], x_rows[bass.ds(t * P, P), :]).then_inc(x_in[par], 16)

            def load_ctx(t, par):
                at(sp, s["dep_made"], t - 2)
                at(sp, s["ctx_sq"], t - 2)
                row = sp.value_load(first_row[0:1, bass.ds(t, 1)], min_val=0, max_val=B * PLEN - P)
                sp.dma_start(ctx[:, par, :], ctx_rows[bass.ds(row, P), :]).then_inc(ctx_loaded[par], 16)

            load_x(0, 0)
            sp.wait_ge(s["tables_ready"], 1)
            sp.wait_ge(s["w_in_turned"], 1)

            def step(i, u):
                if live(i):
                    load_ctx(i, u)
                if isinstance(i, int):
                    if i + 1 < NT:
                        load_x(i + 1, 1 - u)
                else:
                    load_x(i + 1, 1 - u)
                if live(i - 2):
                    at(sp, s["res_made"], i - 2)
                    sp.dma_start(out_rows[bass.ds((i - 2) * P, P), :], res[:, u, :]).then_inc(res_out[u], 16)

            for i in range(LOOP_FROM):
                step(i, i % 2)
            with sp.Fori(LOOP_FROM, NT - 2, 2) as i:
                for u in range(2):
                    step(i + u, u)
            for i in range(NT - 2, NT + 2):
                step(i, i % 2)
            for par in range(2):
                moved(sp, res_out, NT - 2 + par, par)

        @block.gpsimd
        def _(pool):
            g = nc.gpsimd
            g.memset(lens_rows[:, :], 0)
            g.memset(ones[:, :], 1.0)
            g.memset(ones_b[:, :], 1.0)
            g.memset(ident[:, :], 0.0)
            g.memset(cum_mat[:, :], 0.0)
            g.memset(half_z[:, :], -1.0 / NORMALIZER)
            g.memset(sel_e[:, :, :], 0.0)
            g.memset(minus_half[:, :], -0.5)
            g.memset(last_row[:, :], 0.0)
            g.memset(bias_rows[:, :], 0.0)
            g.memset(keep[:, :], 1.0)
            g.memset(w_low[:, :, :], 0.0)
            g.memset(state[:, :, :, :], 0.0)
            g.memset(depool[:, 1, :], 0.0)
            g.iota(row_no[:, :], pattern=[[0, 1]], base=1, channel_multiplier=1,
                   allow_small_or_imprecise_dtypes=True)
            g.iota(rank[:, :], pattern=[[-1, NE]], base=NE, channel_multiplier=0,
                   allow_small_or_imprecise_dtypes=True)
            g.iota(thr, pattern=[[P, TB + 1]], base=0, channel_multiplier=0,
                   allow_small_or_imprecise_dtypes=True)
            g.iota(col_no, pattern=[[1, P]], base=0, channel_multiplier=0,
                   allow_small_or_imprecise_dtypes=True)
            g.iota(row_start, pattern=[[PLEN, B], [0, TB]], base=0, channel_multiplier=0,
                   allow_small_or_imprecise_dtypes=True).then_inc(s["consts_made"], 1)
            pool.wait_ge(s["consts_made"], 1)
            done = 0

            def then(ins):
                nonlocal done
                done += 1
                ins.then_inc(s["consts_selected"], 1)
                pool.wait_ge(s["consts_selected"], done)

            then(g.affine_select(out=ident[:, :], in_=ident[:, :], compare_op=ALU.not_equal, fill=1.0, base=0,
                            pattern=[[-1, P]], channel_multiplier=1))
            then(g.affine_select(out=triu[:, :], in_=ones[:, :], compare_op=ALU.is_ge, fill=0.0, base=0,
                            pattern=[[1, P]], channel_multiplier=-1))
            then(g.affine_select(out=triu_b[:, :], in_=ones_b[:, :], compare_op=ALU.is_ge, fill=0.0, base=0,
                            pattern=[[1, P]], channel_multiplier=-1))
            then(g.affine_select(out=cum_mat[0:64, :], in_=cum_mat[0:64, :], compare_op=ALU.is_ge,
                            fill=1.0 / NORMALIZER, base=0, pattern=[[1, P]], channel_multiplier=-1))
            then(g.affine_select(out=cum_mat[64:P, :], in_=cum_mat[64:P, :], compare_op=ALU.is_gt,
                            fill=-1.0 / NORMALIZER, base=64, pattern=[[-1, P]], channel_multiplier=1))
            then(g.memset(half_z[64:P, 0:1], 0.0))
            then(g.memset(half_z[0:64, 1:2], 0.0))
            then(g.affine_select(out=sel_e[:, :, :], in_=sel_e[:, :, :], compare_op=ALU.not_equal, fill=1.0, base=0,
                            pattern=[[-1, NE], [0, P]], channel_multiplier=1))
            then(g.affine_select(out=last_row[:, :], in_=last_row[:, :], compare_op=ALU.not_equal, fill=1.0,
                            base=-(P - 1), pattern=[[0, 1]], channel_multiplier=1))
            then(g.affine_select(out=bias_rows[:, :], in_=bias_rows[:, :], compare_op=ALU.not_equal, fill=1.0,
                            base=-(LORA + GLR), pattern=[[0, 1]], channel_multiplier=1))
            then(g.affine_select(out=bias_rows[:, :], in_=bias_rows[:, :], compare_op=ALU.not_equal, fill=1.0,
                            base=-(96 + GLR), pattern=[[0, 1]], channel_multiplier=1))
            then(g.memset(keep[:, 0:NT].rearrange("p (b t) -> p b t", t=TB)[:, :, 0:1], 0.0))
            then(g.tensor_scalar(carry_bias[:, :], row_no[:, :], LN_A, 0.0, ALU.mult, ALU.add))

            def step(i, u):
                a, b, c = i, i - 1, i - 2
                pa, pb, pc = u, 1 - u, u
                if live(c):
                    at(pool, s["dec_kept"], c)
                    at(pool, s["state_made"], c - 1)
                    g.tensor_tensor(state[:, :, :, :], state[:, :, :, :],
                                    dec_first[:, pc, :, :].unsqueeze(3).to_broadcast([P, PAIRS, SLOTS, DK]),
                                    ALU.mult).then_inc(s["state_first"], 1)
                if live(a):
                    at(pool, s["x_var"], a)
                    at(pool, s["ctx_var"], a)
                    at(pool, s["past_made"], a - 1)
                    at(pool, s["xhat_made"], a - 1)
                    g.tensor_tensor(rs_a[:, :], var_a[:, :], minus_half[:, 0:2], ALU.pow).then_inc(s["a_rs"], 1)
                    at(pool, s["resid_made"], a - 1)
                    g.tensor_tensor(x_plus_b[:, :], xs[:, pa, :], b_in_s[:, :], ALU.add).then_inc(s["xb_made"], 1)
                if live(c):
                    for j, one, two in ((0, s["a1e_masked"], s["a2e_masked"]), (1, s["a1o_masked"], s["a2o_masked"])):
                        at(pool, one, c)
                        at(pool, two, c)
                        g.tensor_tensor(att1[:, j, :, :], att1[:, j, :, :], att2[:, j, :, :],
                                        ALU.add).then_inc(s["att_summed"], 1)
                if live(b):
                    at(pool, s["sig_made"], b)
                    at(pool, s["g_normed"], b)
                    at(pool, s["o_gated_made"], b - 2)
                    g.tensor_tensor(g_silu[:, pb, :], g_norm[:, :], sig[:, :], ALU.mult).then_inc(s["silu_made"], 1)
                if live(c):
                    at(pool, s["o_sq_made"], c)
                    at(pool, s["silu_made"], c)
                    g.tensor_tensor(o[:, :], o[:, :], g_silu[:, pc, :], ALU.mult).then_inc(s["o_gated_made"], 1)
                    at(pool, s["o_var_made"], c)
                    g.tensor_tensor(o_rs[:, :], o_var[:, :], minus_half[:, :], ALU.pow).then_inc(s["o_rs_made"], 1)
                if live(b):
                    at(pool, s["gt1_exped"], b)
                    at(pool, s["k1_copied"], b)
                    at(pool, s["kvd_made"], b - 2)
                    at(pool, s["k1_turned"], b - 1)
                    at(pool, s["x1_made"], b)
                    at(pool, s["res_made"], b - 2)
                    g.tensor_tensor(kt1[:, pb, :], k1[:, :], e1m[:, :], ALU.mult).then_inc(s["kt1_made"], 1)
                    g.tensor_copy(x1_late[:, pb, :], x1[:, pb, :]).then_inc(s["x1_moved"], 1)
                    at(pool, s["gt2_exped"], b)
                    at(pool, s["k2_exped"], b)
                    at(pool, s["kt2_made"], b - 1)
                    g.tensor_tensor(e2m[:, :], k2_exp[:, :], e2m[:, :], ALU.mult).then_inc(s["k2d_made"], 1)
                if live(a):
                    at(pool, s["dep_copied"], a)
                    g.tensor_tensor(dep_g[:, :], depool[:, pa, :], g_init_s[:, :], ALU.mult).then_inc(s["dep_scaled"], 1)
                    at(pool, s["dep_scaled"], a)
                    at(pool, s["xb_made"], a)
                    at(pool, s["x1_made"], a - 1)
                    g.tensor_tensor(resid[:, :], dep_g[:, :], x_plus_b[:, :], ALU.add).then_inc(s["resid_made"], 1)
                    at(pool, s["x1_var"], a)
                    at(pool, s["xn_made"], a - 1)
                    g.tensor_tensor(rs2[:, :], var2[:, :], minus_half[:, 0:1], ALU.pow).then_inc(s["x1_rs"], 1)
                if live(c):
                    at(pool, s["state_added"], c)
                    g.tensor_tensor(state[:, :, :, :], state[:, :, :, :],
                                    dec[:, pc, 1, :, :].unsqueeze(3).to_broadcast([P, PAIRS, SLOTS, DK]),
                                    ALU.mult).then_inc(s["state_made"], 1)

            run(pool, step)

        @block.scalar
        def _(act):
            sc = nc.scalar
            sc.preload_act_table_set("natural_log_exp_and_others")
            sc.dma_start(g_res_s[:, :], g_res.rearrange("(c p) -> p c", p=P),
                         allow_slow_non_contiguous=True).then_inc(s["small_in"], 16)
            sc.dma_start(b_in_s[:, :], b_in.unsqueeze(0).to_broadcast([P, D])).then_inc(s["small_in"], 16)
            sc.dma_start(g_init_s[:, :], g_init[0:D].unsqueeze(0).to_broadcast([P, D])).then_inc(s["small_in"], 16)
            sc.dma_start(norm_s[:, :], norm_w.unsqueeze(0).to_broadcast([P, DK])).then_inc(s["small_in"], 16)
            sc.dma_start(we_s[:, :, :], we.rearrange("(c p) n -> p c n", p=P)).then_inc(s["small_in"], 16)
            act.wait_ge(s["consts_made"], 1)
            for c0, w, src in ((0, LORA, wqa), (LORA, LORA, wka), (P, LORA, wga), (P + 64, GLR, wg1a),
                               (P + 96, GLR, wg2a)):
                sc.dma_start(w_low[:, :, c0:c0 + w], src.rearrange("(c p) n -> p c n", p=P)).then_inc(s["small_in"], 16)
            for r0, h, src in ((0, 0, wqb), (64, 0, wkb), (0, 1, wgb), (64, 1, wg1b), (96, 1, wg2b)):
                sc.dma_start(w_up[r0:r0 + src.shape[0], h, :], src).then_inc(s["small_in"], 16)
            for r0, src in ((64 + GLR, bg1), (96 + GLR, bg2)):
                sc.dma_start(w_up[r0:r0 + 1, 1, :], src.unsqueeze(0)).then_inc(s["small_in"], 16)

            def step(i, u):
                a, b, c = i, i - 1, i - 2
                pa, pb, pc = u, 1 - u, u
                if live(a):
                    moved(act, ctx_loaded, a, pa)
                    at(act, s["ctx_var"], a - 1)
                    sc.activation(ctx_bin[:, :], ctx[:, pa, :], ACT.Square, accum_out=ctx_ss[:, :]).then_inc(s["ctx_sq"], 1)
                if live(b):
                    at(act, s["l_sub_made"], b)
                    at(act, s["fac_made"], b - 1)
                    sc.activation(l_exp[:, :], l_sub[:, :], ACT.Exp, accum_out=l_sum[:, :]).then_inc(s["l_exp_made"], 1)
                if live(a):
                    at(act, s["xhat_turned"], a)
                    at(act, s["w_made"], a - 1)
                    sc.copy(xhat_t[:, :, :], bank[0][:, :].rearrange("p (c t) -> p c t", c=KC)).then_inc(s["xhat_t_made"], 1)
                    at(act, s["dist_pos"], a)
                    at(act, s["dep_w_made"], a - 1)
                    sc.activation(decay_w[:, :], dist_p[:, :], ACT.Exp, scale=LN_A).then_inc(s["decay_made"], 1)
                    sc.activation(carry_y[96:P, :], dist[96:P, :], ACT.Exp, scale=LN_A,
                                  bias=carry_bias[96:P, :]).then_inc(s["carry_made"], 1)
                if live(b):
                    at(act, s["q1_made"], b)
                    at(act, s["qt1_made"], b - 1)
                    sc.mul(q1[:, :], bank[7][:, :], SCALE).then_inc(s["q1_copied"], 1)
                    at(act, z_min[0], b)
                    sc.activation(gate_l[:, 0, :], gate_l[:, 0, :], ACT.Exp).then_inc(z_exp[0], 1)
                    at(act, s["k1_made"], b)
                    at(act, s["kt1_made"], b - 1)
                    sc.copy(k1[:, :], bank[3][:, :]).then_inc(s["k1_copied"], 1)
                    at(act, z_exp[0], b)
                    sc.activation(gate_l[:, 0, :], gate_l[:, 0, :], ACT.Ln, bias=1.0).then_inc(z_ln[0], 1)
                    for j in (2, 1):
                        at(act, z_min[j], b)
                        sc.activation(gate_l[:, j, :], gate_l[:, j, :], ACT.Exp).then_inc(z_exp[j], 1)
                    at(act, s["q2_made"], b)
                    at(act, s["facq_made"], b)
                    at(act, s["qt2_made"], b - 1)
                    sc.mul(q2[:, :], bank[4][:, :], fac_q[:, 0:1]).then_inc(s["q2_copied"], 1)
                    for j in (2, 1):
                        at(act, z_exp[j], b)
                        sc.activation(gate_l[:, j, :], gate_l[:, j, :], ACT.Ln, bias=1.0).then_inc(z_ln[j], 1)
                    at(act, s["k2_subbed"], b)
                    sc.activation(k2_exp[:, :], k2_exp[:, :], ACT.Exp).then_inc(s["k2_exped"], 1)
                    at(act, l_made[2], b)
                    at(act, s["silu_made"], b - 1)
                    sc.activation(sig[:, :], gate_l[:, 2, :], ACT.Exp, scale=-1.0).then_inc(s["sig_made"], 1)
                if live(c):
                    at(act, s["o_made"], c)
                    at(act, s["o_n_made"], c - 1)
                    oh = heads(o[:, :]).rearrange("p (a two) d -> p a two d", two=2)
                    sc.copy(oh[:, :, 0, :], bank[6][:, 0:PAIRS * DK].rearrange("p (a d) -> p a d", a=PAIRS)).then_inc(s["oe_copied"], 1)
                    sc.copy(oh[:, :, 1, :], bank[7][:, 0:PAIRS * DK].rearrange("p (a d) -> p a d", a=PAIRS)).then_inc(s["o_copied"], 1)
                    at(act, s["oe_copied"], c)
                    at(act, s["o_copied"], c)
                    at(act, s["o_summed"], c - 1)
                    sc.activation(o_sq[:, :], o[:, :], ACT.Square).then_inc(s["o_sq_made"], 1)
                if live(b):
                    at(act, s["gt1_made"], b)
                    at(act, s["q1_turned"], b - 1)
                    at(act, s["kt1_made"], b - 1)
                    sc.activation(e1p[:, :], bank[0][:, :], ACT.Exp)
                    sc.activation(e1m[:, :], bank[0][:, :], ACT.Exp, scale=-1.0).then_inc(s["gt1_exped"], 1)
                    at(act, s["gt2_made"], b)
                    at(act, s["q2_turned"], b - 1)
                    at(act, s["kt2_made"], b - 1)
                    sc.activation(e2p[:, :], bank[1][:, :], ACT.Exp)
                    sc.activation(e2m[:, :], bank[1][:, :], ACT.Exp, scale=-1.0).then_inc(s["gt2_exped"], 1)
                    at(act, s["dec_made"], b)
                    at(act, s["state_made"], b - 2)
                    at(act, s["dec_kept"], b - 2)
                    dv = dec[:, pb, :, :, :].rearrange("p j a s -> p a j s")
                    sc.activation(dv[:, :, :, 0:1], bank[2][:, 0:2 * PAIRS].rearrange("p (a j s) -> p a j s", a=PAIRS, j=2),
                                  ACT.Exp)
                    for j in range(2):
                        last = sc.activation(dv[:, :, j, 1:SLOTS],
                                      bank[2][:, 8:8 + 2 * PAIRS * NE].rearrange("p (a j s) -> p a j s", a=PAIRS, j=2)[:, :, j, :],
                                      ACT.Exp)
                    last.then_inc(s["dec_exped"], 1)
                if live(a):
                    at(act, s["dep_made"], a)
                    at(act, s["dep_scaled"], a - 2)
                    sc.copy(depool[:, pa, :], bank[5][:, :]).then_inc(s["dep_copied"], 1)
                if live(b):
                    at(act, s["v_made"], b)
                    at(act, s["kvd_made"], b - 1)
                    at(act, s["onehot_made"], b)
                    sc.copy(v[:, pb, :], bank[3][:, :])
                    for e in range(NE):
                        last = sc.mul(v_e[:, e, :], bank[3][:, :], onehot[:, e:e + 1])
                    last.then_inc(s["v_copied"], 1)
                    at(act, s["masks_made"], b)
                    at(act, s["q2_te_made"], b - 1)
                    sc.copy(mask_row[:, :, :], bank[4][:, :].rearrange("p (e t) -> p e t", e=NE)).then_inc(s["masks_copied"], 1)
                if live(c):
                    at(act, s["o_turned"], c)
                    at(act, s["y_made"], c - 1)
                    sc.copy(o_t[:, :, :], bank[6][:, :].rearrange("p (c t) -> p c t", c=KC)).then_inc(s["o_t_made"], 1)
                if live(b):
                    at(act, s["q1_turned"], b)
                    at(act, s["o_made"], b - 1)
                    sc.copy(q1_t[:, :, :], bank[3][:, :].rearrange("p (a t) -> p a t", a=PAIRS)).then_inc(s["q1_t_made"], 1)
                    at(act, s["k1_turned"], b)
                    sc.copy(k1_t[:, :, :], bank[4][:, :].rearrange("p (a t) -> p a t", a=PAIRS)).then_inc(s["k1_t_made"], 1)
                    at(act, s["q2_turned"], b)
                    at(act, s["q2_te_made"], b - 1)
                    sc.copy(q2_t[:, :, :], bank[5][:, :].rearrange("p (a t) -> p a t", a=PAIRS)).then_inc(s["q2_t_made"], 1)
                if live(a):
                    at(act, s["xn_turned"], a)
                    at(act, s["v_made"], a - 2)
                    sc.copy(xn_t[:, pa, :, :], bank[1][:, :].rearrange("p (c t) -> p c t", c=KC)).then_inc(s["xn_t_made"], 1)
                if live(b):
                    at(act, s["k2_turned"], b)
                    sc.copy(k2_t[:, :, :], bank[0][:, :].rearrange("p (a t) -> p a t", a=PAIRS)).then_inc(s["k2_t_made"], 1)

            run(act, step)

        @block.tensor
        def _(pe):
            te = nc.tensor
            mm = te.matmul
            pe.wait_ge(s["consts_selected"], 13)
            pe.wait_ge(s["lens_float"], 1)
            te.transpose(bank[0][:, 0:NCOL], lens_f, ident[0:NCOL, 0:NCOL]).then_inc(s["lens_turned"], 1)
            pe.wait_ge(s["lens_turned"], 2)
            mm(bank[1][:, 0:NCOL], triu[:, :], lens_t, start=True, stop=True)
            mm(bank[2][:, 0:NCOL], ones[:, :], lens_t, start=True, stop=True).then_inc(s["lens_summed"], 1)
            for b in range(B):
                pe.wait_ge(s["hot_ready"], b + 1)
                for k in range(LC):
                    last = mm(bank[3][:, b * TB:(b + 1) * TB], lo_hot[b % 2][:, k, :], hi_hot[:, b * LC + k, :],
                              start=(k == 0), stop=(k == LC - 1))
                last.then_inc(s["hot_used"], 1)
            pe.wait_ge(s["counts_ready"], 1)
            mm(bank[4][:, 0:NT], ones[:, :], bound[:, 0:NT], start=True, stop=True).then_inc(s["totals_ready"], 1)
            pe.wait_ge(s["weights_in"], 16 * 5)
            pe.wait_ge(s["tables_ready"], 2)
            for k in range(KC):
                for m in range(KC):
                    last = te.transpose(bank[4 + k][:, m * P:(m + 1) * P], w_in_rows[:, m, k * P:(k + 1) * P], ident[:, :])
            last.then_inc(s["w_in_turned"], 1)
            pe.wait_ge(s["small_in"], 16 * SMALL)
            pe.wait_ge(s["g_scaled"], 1)

            def rows(j):
                return slice(DK * j, DK * j + DK)

            def turn(bk, src):
                for k in range(KC):
                    last = te.transpose(bank[bk][:, k * P:(k + 1) * P], src[:, k * P:(k + 1) * P], ident[:, :])
                return last

            def product(bk, lhs_t, w):
                for k in range(KC):
                    last = mm(bank[bk][:, :], lhs_t[:, k, :], w[:, k, :], start=(k == 0), stop=(k == KC - 1))
                return last

            def step(i, u):
                a, b, c = i, i - 1, i - 2
                pa, pb, pc = u, 1 - u, u
                def attention(kt, qt, bk, made):
                    for pr in range(PAIRS):
                        for j in range(2):
                            last = mm(bank[bk + j][:, pr * P:(pr + 1) * P], kt[rows(j), pr, :], qt[rows(j), pr, :],
                                      start=True, stop=True)
                    last.then_inc(made, 1)

                if live(c):
                    at(pe, s["q1_t_made"], c)
                    at(pe, s["k1_t_made"], c)
                    attention(k1_t, q1_t, 3, s["a1_made"])
                if live(b):
                    at(pe, s["xn_t_made"], b)
                    at(pe, s["res_made"], b - 2)
                    for h in range(2):
                        for k in range(KC):
                            mm(bank[2][:, h * P:(h + 1) * P], w_low[:, k, h * P:(h + 1) * P], xn_t[:, pb, k, :],
                               start=(k == 0), stop=(k == KC - 1))
                    for k in range(KC):
                        last = mm(bank[2][:, 2 * P:2 * P + NE], xn_t[:, pb, k, :], we_s[:, k, :],
                                  start=(k == 0), stop=(k == KC - 1))
                    last.then_inc(s["low_made"], 1)
                if live(c):
                    at(pe, s["q2_t_made"], c)
                    at(pe, s["k2_t_made"], c)
                    at(pe, s["o_t_made"], c - 1)
                    attention(k2_t, q2_t, 5, s["a2_made"])
                if live(a):
                    at(pe, s["xhat_made"], a)
                    at(pe, s["k2_t_made"], a - 2)
                    turn(0, xhat).then_inc(s["xhat_turned"], 1)
                    at(pe, s["tri_made"], a)
                    at(pe, s["xn_t_made"], a - 1)
                    mm(bank[1][:, 0:P], ones_b[:, :], tri_bound[:, :], start=True, stop=True).then_inc(s["cum_made"], 1)
                if live(b):
                    at(pe, s["x1_made"], b)
                    product(7, xn_t[:, pb], wq_s).then_inc(s["q1_made"], 1)
                    at(pe, s["onehot_made"], b)
                    at(pe, s["dist_made"], b + 1)
                    te.transpose(bank[1][0:NE, P:2 * P], onehot[:, :], ident[:, :]).then_inc(s["hot_turned"], 1)
                    at(pe, s["low_copied"], b)
                    at(pe, s["l_read"], b)
                    at(pe, s["xhat_t_made"], b + 1)
                    mm(bank[0][:, :], low[64:64 + GLR + 1, P:2 * P], w_up[64:64 + GLR + 1, 1, :],
                       start=True, stop=True).then_inc(z_made[0], 1)
                    mm(bank[2][:, :], low[0:LORA, P:2 * P], w_up[0:LORA, 1, :],
                       start=True, stop=True).then_inc(z_made[2], 1)
                    at(pe, s["a1e_masked"], b - 1)
                    product(3, xn_t[:, pb], wk_s).then_inc(s["k1_made"], 1)
                    at(pe, s["hot_t_made"], b)
                    mm(bank[1][:, 2 * P:3 * P], onehot_t[:, :], onehot_t[:, :], start=True, stop=True).then_inc(s["same_made"], 1)
                    at(pe, s["a1o_masked"], b - 1)
                    mm(bank[4][:, :], low[0:LORA, 0:P], w_up[0:LORA, 0, :], start=True, stop=True).then_inc(s["q2_made"], 1)
                    at(pe, s["a2e_masked"], b - 1)
                    mm(bank[5][:, :], low[64:P, 0:P], w_up[64:P, 0, :], start=True, stop=True).then_inc(s["k2_made"], 1)
                    at(pe, s["same_used"], b)
                    mm(bank[1][:, :], low[96:96 + GLR + 1, P:2 * P], w_up[96:96 + GLR + 1, 1, :],
                       start=True, stop=True).then_inc(z_made[1], 1)
                if live(c):
                    at(pe, s["a2o_masked"], c)
                    at(pe, s["q1_copied"], c + 1)
                    at(pe, s["q2_te_made"], c)
                    at(pe, s["state_first"], c)
                    for pr in range(PAIRS):
                        for slot in range(SLOTS):
                            for j in range(2):
                                q = q1_t[rows(j), pr, :] if slot == 0 else q2_te[rows(j), slot - 1, pr, :]
                                mm(bank[6 + j][:, pr * DK:(pr + 1) * DK], q, state[rows(j), pr, slot, :],
                                   start=(slot == 0 and pr == 0), stop=False, skip_group_check=True)
                    pe.wait_ge(s["att_summed"], 2 * (c + 1))
                    for j in range(2):
                        for pr in range(PAIRS):
                            hd = slice((2 * pr + j) * DK, (2 * pr + j + 1) * DK)
                            last = mm(bank[6 + j][:, pr * DK:(pr + 1) * DK], att1[:, j, pr, :], v[:, pc, hd],
                                      start=False, stop=True, skip_group_check=True)
                    last.then_inc(s["o_made"], 1)
                    at(pe, s["q2_copied"], c + 1)
                    for bk, prs, made in ((4, (0, 1), s["kv0_made"]), (5, (2, 3), s["kv1_made"])):
                        if bk == 5:
                            at(pe, s["k2_subbed"], c + 1)
                        for n, pr in enumerate(prs):
                            for j in range(2):
                                hd = slice((2 * pr + j) * DK, (2 * pr + j + 1) * DK)
                                last = mm(bank[bk][rows(j), n * NE * DK:(n + 1) * NE * DK], kt2[:, pc, hd],
                                          v_e[:, :, hd], start=True, stop=True)
                        last.then_inc(made, 1)
                    at(pe, s["oe_copied"], c)
                    for pr in range(PAIRS):
                        for j in range(2):
                            hd = slice((2 * pr + j) * DK, (2 * pr + j + 1) * DK)
                            last = mm(bank[6][rows(j), pr * DK:(pr + 1) * DK], kt1[:, pc, hd], v[:, pc, hd],
                                      start=True, stop=True)
                    last.then_inc(s["kvd_made"], 1)
                if live(b):
                    at(pe, l_made[0], b)
                    mm(bank[0][:, :], cum_mat[:, :], gate_l[:, 0, :], start=True, stop=True).then_inc(s["gt1_made"], 1)
                    at(pe, l_made[1], b)
                    mm(bank[1][:, :], cum_mat2[:, :], gate_l[:, 1, :], start=True, stop=True).then_inc(s["gt2_made"], 1)
                    at(pe, l_made[2], b)
                    at(pe, s["g_normed"], b)
                    for pr in range(PAIRS):
                        mm(bank[2][:, 2 * pr:2 * pr + 2], gate_l[:, 0, pr * P:(pr + 1) * P], half_z[:, :],
                           start=True, stop=True)
                        last = mm(bank[2][:, 8 + 8 * pr:16 + 8 * pr], gate_l[:, 1, pr * P:(pr + 1) * P],
                                  z2_half[:, :, :].rearrange("p j e -> p (j e)"), start=True, stop=True)
                    last.then_inc(s["dec_made"], 1)
                if live(a):
                    at(pe, s["dep_w_made"], a)
                    at(pe, s["kv1_added"], a - 2)
                    at(pe, s["dep_copied"], a - 1)
                    mm(bank[5][:, :], w_depool[:, :], ctx[:, pa, 0:D], start=True, stop=False)
                    mm(bank[5][:, :], w_carry[96:P, :], depool[96:P, 1 - pa, :], start=False, stop=True,
                       tile_position=(96, 0)).then_inc(s["dep_made"], 1)
                if live(b):
                    at(pe, s["k1_copied"], b)
                    product(3, xn_t[:, pb], wv_s).then_inc(s["v_made"], 1)
                if live(a):
                    at(pe, s["o_copied"], a - 2)
                    at(pe, s["xhat_t_made"], a)
                    if not live(c):
                        at(pe, s["q1_copied"], a - 1)
                    product(7, xhat_t, w_in_s).then_inc(s["w_made"], 1)
                if live(b):
                    at(pe, s["kv0_added"], b - 1)
                    at(pe, s["q2_copied"], b)
                    for e in range(NE):
                        last = mm(bank[4][:, e * P:(e + 1) * P], sel_e[:, e, :], onehot_t[:, :], start=True, stop=True)
                    last.then_inc(s["masks_made"], 1)
                if live(c):
                    at(pe, s["o_n_made"], c)
                    at(pe, s["state_added"], c)
                    turn(6, o_n).then_inc(s["o_turned"], 1)
                if live(b):
                    at(pe, s["qt1_made"], b)
                    at(pe, s["v_copied"], b)
                    turn(3, e1p).then_inc(s["q1_turned"], 1)
                    at(pe, s["kt1_made"], b)
                    at(pe, s["masks_copied"], b)
                    turn(4, kt1[:, pb]).then_inc(s["k1_turned"], 1)
                if live(c):
                    at(pe, s["o_t_made"], c)
                    at(pe, s["dec_exped"], c + 1)
                    product(2, o_t, wo_s).then_inc(s["y_made"], 1)
                if live(b):
                    at(pe, s["qt2_made"], b)
                    at(pe, s["dep_copied"], b + 1)
                    turn(5, e2p).then_inc(s["q2_turned"], 1)
                if live(a):
                    at(pe, s["xn_made"], a)
                    at(pe, s["gt2_exped"], a - 1)
                    turn(1, xn).then_inc(s["xn_turned"], 1)
                if live(b):
                    at(pe, s["kt2_made"], b)
                    at(pe, s["gt1_exped"], b)
                    turn(0, kt2[:, pb]).then_inc(s["k2_turned"], 1)

            run(pe, step)

        @block.vector
        def _(dve):
            ve = nc.vector
            n = 0

            def then(ins):
                nonlocal n
                n += 1
                ins.then_inc(s["prologue_step"], 1)
                dve.wait_ge(s["prologue_step"], n)

            dve.wait_ge(s["consts_made"], 1)
            dve.wait_ge(s["lens_in"], 16 * (B + 1))
            ve.tensor_copy(lens_f, lens_i32).then_inc(s["lens_float"], 1)
            dve.wait_ge(s["lens_turned"], 1)
            ve.tensor_copy(lens_t, bank[0][:, 0:NCOL]).then_inc(s["lens_turned"], 1)
            dve.wait_ge(s["lens_summed"], 1)

            def by_batch(ap):
                return ap[:, 0:B * LCF].rearrange("p (b c) -> p b c", b=B), ap[:, B * LCF:NCOL].unsqueeze(2)

            for dst, bk in ((ends, 1), (totals, 2)):
                full, tail = by_batch(bank[bk])
                ve.tensor_copy(dst[:, :, 0:LCF], full)
                then(ve.tensor_copy(dst[:, :, LCF:LC], tail))
            then(ve.memset(offs[:, :, 0:1], -1.0))
            for k in range(1, LC):
                then(ve.tensor_tensor(offs[:, :, k:k + 1], offs[:, :, k - 1:k], totals[:, :, k - 1:k], ALU.add))
            flat_ends = ends.rearrange("p b c -> p (b c)")
            then(ve.tensor_tensor(flat_ends, flat_ends, offs.rearrange("p b c -> p (b c)"), ALU.add))
            then(ve.tensor_scalar(wrapped, flat_ends, 0.0, float(S), ALU.is_lt, ALU.mult))
            then(ve.tensor_tensor(flat_ends, flat_ends, wrapped, ALU.add))
            then(ve.tensor_tensor(reached, flat_ends.unsqueeze(2).to_broadcast([P, NCOL, TB + 1]),
                                  thr.unsqueeze(1).to_broadcast([P, NCOL, TB + 1]), ALU.is_ge))
            then(ve.tensor_tensor(hi_hot, reached[:, :, 0:TB], reached[:, :, 1:TB + 1], ALU.subtract))
            then(ve.tensor_reduce(hi_no.unsqueeze(2), reached[:, :, 1:TB + 1], AX.X, ALU.add))
            then(ve.scalar_tensor_tensor(lo_no, hi_no, float(-P), flat_ends, ALU.mult, ALU.add))
            for b in range(B):
                if b >= 2:
                    dve.wait_ge(s["hot_used"], b - 1)
                ve.tensor_tensor(lo_hot[b % 2], lo_no[:, b * LC:(b + 1) * LC].unsqueeze(2).to_broadcast([P, LC, P]),
                                 col_no.unsqueeze(1).to_broadcast([P, LC, P]), ALU.is_equal).then_inc(s["hot_ready"], 1)
            dve.wait_ge(s["hot_used"], B)
            ve.tensor_scalar(bound[:, 0:NT], bank[3][:, 0:NT], 1.0, None, ALU.min).then_inc(s["counts_ready"], 1)
            dve.wait_ge(s["totals_ready"], 1)
            then(ve.tensor_copy(tile_tot, bank[4][:, 0:NT].rearrange("p (b t) -> p b t", b=B)))
            then(ve.memset(before[:, :, 0:1], 0.0))
            for t in range(1, TB):
                then(ve.tensor_tensor(before[:, :, t:t + 1], before[:, :, t - 1:t], tile_tot[:, :, t - 1:t], ALU.add))
            flat_before = before.rearrange("p b t -> p (b t)")
            then(ve.tensor_tensor(row_first, before, row_start, ALU.add))
            ve.tensor_copy(first_row[:, :], row_first[0:1].rearrange("p b t -> p (b t)")).then_inc(s["tables_ready"], 1)
            then(ve.tensor_scalar(started[:, 0:NT], flat_before, 1.0, None, ALU.min))
            then(ve.tensor_scalar(unstarted[:, 0:NT], started[:, 0:NT], -1.0, 1.0, ALU.mult, ALU.add))
            dve.wait_ge(s["consts_selected"], 13)
            ve.memset(onehot[:, :], 0.0).then_inc(s["tables_ready"], 1)
            dve.wait_ge(s["small_in"], 16 * SMALL)
            ve.tensor_scalar(g_init_s[:, :], g_init_s[:, :], B_COEF, None, ALU.mult)
            dve.wait_ge(s["w_in_turned"], 1)
            for k in range(KC):
                last = ve.tensor_scalar(w_in_s[:, k, :], bank[4 + k][:, :], g_res_s[:, k:k + 1], None, ALU.mult)
            last.then_inc(s["g_scaled"], 1)

            def step(i, u):
                a, b, c = i, i - 1, i - 2
                pa, pb, pc = u, 1 - u, u
                if live(a):
                    moved(dve, x_in, a, pa)
                    ve.bn_stats(stat[:, :], xs[:, pa, :]).then_inc(s["x_stats"], 1)
                    at(dve, s["cum_made"], a - 1)
                    ve.tensor_scalar(tri_bound[:, :], triu_b[:, :], bound[:, bass.ds(a, 1)], None,
                                     ALU.mult).then_inc(s["tri_made"], 1)
                    at(dve, s["ctx_sq"], a)
                    at(dve, s["a_rs"], a - 1)
                    at(dve, s["x_stats"], a)
                    ve.tensor_scalar(var_a[:, 1:2], ctx_ss[:, :], 1.0 / DG, RMS_EPS, ALU.mult,
                                     ALU.add).then_inc(s["ctx_var"], 1)
                    ve.bn_aggr(mv[:, :], stat[:, :]).then_inc(s["x_mean"], 1)
                    at(dve, s["x_mean"], a)
                    ve.tensor_scalar(var_a[:, 0:1], mv[:, 1:2], 1.0 + RMS_EPS, RMS_EPS * LN_EPS, ALU.mult,
                                     ALU.add).then_inc(s["x_var"], 1)
                if live(b):
                    at(dve, s["low_made"], b)
                    at(dve, s["q2_made"], b - 1)
                    at(dve, s["k2_made"], b - 1)
                    logits = bank[2][:, 2 * P:2 * P + NE]
                    ve.tensor_reduce(l_max[:, :], logits, AX.X, ALU.max).then_inc(s["l_max_made"], 1)
                    ve.tensor_copy(low[:, 0:P], bank[2][:, 0:P])
                    ve.tensor_scalar(low[:, P:2 * P], bank[2][:, P:2 * P], bias_rows[:, 0:1], None,
                                     ALU.add).then_inc(s["low_copied"], 1)
                    at(dve, s["l_max_made"], b)
                    at(dve, s["l_exp_made"], b - 1)
                    ve.tensor_scalar(l_sub[:, :], logits, l_max[:, 0:1], None, ALU.subtract).then_inc(s["l_sub_made"], 1)
                    ve.scalar_tensor_tensor(l_rank[:, :], logits, l_max[:, 0:1], rank[:, :], ALU.is_equal,
                                            ALU.mult).then_inc(s["l_read"], 1)
                if live(a):
                    at(dve, s["a_rs"], a)
                    at(dve, s["xhat_turned"], a - 1)
                    ve.tensor_scalar(xhat[:, :], xs[:, pa, :], mv[:, 0:1], rs_a[:, 0:1], ALU.subtract,
                                     ALU.mult).then_inc(s["xhat_made"], 1)
                if live(b):
                    at(dve, s["l_read"], b)
                    ve.tensor_reduce(l_best[:, :], l_rank[:, :], AX.X, ALU.max).then_inc(s["l_best_made"], 1)
                tri = triu[:, :].unsqueeze(1).to_broadcast([P, PAIRS, P])
                if live(c):
                    at(dve, s["o_made"], c - 1)
                    at(dve, s["a1_made"], c)
                    for j, masked in ((0, s["a1e_masked"]), (1, s["a1o_masked"])):
                        ve.tensor_tensor(att1[:, j, :, :], bank[3 + j][:, :].rearrange("p (a t) -> p a t", a=PAIRS),
                                         tri, ALU.mult).then_inc(masked, 1)
                if live(b):
                    at(dve, s["l_best_made"], b)
                    at(dve, s["v_copied"], b - 1)
                    at(dve, s["hot_turned"], b - 1)
                    ve.tensor_scalar(onehot[:, :], l_rank[:, :], l_best[:, 0:1], None, ALU.is_equal).then_inc(s["onehot_made"], 1)
                if live(a):
                    at(dve, s["cum_made"], a)
                    at(dve, s["carry_made"], a - 1)
                    at(dve, s["past_made"], a - 1)
                    ve.tensor_scalar(dist[:, :], bank[1][:, 0:P], unstarted[:, bass.ds(a, 1)], row_no[:, 0:1], ALU.max,
                                     ALU.subtract).then_inc(s["dist_made"], 1)
                if live(c):
                    same = mask2[:, pc, :].unsqueeze(1).to_broadcast([P, PAIRS, P])
                    at(dve, s["a2_made"], c)
                    for j, masked in ((0, s["a2e_masked"]), (1, s["a2o_masked"])):
                        ve.tensor_tensor(att2[:, j, :, :], bank[5 + j][:, :].rearrange("p (a t) -> p a t", a=PAIRS),
                                         same, ALU.mult).then_inc(masked, 1)
                if live(a):
                    at(dve, s["dist_made"], a)
                    at(dve, s["decay_made"], a - 1)
                    ve.tensor_scalar(dist_p[:, :], dist[:, :], 0.0, None, ALU.max).then_inc(s["dist_pos"], 1)
                    at(dve, s["dep_w_made"], a - 1)
                    at(dve, s["a_rs"], a)
                    ve.tensor_scalar(in_past[:, :], dist[:, :], 0.0, rs_a[:, 1:2], ALU.is_ge,
                                     ALU.mult).then_inc(s["past_made"], 1)
                if live(b):
                    at(dve, s["l_exp_made"], b)
                    at(dve, s["kt2_made"], b - 1)
                    ve.reciprocal(fac[:, :], l_sum[:, :]).then_inc(s["fac_made"], 1)
                    at(dve, s["hot_turned"], b)
                    at(dve, s["masks_made"], b - 1)
                    ve.tensor_copy(onehot_t[:, :], bank[1][0:NE, P:2 * P]).then_inc(s["hot_t_made"], 1)
                    at(dve, s["fac_made"], b)
                    at(dve, s["q2_copied"], b - 1)
                    ve.tensor_scalar(fac_q[:, :], fac[:, :], SCALE, None, ALU.mult).then_inc(s["facq_made"], 1)
                    for j in (0, 2):
                        at(dve, z_made[j], b)
                        at(dve, (s["dec_made"], s["dec_made"], s["sig_made"])[j], b - 1)
                        ve.tensor_scalar(gate_l[:, j, :], bank[j][:, :], -1.0, 40.0, ALU.mult, ALU.min).then_inc(z_min[j], 1)
                if live(c):
                    at(dve, s["q2_t_made"], c)
                    at(dve, s["masks_copied"], c)
                    at(dve, s["o_made"], c - 1)
                    for e in range(NE):
                        last = ve.tensor_tensor(q2_te[:, e, :, :], q2_t[:, :, :],
                                                mask_row[:, e, :].unsqueeze(1).to_broadcast([P, PAIRS, P]), ALU.mult)
                    last.then_inc(s["q2_te_made"], 1)
                if live(b):
                    at(dve, s["same_made"], b)
                    at(dve, s["a2o_masked"], b - 2)
                    at(dve, s["gt2_made"], b - 1)
                    ve.tensor_tensor(mask2[:, pb, :], bank[1][:, 2 * P:3 * P], triu[:, :], ALU.mult)
                    ve.tensor_tensor(cum_mat2[:, :], bank[1][:, 2 * P:3 * P], cum_mat[:, :], ALU.mult).then_inc(s["same_used"], 1)
                    at(dve, s["dec_made"], b - 1)
                    at(dve, s["onehot_made"], b)
                    ve.tensor_tensor(z2_half[:, :, :], onehot[:, :].unsqueeze(1).to_broadcast([P, 2, NE]),
                                     half_z[:, :].unsqueeze(2).to_broadcast([P, 2, NE]), ALU.mult)
                if live(a):
                    at(dve, s["past_made"], a)
                    at(dve, s["decay_made"], a)
                    at(dve, s["dep_made"], a - 1)
                    ve.tensor_tensor(w_depool[:, :], decay_w[:, :], in_past[:, :], ALU.mult)
                    at(dve, s["carry_made"], a)
                    ve.tensor_scalar(w_carry[96:P, :], carry_y[96:P, :], started[96:P, bass.ds(a, 1)], last_row[96:P, 0:1],
                                     ALU.mult, ALU.mult).then_inc(s["dep_w_made"], 1)
                if live(b):
                    at(dve, s["k2_made"], b)
                    at(dve, s["k2d_made"], b - 1)
                    at(dve, s["k2_summed"], b - 1)
                    ve.tensor_reduce(k2_max[:, :], heads(bank[5][:, :]), AX.X, ALU.max).then_inc(s["k2_maxed"], 1)
                    at(dve, z_made[1], b)
                    at(dve, s["dec_made"], b - 1)
                    ve.tensor_scalar(gate_l[:, 1, :], bank[1][:, :], -1.0, 40.0, ALU.mult, ALU.min).then_inc(z_min[1], 1)
                    at(dve, s["k2_maxed"], b)
                    ve.tensor_tensor(heads(k2_exp[:, :]), heads(bank[5][:, :]), over_heads(k2_max[:, :]),
                                     ALU.subtract).then_inc(s["k2_subbed"], 1)
                    for j in (0, 2, 1):
                        at(dve, z_ln[j], b)
                        ve.scalar_tensor_tensor(gate_l[:, j, :], bank[j][:, :], -1.0, gate_l[:, j, :], ALU.mult,
                                                ALU.max).then_inc(l_made[j], 1)
                    at(dve, s["silu_made"], b - 1)
                    ve.tensor_tensor(heads(g_norm[:, :]), heads(bank[2][:, :]),
                                     norm_s[:, :].unsqueeze(1).to_broadcast([P, H, DK]), ALU.mult).then_inc(s["g_normed"], 1)
                    at(dve, s["k2_exped"], b)
                    ve.tensor_reduce(k2_sum[:, :], heads(k2_exp[:, :]), AX.X, ALU.add).then_inc(s["k2_summed"], 1)
                    at(dve, s["k2_summed"], b)
                    ve.reciprocal(k2_rec[:, :], k2_sum[:, :]).then_inc(s["k2_reced"], 1)
                    at(dve, s["k2_reced"], b)
                    at(dve, s["kt2_made"], b - 1)
                    ve.tensor_scalar(k2_fac[:, :], k2_rec[:, :], fac[:, 0:1], None, ALU.mult).then_inc(s["k2_faced"], 1)
                if live(c):
                    at(dve, s["o_made"], c)
                    at(dve, s["kv0_made"], c)
                    part = state[:, 0:2, 1:SLOTS, :]
                    ve.tensor_tensor(part, part, bank[4][:, :].rearrange("p (a e d) -> p a e d", a=2, e=NE),
                                     ALU.add).then_inc(s["kv0_added"], 1)
                    at(dve, s["o_sq_made"], c)
                    at(dve, s["o_var_made"], c - 1)
                    ve.tensor_reduce(o_ss[:, :], heads(o_sq[:, :]), AX.X, ALU.add).then_inc(s["o_summed"], 1)
                    at(dve, s["kv1_made"], c)
                    part = state[:, 2:4, 1:SLOTS, :]
                    ve.tensor_tensor(part, part, bank[5][:, :].rearrange("p (a e d) -> p a e d", a=2, e=NE),
                                     ALU.add).then_inc(s["kv1_added"], 1)
                    at(dve, s["o_summed"], c)
                    at(dve, s["o_rs_made"], c - 1)
                    ve.tensor_scalar(o_var[:, :], o_ss[:, :], 1.0 / DK, LN_EPS, ALU.mult, ALU.add).then_inc(s["o_var_made"], 1)
                    at(dve, s["kvd_made"], c)
                    part = state[:, :, 0, :]
                    ve.tensor_tensor(part, part, bank[6][:, 0:PAIRS * DK].rearrange("p (a d) -> p a d", a=PAIRS),
                                     ALU.add).then_inc(s["state_added"], 1)
                if live(b):
                    at(dve, s["gt1_exped"], b)
                    at(dve, s["q1_copied"], b)
                    ve.tensor_tensor(e1p[:, :], q1[:, :], e1p[:, :], ALU.mult).then_inc(s["qt1_made"], 1)
                    at(dve, s["gt2_exped"], b)
                    at(dve, s["q2_copied"], b)
                    at(dve, s["q2_turned"], b - 1)
                    ve.tensor_tensor(e2p[:, :], q2[:, :], e2p[:, :], ALU.mult).then_inc(s["qt2_made"], 1)
                    at(dve, s["dec_exped"], b)
                    at(dve, s["state_first"], b - 2)
                    ve.tensor_scalar(dec_first[:, pb, :, :], dec[:, pb, 0, :, :], keep[:, bass.ds(b, 1)], None,
                                     ALU.mult).then_inc(s["dec_kept"], 1)
                if live(c):
                    at(dve, s["o_gated_made"], c)
                    at(dve, s["o_rs_made"], c)
                    at(dve, s["o_turned"], c - 1)
                    ve.tensor_tensor(heads(o_n[:, :]), heads(o[:, :]), over_heads(o_rs[:, :]),
                                     ALU.mult).then_inc(s["o_n_made"], 1)
                if live(b):
                    at(dve, s["k2d_made"], b)
                    at(dve, s["k2_faced"], b)
                    at(dve, s["kv1_made"], b - 2)
                    ve.tensor_tensor(heads(kt2[:, pb, :]), heads(e2m[:, :]), over_heads(k2_fac[:, :]),
                                     ALU.mult).then_inc(s["kt2_made"], 1)
                if live(a):
                    at(dve, s["w_made"], a)
                    at(dve, s["resid_made"], a)
                    at(dve, s["x1_moved"], a - 2)
                    ve.tensor_tensor(x1[:, pa, :], bank[7][:, :], resid[:, :], ALU.add).then_inc(s["x1_made"], 1)
                    at(dve, s["x1_made"], a)
                    ve.bn_stats(stat2[:, :], x1[:, pa, :]).then_inc(s["x1_stats"], 1)
                    at(dve, s["x1_stats"], a)
                    at(dve, s["xn_made"], a - 1)
                    ve.memset(idle[:, :], 0.0)
                    ve.bn_aggr(mv2[:, :], stat2[:, :]).then_inc(s["x1_mean"], 1)
                    at(dve, s["x1_mean"], a)
                    at(dve, s["x1_rs"], a - 1)
                    ve.tensor_scalar(var2[:, :], mv2[:, 1:2], LN_EPS, None, ALU.add).then_inc(s["x1_var"], 1)
                    at(dve, s["x1_rs"], a)
                    at(dve, s["xn_turned"], a - 1)
                    ve.tensor_scalar(xn[:, :], x1[:, pa, :], mv2[:, 0:1], rs2[:, 0:1], ALU.subtract,
                                     ALU.mult).then_inc(s["xn_made"], 1)
                if live(c):
                    at(dve, s["y_made"], c)
                    at(dve, s["x1_moved"], c)
                    moved(dve, res_out, c - 2, pc)
                    ve.tensor_tensor(res[:, pc, :], bank[2][:, :], x1_late[:, pc, :], ALU.add).then_inc(s["res_made"], 1)

            run(dve, step)


_INS = ['x', 'ctx_2048', 'mask_BxS2_if0', 'L0_xattn_W_in', 'L0_xattn_b_in', 'L0_xattn_g_res', 'L0_xattn_g_init',
        'L0_ffn_Wq', 'L0_ffn_Wk', 'L0_ffn_Wv', 'L0_ffn_Wqa', 'L0_ffn_Wqb', 'L0_ffn_Wka', 'L0_ffn_Wkb',
        'L0_ffn_Wg1a', 'L0_ffn_Wg1b', 'L0_ffn_bg1', 'L0_ffn_Wg2a', 'L0_ffn_Wg2b', 'L0_ffn_bg2', 'L0_ffn_We',
        'L0_ffn_Wga', 'L0_ffn_Wgb', 'L0_ffn_norm_w', 'L0_ffn_Wo']


def kernel(**inputs):
    import numpy as np
    import concourse.bacc as bacc
    from concourse.bass_utils import run_bass_kernel_spmd

    nc = bacc.Bacc("TRN2", target_bir_lowering=False, num_devices=1)
    arrays, args = {}, []
    for name in _INS:
        a = np.ascontiguousarray(inputs[name])
        arrays[f"in_{name}"] = a
        args.append(nc.dram_tensor(f"in_{name}", a.shape, mybir.dt.from_np(a.dtype), kind="ExternalInput").ap())
    out = nc.dram_tensor("out", inputs["x"].shape, F32, kind="ExternalOutput").ap()
    xattn_ffn(nc, *args, out)
    r = run_bass_kernel_spmd(nc, [arrays], core_ids=[0])
    return r.results[0]["out"]
```

```python
import math
from contextlib import ExitStack

import concourse.bass as bass
from concourse import mybir

ALU = mybir.AluOpType
ACT = mybir.ActivationFunctionType
AX = mybir.AxisListType
F32 = mybir.dt.float32
BF16 = mybir.dt.bfloat16
I32 = mybir.dt.int32

LOOP_FROM, UNROLL = 4, 2
P = 128
D = 512
KC = D // P
H, DK = 8, 64
PAIRS = H // 2
NE = 4
SLOTS = 1 + NE
LORA, GLR = 64, 16
LN_EPS = 1e-5
RMS_EPS = 1e-5
NORMALIZER = 16.0
SCALE = DK ** -0.5
LOGP = -0.001
B_COEF = math.exp(LOGP)
SELECTED = 12
SMALL = 5 + 5 + 5 + 2
LN_A = math.log(-math.expm1(LOGP))


def xattn_ffn(nc, x, ctx_in, lens, w_in, b_in, g_res, g_init, wq, wk, wv, wqa, wqb, wka, wkb,
              wg1a, wg1b, bg1, wg2a, wg2b, bg2, we, wga, wgb, norm_w, wo, out):
    B, S, _ = x.shape
    PLEN, DG = ctx_in.shape[1], ctx_in.shape[2]
    TB = S // P
    NT = B * TB
    LC = -(-PLEN // P)
    LCF = PLEN // P
    TAIL = PLEN - LCF * P
    NCOL = B * LC
    x_rows = x.rearrange("b s d -> (b s) d")
    out_rows = out.rearrange("b s d -> (b s) d")
    ctx_rows = ctx_in.rearrange("b p d -> (b p) d")

    stack = ExitStack()
    with stack:
        def sb(name, shape, dt=F32):
            return stack.enter_context(nc.sbuf_tensor(name, shape, dt))

        def sem(name):
            return stack.enter_context(nc.semaphore(name))

        bank = [stack.enter_context(nc.psum_tensor(f"bank{i}", [P, D], F32)) for i in range(8)]

        ident = sb("ident", [P, P])
        triu = sb("triu", [P, P])
        triu_b = sb("triu_b", [P, P], BF16)
        ones = sb("ones", [P, P])
        ones_b = sb("ones_b", [P, P], BF16)
        cum_mat = sb("cum_mat", [P, P])
        half_z = sb("half_z", [P, 2])
        rank = sb("rank", [P, NE])
        minus_half = sb("minus_half", [P, H])
        row_no = sb("row_no", [P, 1])
        carry_bias = sb("carry_bias", [P, 1])
        last_row = sb("last_row", [P, 1])
        bias_rows = sb("bias_rows", [P, 1])
        keep = sb("keep", [P, NT + UNROLL])
        w_in_s = sb("w_in_s", [P, KC, D])
        wq_s = sb("wq_s", [P, KC, D])
        wk_s = sb("wk_s", [P, KC, D])
        wv_s = sb("wv_s", [P, KC, D])
        wo_s = sb("wo_s", [P, KC, D])
        w_low = sb("w_low", [P, KC, 2 * P])
        we_s = sb("we_s", [P, KC, NE])
        w_up = sb("w_up", [P, 2, D])
        g_res_s = sb("g_res_s", [P, KC])
        b_in_s = sb("b_in_s", [P, D])
        g_init_s = sb("g_init_s", [P, D])
        norm_s = sb("norm_s", [P, DK])
        bound = sb("bound", [P, NT + UNROLL])
        started = sb("started", [P, NT + UNROLL])
        unstarted = sb("unstarted", [P, NT + UNROLL])
        first_row = sb("first_row", [1, NT], I32)

        lens_rows = sb("lens_rows", [P, P], I32)

        xs = sb("xs", [P, 2, D])
        ctx = sb("ctx", [P, 2, DG])
        stat = sb("stat", [P, 6])
        stat2 = sb("stat2", [P, 6])
        mv = sb("mv", [P, 2])
        mv2 = sb("mv2", [P, 2])
        var_a = sb("var_a", [P, 2])
        rs_a = sb("rs_a", [P, 2])
        ctx_ss = sb("ctx_ss", [P, 1])
        var2 = sb("var2", [P, 1])
        idle = sb("idle", [P, 1])
        rs2 = sb("rs2", [P, 1])
        xhat = sb("xhat", [P, D])
        xhat_t = sb("xhat_t", [P, KC, P])
        tri_bound = sb("tri_bound", [P, P], BF16)
        ctx_bin = sb("ctx_bin", [P, DG], BF16)
        dist = sb("dist", [P, P])
        dist_p = sb("dist_p", [P, P])
        decay_w = sb("decay_w", [P, P])
        carry_y = sb("carry_y", [P, P])
        in_past = sb("in_past", [P, P])
        w_depool = sb("w_depool", [P, P])
        w_carry = sb("w_carry", [P, P])
        depool = sb("depool", [P, 2, D])
        x_plus_b = sb("x_plus_b", [P, D])
        dep_g = sb("dep_g", [P, D])
        resid = sb("resid", [P, D])
        x1 = sb("x1", [P, 2, D])
        xn = sb("xn", [P, D])
        xn_t = sb("xn_t", [P, 2, KC, P])
        x1_late = sb("x1_late", [P, 2, D])
        low = sb("low", [P, 2 * P])
        l_max = sb("l_max", [P, 1])
        l_sub = sb("l_sub", [P, NE])
        l_exp = sb("l_exp", [P, NE])
        l_sum = sb("l_sum", [P, 1])
        l_rank = sb("l_rank", [P, NE])
        l_best = sb("l_best", [P, 1])
        onehot = sb("onehot", [P, NE])
        onehot_late = sb("onehot_late", [P, 2, NE])
        fac = sb("fac", [P, 1])
        fac_q = sb("fac_q", [P, 1])
        onehot_t = sb("onehot_t", [NE, P], BF16)
        mask2 = sb("mask2", [P, 2, P])
        cum_mat2 = sb("cum_mat2", [P, P])
        z2_half = sb("z2_half", [P, 2, NE])
        q1 = sb("q1", [P, D])
        k1 = sb("k1", [P, D])
        q2 = sb("q2", [P, D])
        v = sb("v", [P, 2, D])
        v_e = sb("v_e", [P, NE, D])
        gate_l = sb("gate_l", [P, 3, D])
        g_norm = sb("g_norm", [P, D])
        sig = sb("sig", [P, D])
        g_silu = sb("g_silu", [P, 2, D])
        k2_max = sb("k2_max", [P, H])
        k2_exp = sb("k2_exp", [P, D])
        k2_sum = sb("k2_sum", [P, H])
        k2_rec = sb("k2_rec", [P, H])
        k2_fac = sb("k2_fac", [P, H])
        e1p = sb("e1p", [P, D])
        e1m = sb("e1m", [P, D])
        e2p = sb("e2p", [P, D])
        e2m = sb("e2m", [P, D])
        dec = sb("dec", [P, 2, 2, PAIRS, SLOTS])
        dec_first = sb("dec_first", [P, 2, PAIRS, SLOTS])
        kt1 = sb("kt1", [P, 2, D])
        kt2 = sb("kt2", [P, 2, D])
        q1_t = sb("q1_t", [P, PAIRS, P])
        k1_t = sb("k1_t", [P, PAIRS, P])
        q2_t = sb("q2_t", [P, PAIRS, P])
        k2_t = sb("k2_t", [P, PAIRS, P])
        scratch = sb("scratch", [P, 4, 4, P])
        att1 = sb("att1", [P, 2, PAIRS, P])
        att2 = sb("att2", [P, 2, PAIRS, P])
        state = sb("state", [P, PAIRS, SLOTS, DK])
        o = sb("o", [P, D])
        o_sq = sb("o_sq", [P, D])
        o_ss = sb("o_ss", [P, H])
        o_var = sb("o_var", [P, H])
        o_rs = sb("o_rs", [P, H])
        o_n = sb("o_n", [P, D])
        o_t = sb("o_t", [P, KC, P])
        res = sb("res", [P, 2, D])
        lens_i = lens_rows[0:NCOL, :]
        lens_i32 = lens_i
        lens_f = scratch[0:NCOL, 0, 1, :]
        lens_t = scratch[:, 0, 2, 0:NCOL]
        totals = scratch[:, 0, 3, 0:NCOL].rearrange("p (b c) -> p b c", b=B)
        offs = scratch[:, 1, 0, 0:NCOL].rearrange("p (b c) -> p b c", b=B)
        ends = scratch[:, 1, 1, 0:NCOL].rearrange("p (b c) -> p b c", b=B)
        wrapped = scratch[:, 1, 2, 0:NCOL]
        hi_no = scratch[:, 1, 3, 0:NCOL]
        w_in_rows = ctx[:, :, :].rearrange("p a n -> p (a n)").rearrange("p (c n) -> p c n", c=KC)
        lo_no = scratch[:, 2, 0, 0:NCOL]
        thr = scratch[:, 2, 1, 0:TB + 1]
        col_no = scratch[:, 2, 2, :]
        row_start = scratch[:, 2, 3, 0:NT].rearrange("p (b t) -> p b t", b=B)
        before = scratch[:, 3, 0, 0:NT].rearrange("p (b t) -> p b t", b=B)
        tile_tot = scratch[:, 3, 1, 0:NT].rearrange("p (b t) -> p b t", b=B)
        row_first = scratch[:, 3, 2, 0:NT].rearrange("p (b t) -> p b t", b=B)
        reached = v_e[:, 0:2, :].bitcast(BF16).rearrange("p a n -> p (a n)")[:, 0:NCOL * (TB + 1)]\
            .rearrange("p (c j) -> p c j", j=TB + 1)
        hi_hot = v_e[:, 2:4, :].bitcast(BF16).rearrange("p a n -> p (a n)")[:, 0:NCOL * TB]\
            .rearrange("p (c j) -> p c j", j=TB)
        lo_hot = [att1[:, :, :, :].bitcast(BF16).rearrange("p j a n -> p (j a n)")[:, 0:LC * P],
                  gate_l[:, :, :].bitcast(BF16).rearrange("p a n -> p (a n)")[:, 0:LC * P]]
        lo_hot = [h.rearrange("p (c n) -> p c n", n=P) for h in lo_hot]

        s = {n: sem(n) for n in """
            consts_made consts_selected weights_in lens_in small_in lens_float lens_turned lens_summed
            prologue_step g_scaled counts_ready w_in_turned hot_ready hot_used totals_ready tables_ready
            x_stats x_mean x_var a_rs xhat_made xhat_turned xhat_t_made
            ctx_sq ctx_var tri_made cum_made dist_made dist_pos decay_made carry_made past_made dep_w_made
            dep_made dep_copied xb_made dep_scaled resid_made w_made x1_made x1_stats x1_mean x1_var x1_rs
            xn_made xn_turned xn_t_made x1_moved
            low_made logits_made low_copied l_max_made l_read l_sub_made l_rank_made l_best_made onehot_made l_exp_made fac_made facq_made
            q1_made k1_made v_made q1_copied k1_copied v_copied
            q2_made k2_made q2_copied k2_maxed k2_subbed k2_exped k2_summed k2_reced k2_faced
            g_normed sig_made silu_made
            hot_turned hot_t_made same_made same_used z2_made
            gt1_made gt2_made dec_made gt1_exped gt2_exped dec_exped dec_kept
            qt1_made qt2_made k2d_made kt1_made kt2_made
            q1_turned k1_turned q2_turned k2_turned q1_t_made k1_t_made q2_t_made k2_t_made 
            a1_made a2_made a1e_masked a1o_masked a2e_masked a2o_masked att_summed state_first o_even_made o_base_made o_half_made o_made o_sum o_sq_made kv0_made kv1_made kvd_made kv0_added kv1_added
            state_added state_made o_summed o_var_made o_rs_made o_gated_made o_n_made
            o_turned o_t_made y_made res_made
            """.split()}

        z_made = [sem(f"z_made{j}") for j in range(3)]
        z_min = [sem(f"z_min{j}") for j in range(3)]
        z_exp = [sem(f"z_exp{j}") for j in range(3)]
        z_ln = [sem(f"z_ln{j}") for j in range(3)]
        l_made = [sem(f"l_made{j}") for j in range(3)]

        x_in = [sem(f"x_in{j}") for j in range(2)]
        ctx_loaded = [sem(f"ctx_loaded{j}") for j in range(2)]
        res_out = [sem(f"res_out{j}") for j in range(2)]

        def moved(eng, semaphores, tile, par):
            if not isinstance(tile, int) or tile >= 0:
                eng.wait_ge(semaphores[par], (tile - par) * 8 + 16)

        def at(eng, semaphore, tile):
            if isinstance(tile, int):
                if tile < 0:
                    return
                tile = min(tile, NT - 1)
            eng.wait_ge(semaphore, tile + 1)

        def summed(eng, tile, parts=2 * NE + 1):
            eng.wait_ge(s["o_sum"], (2 * NE + 1) * tile + parts)

        def heads(a):
            return a.rearrange("p (h d) -> p h d", h=H)

        def over_heads(col):
            return col.unsqueeze(2).to_broadcast([P, H, DK])


        def run(eng, step):
            for i in range(LOOP_FROM):
                step(i, i % UNROLL)
            with eng.Fori(LOOP_FROM, NT, UNROLL) as i:
                for u in range(UNROLL):
                    step(i + u, u)
            for i in range(NT, NT + 2):
                step(i, i % UNROLL)

        def live(tile):
            return not isinstance(tile, int) or 0 <= tile < NT

        block = stack.enter_context(nc.Block())

        @block.sync
        def _(sp):
            sp.wait_ge(s["consts_made"], 1)
            for b in range(B):
                sp.dma_start(lens_i[b * LCF:(b + 1) * LCF, :],
                             lens[b, 0:LCF * P].rearrange("(c k) -> c k", k=P)).then_inc(s["lens_in"], 16)
            sp.dma_start(lens_i[B * LCF:NCOL, 0:TAIL], lens[:, LCF * P:PLEN]).then_inc(s["lens_in"], 16)
            for dst, src in ((w_in_rows, w_in), (wq_s, wq), (wk_s, wk), (wv_s, wv), (wo_s, wo)):
                sp.dma_start(dst[:, :, :], src.rearrange("(c p) n -> p c n", p=P)).then_inc(s["weights_in"], 16)

            def load_x(t, par):
                at(sp, s["xb_made"], t - 2)
                at(sp, s["xhat_made"], t - 2)
                sp.dma_start(xs[:, par, :], x_rows[bass.ds(t * P, P), :]).then_inc(x_in[par], 16)

            def load_ctx(t, par):
                at(sp, s["dep_made"], t - 2)
                at(sp, s["ctx_sq"], t - 2)
                row = sp.value_load(first_row[0:1, bass.ds(t, 1)], min_val=0, max_val=B * PLEN - P)
                sp.dma_start(ctx[:, par, :], ctx_rows[bass.ds(row, P), :]).then_inc(ctx_loaded[par], 16)

            load_x(0, 0)
            sp.wait_ge(s["tables_ready"], 1)
            sp.wait_ge(s["w_in_turned"], 1)

            load_ctx(0, 0)

            def step(i, u):
                if not isinstance(i, int) or i + 1 < NT:
                    load_ctx(i + 1, 1 - u)
                    load_x(i + 1, 1 - u)
                if live(i - 2):
                    at(sp, s["res_made"], i - 2)
                    sp.dma_start(out_rows[bass.ds((i - 2) * P, P), :], res[:, u, :]).then_inc(res_out[u], 16)

            for i in range(LOOP_FROM):
                step(i, i % 2)
            with sp.Fori(LOOP_FROM, NT - 2, 2) as i:
                for u in range(2):
                    step(i + u, u)
            for i in range(NT - 2, NT + 2):
                step(i, i % 2)
            for par in range(2):
                moved(sp, res_out, NT - 2 + par, par)

        @block.gpsimd
        def _(pool):
            g = nc.gpsimd
            g.memset(lens_rows[:, :], 0)
            g.memset(ones[:, :], 1.0)
            g.memset(ones_b[:, :], 1.0)
            g.memset(ident[:, :], 0.0)
            g.memset(cum_mat[:, :], 0.0)
            g.memset(half_z[:, :], -1.0 / NORMALIZER)
            g.memset(minus_half[:, :], -0.5)
            g.memset(last_row[:, :], 0.0)
            g.memset(bias_rows[:, :], 0.0)
            g.memset(keep[:, :], 1.0)
            g.memset(w_low[:, :, :], 0.0)
            g.memset(state[:, :, :, :], 0.0)
            g.memset(depool[:, 1, :], 0.0)
            g.iota(row_no[:, :], pattern=[[0, 1]], base=1, channel_multiplier=1,
                   allow_small_or_imprecise_dtypes=True)
            g.iota(rank[:, :], pattern=[[-1, NE]], base=NE, channel_multiplier=0,
                   allow_small_or_imprecise_dtypes=True)
            g.iota(thr, pattern=[[P, TB + 1]], base=0, channel_multiplier=0,
                   allow_small_or_imprecise_dtypes=True)
            g.iota(col_no, pattern=[[1, P]], base=0, channel_multiplier=0,
                   allow_small_or_imprecise_dtypes=True)
            g.iota(row_start, pattern=[[PLEN, B], [0, TB]], base=0, channel_multiplier=0,
                   allow_small_or_imprecise_dtypes=True).then_inc(s["consts_made"], 1)
            pool.wait_ge(s["consts_made"], 1)
            done = 0

            def then(ins):
                nonlocal done
                done += 1
                ins.then_inc(s["consts_selected"], 1)
                pool.wait_ge(s["consts_selected"], done)

            then(g.affine_select(out=ident[:, :], in_=ident[:, :], compare_op=ALU.not_equal, fill=1.0, base=0,
                            pattern=[[-1, P]], channel_multiplier=1))
            then(g.affine_select(out=triu[:, :], in_=ones[:, :], compare_op=ALU.is_ge, fill=0.0, base=0,
                            pattern=[[1, P]], channel_multiplier=-1))
            then(g.affine_select(out=triu_b[:, :], in_=ones_b[:, :], compare_op=ALU.is_ge, fill=0.0, base=0,
                            pattern=[[1, P]], channel_multiplier=-1))
            then(g.affine_select(out=cum_mat[0:64, :], in_=cum_mat[0:64, :], compare_op=ALU.is_ge,
                            fill=1.0 / NORMALIZER, base=0, pattern=[[1, P]], channel_multiplier=-1))
            then(g.affine_select(out=cum_mat[64:P, :], in_=cum_mat[64:P, :], compare_op=ALU.is_gt,
                            fill=-1.0 / NORMALIZER, base=64, pattern=[[-1, P]], channel_multiplier=1))
            then(g.memset(half_z[64:P, 0:1], 0.0))
            then(g.memset(half_z[0:64, 1:2], 0.0))
            then(g.affine_select(out=last_row[:, :], in_=last_row[:, :], compare_op=ALU.not_equal, fill=1.0,
                            base=-(P - 1), pattern=[[0, 1]], channel_multiplier=1))
            then(g.affine_select(out=bias_rows[:, :], in_=bias_rows[:, :], compare_op=ALU.not_equal, fill=1.0,
                            base=-(LORA + GLR), pattern=[[0, 1]], channel_multiplier=1))
            then(g.affine_select(out=bias_rows[:, :], in_=bias_rows[:, :], compare_op=ALU.not_equal, fill=1.0,
                            base=-(96 + GLR), pattern=[[0, 1]], channel_multiplier=1))
            then(g.memset(keep[:, 0:NT].rearrange("p (b t) -> p b t", t=TB)[:, :, 0:1], 0.0))
            then(g.tensor_scalar(carry_bias[:, :], row_no[:, :], LN_A, 0.0, ALU.mult, ALU.add))

            def step(i, u):
                a, b, c = i, i - 1, i - 2
                pa, pb, pc = u, 1 - u, u
                if live(c):
                    at(pool, s["dec_kept"], c)
                    at(pool, s["state_made"], c - 1)
                    g.tensor_tensor(state[:, :, :, :], state[:, :, :, :],
                                    dec_first[:, pc, :, :].unsqueeze(3).to_broadcast([P, PAIRS, SLOTS, DK]),
                                    ALU.mult).then_inc(s["state_first"], 1)
                if live(a):
                    at(pool, s["x_var"], a)
                    at(pool, s["ctx_var"], a)
                    at(pool, s["past_made"], a - 1)
                    at(pool, s["xhat_made"], a - 1)
                    g.tensor_tensor(rs_a[:, :], var_a[:, :], minus_half[:, 0:2], ALU.pow).then_inc(s["a_rs"], 1)
                    at(pool, s["resid_made"], a - 1)
                    at(pool, s["x1_made"], b)
                    at(pool, s["res_made"], b - 2)
                    g.tensor_tensor(x_plus_b[:, :], xs[:, pa, :], b_in_s[:, :], ALU.add).then_inc(s["xb_made"], 1)
                if live(b):
                    if not live(a):
                        at(pool, s["x1_made"], b)
                        at(pool, s["res_made"], b - 2)
                    g.tensor_copy(x1_late[:, pb, :], x1[:, pb, :]).then_inc(s["x1_moved"], 1)
                if live(c):
                    for j, one, two in ((0, s["a1e_masked"], s["a2e_masked"]), (1, s["a1o_masked"], s["a2o_masked"])):
                        at(pool, one, c)
                        at(pool, two, c)
                        g.tensor_tensor(att1[:, j, :, :], att1[:, j, :, :], att2[:, j, :, :],
                                        ALU.add).then_inc(s["att_summed"], 1)
                if live(b):
                    at(pool, s["sig_made"], b)
                    at(pool, s["g_normed"], b)
                    at(pool, s["o_gated_made"], b - 2)
                    g.tensor_tensor(g_silu[:, pb, :], g_norm[:, :], sig[:, :], ALU.mult).then_inc(s["silu_made"], 1)
                if live(c):
                    at(pool, s["o_sq_made"], c)
                    at(pool, s["silu_made"], c)
                    g.tensor_tensor(o[:, :], o[:, :], g_silu[:, pc, :], ALU.mult).then_inc(s["o_gated_made"], 1)
                    at(pool, s["o_var_made"], c)
                    g.tensor_tensor(o_rs[:, :], o_var[:, :], minus_half[:, :], ALU.pow).then_inc(s["o_rs_made"], 1)
                if live(b):
                    at(pool, s["gt1_exped"], b)
                    at(pool, s["k1_copied"], b)
                    at(pool, s["kvd_made"], b - 2)
                    at(pool, s["k1_turned"], b - 1)
                    g.tensor_tensor(kt1[:, pb, :], k1[:, :], e1m[:, :], ALU.mult).then_inc(s["kt1_made"], 1)
                    at(pool, s["gt2_exped"], b)
                    at(pool, s["k2_exped"], b)
                    at(pool, s["kt2_made"], b - 1)
                    g.tensor_tensor(e2m[:, :], k2_exp[:, :], e2m[:, :], ALU.mult).then_inc(s["k2d_made"], 1)
                if live(a):
                    at(pool, s["dep_copied"], a)
                    g.tensor_tensor(dep_g[:, :], depool[:, pa, :], g_init_s[:, :], ALU.mult).then_inc(s["dep_scaled"], 1)
                    at(pool, s["dep_scaled"], a)
                    at(pool, s["xb_made"], a)
                    at(pool, s["x1_made"], a - 1)
                    g.tensor_tensor(resid[:, :], dep_g[:, :], x_plus_b[:, :], ALU.add).then_inc(s["resid_made"], 1)
                    at(pool, s["x1_var"], a)
                    at(pool, s["xn_made"], a - 1)
                    g.tensor_tensor(rs2[:, :], var2[:, :], minus_half[:, 0:1], ALU.pow).then_inc(s["x1_rs"], 1)
                if live(c):
                    at(pool, s["state_added"], c)
                    g.tensor_tensor(state[:, :, :, :], state[:, :, :, :],
                                    dec[:, pc, 1, :, :].unsqueeze(3).to_broadcast([P, PAIRS, SLOTS, DK]),
                                    ALU.mult).then_inc(s["state_made"], 1)

            run(pool, step)

        @block.scalar
        def _(act):
            sc = nc.scalar
            sc.preload_act_table_set("natural_log_exp_and_others")
            sc.dma_start(g_res_s[:, :], g_res.rearrange("(c p) -> p c", p=P),
                         allow_slow_non_contiguous=True).then_inc(s["small_in"], 16)
            sc.dma_start(b_in_s[:, :], b_in.unsqueeze(0).to_broadcast([P, D])).then_inc(s["small_in"], 16)
            sc.dma_start(g_init_s[:, :], g_init[0:D].unsqueeze(0).to_broadcast([P, D])).then_inc(s["small_in"], 16)
            sc.dma_start(norm_s[:, :], norm_w.unsqueeze(0).to_broadcast([P, DK])).then_inc(s["small_in"], 16)
            sc.dma_start(we_s[:, :, :], we.rearrange("(c p) n -> p c n", p=P)).then_inc(s["small_in"], 16)
            act.wait_ge(s["consts_made"], 1)
            for c0, w, src in ((0, LORA, wqa), (LORA, LORA, wka), (P, LORA, wga), (P + 64, GLR, wg1a),
                               (P + 96, GLR, wg2a)):
                sc.dma_start(w_low[:, :, c0:c0 + w], src.rearrange("(c p) n -> p c n", p=P)).then_inc(s["small_in"], 16)
            for r0, h, src in ((0, 0, wqb), (64, 0, wkb), (0, 1, wgb), (64, 1, wg1b), (96, 1, wg2b)):
                sc.dma_start(w_up[r0:r0 + src.shape[0], h, :], src).then_inc(s["small_in"], 16)
            for r0, src in ((64 + GLR, bg1), (96 + GLR, bg2)):
                sc.dma_start(w_up[r0:r0 + 1, 1, :], src.unsqueeze(0)).then_inc(s["small_in"], 16)

            def step(i, u):
                a, b, c = i, i - 1, i - 2
                pa, pb, pc = u, 1 - u, u
                if live(a):
                    moved(act, ctx_loaded, a, pa)
                    at(act, s["ctx_var"], a - 1)
                    sc.activation(ctx_bin[:, :], ctx[:, pa, :], ACT.Square, accum_out=ctx_ss[:, :]).then_inc(s["ctx_sq"], 1)
                if live(b):
                    at(act, s["l_sub_made"], b)
                    at(act, s["fac_made"], b - 1)
                    sc.activation(l_exp[:, :], l_sub[:, :], ACT.Exp, accum_out=l_sum[:, :]).then_inc(s["l_exp_made"], 1)
                if live(a):
                    at(act, s["xhat_turned"], a)
                    at(act, s["w_made"], a - 1)
                    sc.copy(xhat_t[:, :, :], bank[0][:, :].rearrange("p (c t) -> p c t", c=KC)).then_inc(s["xhat_t_made"], 1)
                    at(act, s["dist_pos"], a)
                    at(act, s["dep_w_made"], a - 1)
                    sc.activation(decay_w[:, :], dist_p[:, :], ACT.Exp, scale=LN_A).then_inc(s["decay_made"], 1)
                    sc.activation(carry_y[96:P, :], dist[96:P, :], ACT.Exp, scale=LN_A,
                                  bias=carry_bias[96:P, :]).then_inc(s["carry_made"], 1)
                if live(b):
                    at(act, s["q1_made"], b)
                    at(act, s["qt1_made"], b - 1)
                    sc.mul(q1[:, :], bank[7][:, :], SCALE).then_inc(s["q1_copied"], 1)
                    at(act, z_min[0], b)
                    sc.activation(gate_l[:, 0, :], gate_l[:, 0, :], ACT.Exp).then_inc(z_exp[0], 1)
                    at(act, z_min[2], b)
                    sc.activation(gate_l[:, 2, :], gate_l[:, 2, :], ACT.Exp).then_inc(z_exp[2], 1)
                    at(act, z_exp[0], b)
                    sc.activation(gate_l[:, 0, :], gate_l[:, 0, :], ACT.Ln, bias=1.0).then_inc(z_ln[0], 1)
                    at(act, s["q2_made"], b)
                    at(act, s["facq_made"], b)
                    at(act, s["qt2_made"], b - 1)
                    sc.mul(q2[:, :], bank[4][:, :], fac_q[:, 0:1]).then_inc(s["q2_copied"], 1)
                    at(act, z_exp[2], b)
                    sc.activation(gate_l[:, 2, :], gate_l[:, 2, :], ACT.Ln, bias=1.0).then_inc(z_ln[2], 1)
                    at(act, z_min[1], b)
                    sc.activation(gate_l[:, 1, :], gate_l[:, 1, :], ACT.Exp).then_inc(z_exp[1], 1)
                    at(act, s["k1_made"], b)
                    at(act, s["kt1_made"], b - 1)
                    sc.copy(k1[:, :], bank[3][:, :]).then_inc(s["k1_copied"], 1)
                    at(act, z_exp[1], b)
                    sc.activation(gate_l[:, 1, :], gate_l[:, 1, :], ACT.Ln, bias=1.0).then_inc(z_ln[1], 1)
                    at(act, s["k2_subbed"], b)
                    sc.activation(k2_exp[:, :], k2_exp[:, :], ACT.Exp).then_inc(s["k2_exped"], 1)
                    at(act, l_made[2], b)
                    at(act, s["silu_made"], b - 1)
                    sc.activation(sig[:, :], gate_l[:, 2, :], ACT.Exp, scale=-1.0).then_inc(s["sig_made"], 1)
                if live(b):
                    at(act, s["gt1_made"], b)
                    at(act, s["q1_turned"], b - 1)
                    at(act, s["kt1_made"], b - 1)
                    sc.activation(e1p[:, :], bank[0][:, :], ACT.Exp)
                    sc.activation(e1m[:, :], bank[0][:, :], ACT.Exp, scale=-1.0).then_inc(s["gt1_exped"], 1)
                    at(act, s["gt2_made"], b)
                    at(act, s["q2_turned"], b - 1)
                    at(act, s["kt2_made"], b - 1)
                    sc.activation(e2p[:, :], bank[1][:, :], ACT.Exp)
                    sc.activation(e2m[:, :], bank[1][:, :], ACT.Exp, scale=-1.0).then_inc(s["gt2_exped"], 1)
                if live(c):
                    summed(act, c)
                    at(act, s["o_summed"], c - 1)
                    sc.activation(o_sq[:, :], o[:, :], ACT.Square).then_inc(s["o_sq_made"], 1)
                if live(a):
                    at(act, s["dep_made"], a)
                    at(act, s["dep_scaled"], a - 2)
                    sc.copy(depool[:, pa, :], bank[5][:, :]).then_inc(s["dep_copied"], 1)
                if live(b):
                    at(act, s["v_made"], b)
                    at(act, s["kvd_made"], b - 2)
                    at(act, s["onehot_made"], b)
                    sc.copy(v[:, pb, :], bank[3][:, :])
                    at(act, s["kv1_made"], b - 1)
                    for e in range(NE):
                        last = sc.mul(v_e[:, e, :], bank[3][:, :], onehot[:, e:e + 1])
                    last.then_inc(s["v_copied"], 1)
                    at(act, s["dec_made"], b)
                    at(act, s["state_made"], b - 2)
                    at(act, s["dec_kept"], b - 2)
                    dv = dec[:, pb, :, :, :].rearrange("p j a s -> p a j s")
                    sc.activation(dv[:, :, :, 0:1], bank[2][:, 0:2 * PAIRS].rearrange("p (a j s) -> p a j s", a=PAIRS, j=2),
                                  ACT.Exp)
                    for j in range(2):
                        last = sc.activation(dv[:, :, j, 1:SLOTS],
                                      bank[2][:, 8:8 + 2 * PAIRS * NE].rearrange("p (a j s) -> p a j s", a=PAIRS, j=2)[:, :, j, :],
                                      ACT.Exp)
                    last.then_inc(s["dec_exped"], 1)
                if live(b):
                    at(act, s["q1_turned"], b)
                    at(act, s["o_made"], b - 1)
                    sc.copy(q1_t[:, :, :], bank[3][:, :].rearrange("p (a t) -> p a t", a=PAIRS)).then_inc(s["q1_t_made"], 1)
                    at(act, s["k1_turned"], b)
                    sc.copy(k1_t[:, :, :], bank[4][:, :].rearrange("p (a t) -> p a t", a=PAIRS)).then_inc(s["k1_t_made"], 1)
                if live(c):
                    at(act, s["o_turned"], c)
                    at(act, s["y_made"], c - 1)
                    sc.copy(o_t[:, :, :], bank[6][:, :].rearrange("p (c t) -> p c t", c=KC)).then_inc(s["o_t_made"], 1)
                if live(b):
                    at(act, s["q2_turned"], b)
                    sc.copy(q2_t[:, :, :], bank[5][:, :].rearrange("p (a t) -> p a t", a=PAIRS)).then_inc(s["q2_t_made"], 1)
                if live(a):
                    at(act, s["xn_turned"], a)
                    at(act, s["v_made"], a - 2)
                    sc.copy(xn_t[:, pa, :, :], bank[1][:, :].rearrange("p (c t) -> p c t", c=KC)).then_inc(s["xn_t_made"], 1)
                if live(b):
                    at(act, s["k2_turned"], b)
                    sc.copy(k2_t[:, :, :], bank[0][:, :].rearrange("p (a t) -> p a t", a=PAIRS)).then_inc(s["k2_t_made"], 1)

            run(act, step)

        @block.tensor
        def _(pe):
            te = nc.tensor
            mm = te.matmul
            pe.wait_ge(s["consts_selected"], SELECTED)
            pe.wait_ge(s["lens_float"], 1)
            te.transpose(bank[0][:, 0:NCOL], lens_f, ident[0:NCOL, 0:NCOL]).then_inc(s["lens_turned"], 1)
            pe.wait_ge(s["lens_turned"], 2)
            mm(bank[1][:, 0:NCOL], triu[:, :], lens_t, start=True, stop=True)
            mm(bank[2][:, 0:NCOL], ones[:, :], lens_t, start=True, stop=True).then_inc(s["lens_summed"], 1)
            for b in range(B):
                pe.wait_ge(s["hot_ready"], b + 1)
                for k in range(LC):
                    last = mm(bank[3][:, b * TB:(b + 1) * TB], lo_hot[b % 2][:, k, :], hi_hot[:, b * LC + k, :],
                              start=(k == 0), stop=(k == LC - 1))
                last.then_inc(s["hot_used"], 1)
            pe.wait_ge(s["counts_ready"], 1)
            mm(bank[4][:, 0:NT], ones[:, :], bound[:, 0:NT], start=True, stop=True).then_inc(s["totals_ready"], 1)
            pe.wait_ge(s["weights_in"], 16 * 5)
            pe.wait_ge(s["tables_ready"], 2)
            for k in range(KC):
                for m in range(KC):
                    last = te.transpose(bank[4 + k][:, m * P:(m + 1) * P], w_in_rows[:, m, k * P:(k + 1) * P], ident[:, :])
            last.then_inc(s["w_in_turned"], 1)
            pe.wait_ge(s["small_in"], 16 * SMALL)
            pe.wait_ge(s["g_scaled"], 1)

            def rows(j):
                return slice(DK * j, DK * j + DK)

            def turn(bk, src):
                for k in range(KC):
                    last = te.transpose(bank[bk][:, k * P:(k + 1) * P], src[:, k * P:(k + 1) * P], ident[:, :])
                return last

            def product(bk, lhs_t, w):
                for k in range(KC):
                    last = mm(bank[bk][:, :], lhs_t[:, k, :], w[:, k, :], start=(k == 0), stop=(k == KC - 1))
                return last

            def step(i, u):
                a, b, c = i, i - 1, i - 2
                pa, pb, pc = u, 1 - u, u
                def attention(kt, qt, bk, pr):
                    for j in range(2):
                        last = mm(bank[bk + j][:, pr * P:(pr + 1) * P], kt[rows(j), pr, :], qt[rows(j), pr, :],
                                  start=True, stop=True)
                    return last

                if live(c):
                    at(pe, s["q1_t_made"], c)
                    at(pe, s["k1_t_made"], c)
                    for pr in range(PAIRS):
                        last = attention(k1_t, q1_t, 3, pr)
                    last.then_inc(s["a1_made"], 1)
                if live(b):
                    at(pe, s["xn_t_made"], b)
                    at(pe, s["res_made"], b - 2)
                    for h in range(2):
                        for k in range(KC):
                            last = mm(bank[2][:, h * P:(h + 1) * P], w_low[:, k, h * P:(h + 1) * P], xn_t[:, pb, k, :],
                                      start=(k == 0), stop=(k == KC - 1))
                    last.then_inc(s["low_made"], 1)
                if live(c):
                    at(pe, s["q2_t_made"], c)
                    at(pe, s["k2_t_made"], c)
                    at(pe, s["o_t_made"], c - 1)
                if live(b):
                    at(pe, s["x1_made"], b)
                for k in range(KC):
                    if live(c):
                        last = attention(k2_t, q2_t, 5, k)
                        if k == KC - 1:
                            last.then_inc(s["a2_made"], 1)
                    if live(b):
                        last = mm(bank[7][:, 0:NE], xn_t[:, pb, k, :], we_s[:, k, :],
                                  start=(k == 0), stop=(k == KC - 1))
                        if k == KC - 1:
                            last.then_inc(s["logits_made"], 1)
                if live(a):
                    at(pe, s["xhat_made"], a)
                    at(pe, s["k2_t_made"], a - 2)
                    turn(0, xhat).then_inc(s["xhat_turned"], 1)
                    at(pe, s["tri_made"], a)
                    at(pe, s["xn_t_made"], a - 1)
                    mm(bank[1][:, 0:P], ones_b[:, :], tri_bound[:, :], start=True, stop=True).then_inc(s["cum_made"], 1)
                if live(b):
                    at(pe, s["l_read"], b)
                    product(7, xn_t[:, pb], wq_s).then_inc(s["q1_made"], 1)
                    at(pe, s["onehot_made"], b)
                    at(pe, s["dist_made"], b + 1)
                    te.transpose(bank[1][0:NE, P:2 * P], onehot[:, :], ident[:, :]).then_inc(s["hot_turned"], 1)
                def head_cols(pr, j):
                    return slice((2 * pr + j) * DK, (2 * pr + j + 1) * DK)

                def dense(j):
                    for pr in range(PAIRS):
                        last = mm(bank[6][:, head_cols(pr, j)], q1_t[rows(j), pr, :], state[rows(j), pr, 0, :],
                                  start=(j == 0 and pr == 0), stop=(j == 1), skip_group_check=True)
                    return last

                def own(pr, j):
                    mm(bank[6][:, head_cols(pr, j)], att1[:, j, pr, :], v[:, pc, head_cols(pr, j)],
                       start=False, stop=(j == 0), skip_group_check=True)

                def routed(half, banks):
                    for pr in (2 * half, 2 * half + 1):
                        for j in range(2):
                            last = mm(bank[banks[j]][:, (pr % 2) * NE * DK:(pr % 2 + 1) * NE * DK], q2_t[rows(j), pr, :],
                                      state[rows(j), pr, 1:SLOTS, :], start=True, stop=True)
                    return last

                if live(b):
                    at(pe, s["low_copied"], b)
                    at(pe, s["xhat_t_made"], b + 1)
                    mm(bank[0][:, :], low[64:64 + GLR + 1, P:2 * P], w_up[64:64 + GLR + 1, 1, :],
                       start=True, stop=True).then_inc(z_made[0], 1)
                if live(c):
                    at(pe, s["a2o_masked"], c)
                    at(pe, s["state_first"], c)
                    dense(0).then_inc(s["o_even_made"], 1)

                def keys_and_own(k):
                    if live(b):
                        last = mm(bank[3][:, :], xn_t[:, pb, k, :], wk_s[:, k, :], start=(k == 0), stop=(k == KC - 1))
                        if k == KC - 1:
                            last.then_inc(s["k1_made"], 1)
                    if live(c):
                        if k % 2 == 0:
                            pe.wait_ge(s["att_summed"], 2 * c + 1 + k // 2)
                        own(2 * (k % 2), k // 2)
                        own(2 * (k % 2) + 1, k // 2)

                if live(b):
                    at(pe, s["a1e_masked"], b - 1)
                keys_and_own(0)
                if live(b):
                    mm(bank[2][:, :], low[0:LORA, P:2 * P], w_up[0:LORA, 1, :],
                       start=True, stop=True).then_inc(z_made[2], 1)
                    at(pe, s["hot_t_made"], b)
                    mm(bank[1][:, 2 * P:3 * P], onehot_t[:, :], onehot_t[:, :], start=True, stop=True).then_inc(s["same_made"], 1)
                keys_and_own(1)
                if live(b):
                    at(pe, s["a2e_masked"], b - 1)
                    mm(bank[5][:, :], low[64:P, 0:P], w_up[64:P, 0, :], start=True, stop=True).then_inc(s["k2_made"], 1)
                    at(pe, s["a1o_masked"], b - 1)
                    mm(bank[4][:, :], low[0:LORA, 0:P], w_up[0:LORA, 0, :], start=True, stop=True).then_inc(s["q2_made"], 1)
                keys_and_own(2)
                if live(b):
                    at(pe, s["same_used"], b)
                    mm(bank[1][:, :], low[96:96 + GLR + 1, P:2 * P], w_up[96:96 + GLR + 1, 1, :],
                       start=True, stop=True).then_inc(z_made[1], 1)
                keys_and_own(3)
                if live(c):
                    at(pe, s["o_even_made"], c)
                    dense(1).then_inc(s["o_base_made"], 1)
                if live(c):
                    at(pe, s["q1_copied"], c + 1)
                    at(pe, s["k1_copied"], c + 1)
                    routed(0, (7, 3)).then_inc(s["o_half_made"], 1)
                if live(b):
                    at(pe, l_made[0], b)
                    mm(bank[0][:, :], cum_mat[:, :], gate_l[:, 0, :], start=True, stop=True).then_inc(s["gt1_made"], 1)
                if live(c):
                    at(pe, s["q2_copied"], c + 1)
                    at(pe, s["k2_subbed"], c + 1)
                    routed(1, (4, 5)).then_inc(s["o_made"], 1)
                if live(b):
                    at(pe, l_made[1], b)
                    mm(bank[1][:, :], cum_mat2[:, :], gate_l[:, 1, :], start=True, stop=True).then_inc(s["gt2_made"], 1)
                if live(b):
                    if live(c):
                        summed(pe, c, NE)
                    at(pe, s["k1_copied"], b)
                    at(pe, l_made[2], b)
                    at(pe, s["g_normed"], b)
                    for k in range(KC):
                        last = mm(bank[3][:, :], xn_t[:, pb, k, :], wv_s[:, k, :], start=(k == 0), stop=(k == KC - 1))
                        if k == KC - 1:
                            last.then_inc(s["v_made"], 1)
                        mm(bank[2][:, 2 * k:2 * k + 2], gate_l[:, 0, k * P:(k + 1) * P], half_z[:, :],
                           start=True, stop=True)
                        last = mm(bank[2][:, 8 + 8 * k:16 + 8 * k], gate_l[:, 1, k * P:(k + 1) * P],
                                  z2_half[:, :, :].rearrange("p j e -> p (j e)"), start=True, stop=True)
                    last.then_inc(s["dec_made"], 1)
                if live(c):
                    summed(pe, c)
                if live(a):
                    at(pe, s["dep_w_made"], a)
                    at(pe, s["dep_copied"], a - 1)
                    mm(bank[5][:, :], w_depool[:, :], ctx[:, pa, 0:D], start=True, stop=False)
                    mm(bank[5][:, :], w_carry[96:P, :], depool[96:P, 1 - pa, :], start=False, stop=True,
                       tile_position=(96, 0)).then_inc(s["dep_made"], 1)
                if live(c):
                    for bk, prs, made in ((4, (0, 1), s["kv0_made"]), (5, (2, 3), s["kv1_made"])):
                        if bk == 5:
                            at(pe, s["dep_copied"], c + 2)
                        for n, pr in enumerate(prs):
                            for j in range(2):
                                hd = slice((2 * pr + j) * DK, (2 * pr + j + 1) * DK)
                                last = mm(bank[bk][rows(j), n * NE * DK:(n + 1) * NE * DK], kt2[:, pc, hd],
                                          v_e[:, :, hd], start=True, stop=True)
                        last.then_inc(made, 1)
                if live(a):
                    at(pe, s["xhat_t_made"], a)
                    if not live(c):
                        at(pe, s["q1_copied"], a - 1)
                for k in range(KC):
                    if live(a):
                        last = mm(bank[7][:, :], xhat_t[:, k, :], w_in_s[:, k, :], start=(k == 0), stop=(k == KC - 1))
                        if k == KC - 1:
                            last.then_inc(s["w_made"], 1)
                    if live(c):
                        for j in range(2):
                            last = mm(bank[6][rows(j), k * DK:(k + 1) * DK], kt1[:, pc, head_cols(k, j)],
                                      v[:, pc, head_cols(k, j)], start=True, stop=True)
                        if k == KC - 1:
                            last.then_inc(s["kvd_made"], 1)
                if live(b):
                    at(pe, s["qt1_made"], b)
                    at(pe, s["v_copied"], b)
                    turn(3, e1p).then_inc(s["q1_turned"], 1)
                    at(pe, s["kt1_made"], b)
                    at(pe, s["kv0_added"], b - 1)
                    turn(4, kt1[:, pb]).then_inc(s["k1_turned"], 1)
                if live(c):
                    at(pe, s["o_n_made"], c)
                    at(pe, s["state_added"], c)
                    turn(6, o_n).then_inc(s["o_turned"], 1)
                if live(b):
                    at(pe, s["qt2_made"], b)
                    at(pe, s["dep_copied"], b + 1)
                    at(pe, s["kv1_added"], b - 1)
                    turn(5, e2p).then_inc(s["q2_turned"], 1)
                if live(c):
                    at(pe, s["o_t_made"], c)
                    at(pe, s["dec_exped"], c + 1)
                    product(2, o_t, wo_s).then_inc(s["y_made"], 1)
                if live(a):
                    at(pe, s["xn_made"], a)
                    at(pe, s["gt2_exped"], a - 1)
                    turn(1, xn).then_inc(s["xn_turned"], 1)
                if live(b):
                    at(pe, s["kt2_made"], b)
                    at(pe, s["gt1_exped"], b)
                    turn(0, kt2[:, pb]).then_inc(s["k2_turned"], 1)

            run(pe, step)

        @block.vector
        def _(dve):
            ve = nc.vector
            n = 0

            def then(ins):
                nonlocal n
                n += 1
                ins.then_inc(s["prologue_step"], 1)
                dve.wait_ge(s["prologue_step"], n)

            dve.wait_ge(s["consts_made"], 1)
            dve.wait_ge(s["lens_in"], 16 * (B + 1))
            ve.tensor_copy(lens_f, lens_i32).then_inc(s["lens_float"], 1)
            dve.wait_ge(s["lens_turned"], 1)
            ve.tensor_copy(lens_t, bank[0][:, 0:NCOL]).then_inc(s["lens_turned"], 1)
            dve.wait_ge(s["lens_summed"], 1)

            def by_batch(ap):
                return ap[:, 0:B * LCF].rearrange("p (b c) -> p b c", b=B), ap[:, B * LCF:NCOL].unsqueeze(2)

            for dst, bk in ((ends, 1), (totals, 2)):
                full, tail = by_batch(bank[bk])
                ve.tensor_copy(dst[:, :, 0:LCF], full)
                then(ve.tensor_copy(dst[:, :, LCF:LC], tail))
            then(ve.memset(offs[:, :, 0:1], -1.0))
            for k in range(1, LC):
                then(ve.tensor_tensor(offs[:, :, k:k + 1], offs[:, :, k - 1:k], totals[:, :, k - 1:k], ALU.add))
            flat_ends = ends.rearrange("p b c -> p (b c)")
            then(ve.tensor_tensor(flat_ends, flat_ends, offs.rearrange("p b c -> p (b c)"), ALU.add))
            then(ve.tensor_scalar(wrapped, flat_ends, 0.0, float(S), ALU.is_lt, ALU.mult))
            then(ve.tensor_tensor(flat_ends, flat_ends, wrapped, ALU.add))
            then(ve.tensor_tensor(reached, flat_ends.unsqueeze(2).to_broadcast([P, NCOL, TB + 1]),
                                  thr.unsqueeze(1).to_broadcast([P, NCOL, TB + 1]), ALU.is_ge))
            then(ve.tensor_tensor(hi_hot, reached[:, :, 0:TB], reached[:, :, 1:TB + 1], ALU.subtract))
            then(ve.tensor_reduce(hi_no.unsqueeze(2), reached[:, :, 1:TB + 1], AX.X, ALU.add))
            then(ve.scalar_tensor_tensor(lo_no, hi_no, float(-P), flat_ends, ALU.mult, ALU.add))
            for b in range(B):
                if b >= 2:
                    dve.wait_ge(s["hot_used"], b - 1)
                ve.tensor_tensor(lo_hot[b % 2], lo_no[:, b * LC:(b + 1) * LC].unsqueeze(2).to_broadcast([P, LC, P]),
                                 col_no.unsqueeze(1).to_broadcast([P, LC, P]), ALU.is_equal).then_inc(s["hot_ready"], 1)
            dve.wait_ge(s["hot_used"], B)
            ve.tensor_scalar(bound[:, 0:NT], bank[3][:, 0:NT], 1.0, None, ALU.min).then_inc(s["counts_ready"], 1)
            dve.wait_ge(s["totals_ready"], 1)
            then(ve.tensor_copy(tile_tot, bank[4][:, 0:NT].rearrange("p (b t) -> p b t", b=B)))
            then(ve.memset(before[:, :, 0:1], 0.0))
            for t in range(1, TB):
                then(ve.tensor_tensor(before[:, :, t:t + 1], before[:, :, t - 1:t], tile_tot[:, :, t - 1:t], ALU.add))
            flat_before = before.rearrange("p b t -> p (b t)")
            then(ve.tensor_tensor(row_first, before, row_start, ALU.add))
            ve.tensor_copy(first_row[:, :], row_first[0:1].rearrange("p b t -> p (b t)")).then_inc(s["tables_ready"], 1)
            then(ve.tensor_scalar(started[:, 0:NT], flat_before, 1.0, None, ALU.min))
            then(ve.tensor_scalar(unstarted[:, 0:NT], started[:, 0:NT], -1.0, 1.0, ALU.mult, ALU.add))
            dve.wait_ge(s["consts_selected"], SELECTED)
            ve.memset(onehot[:, :], 0.0).then_inc(s["tables_ready"], 1)
            dve.wait_ge(s["small_in"], 16 * SMALL)
            ve.tensor_scalar(g_init_s[:, :], g_init_s[:, :], B_COEF, None, ALU.mult)
            dve.wait_ge(s["w_in_turned"], 1)
            for k in range(KC):
                last = ve.tensor_scalar(w_in_s[:, k, :], bank[4 + k][:, :], g_res_s[:, k:k + 1], None, ALU.mult)
            last.then_inc(s["g_scaled"], 1)

            def step(i, u):
                a, b, c = i, i - 1, i - 2
                pa, pb, pc = u, 1 - u, u
                if live(a):
                    moved(dve, x_in, a, pa)
                    ve.bn_stats(stat[:, :], xs[:, pa, :]).then_inc(s["x_stats"], 1)
                    at(dve, s["cum_made"], a - 1)
                    ve.tensor_scalar(tri_bound[:, :], triu_b[:, :], bound[:, bass.ds(a, 1)], None,
                                     ALU.mult).then_inc(s["tri_made"], 1)
                    at(dve, s["ctx_sq"], a)
                    at(dve, s["a_rs"], a - 1)
                    at(dve, s["x_stats"], a)
                    ve.tensor_scalar(var_a[:, 1:2], ctx_ss[:, :], 1.0 / DG, RMS_EPS, ALU.mult,
                                     ALU.add).then_inc(s["ctx_var"], 1)
                    ve.bn_aggr(mv[:, :], stat[:, :]).then_inc(s["x_mean"], 1)
                    at(dve, s["x_mean"], a)
                    ve.tensor_scalar(var_a[:, 0:1], mv[:, 1:2], 1.0 + RMS_EPS, RMS_EPS * LN_EPS, ALU.mult,
                                     ALU.add).then_inc(s["x_var"], 1)
                if live(b):
                    at(dve, s["low_made"], b)
                    at(dve, s["q2_made"], b - 1)
                    at(dve, s["k2_made"], b - 1)
                    ve.tensor_copy(low[:, 0:P], bank[2][:, 0:P])
                    ve.tensor_scalar(low[:, P:2 * P], bank[2][:, P:2 * P], bias_rows[:, 0:1], None,
                                     ALU.add).then_inc(s["low_copied"], 1)
                if live(a):
                    at(dve, s["a_rs"], a)
                    at(dve, s["xhat_turned"], a - 1)
                    ve.tensor_scalar(xhat[:, :], xs[:, pa, :], mv[:, 0:1], rs_a[:, 0:1], ALU.subtract,
                                     ALU.mult).then_inc(s["xhat_made"], 1)
                if live(b):
                    logits = bank[7][:, 0:NE]
                    at(dve, s["logits_made"], b)
                    ve.tensor_reduce(l_max[:, :], logits, AX.X, ALU.max).then_inc(s["l_max_made"], 1)
                    at(dve, s["l_max_made"], b)
                    at(dve, s["l_exp_made"], b - 1)
                    ve.tensor_scalar(l_sub[:, :], logits, l_max[:, 0:1], None, ALU.subtract).then_inc(s["l_sub_made"], 1)
                    ve.scalar_tensor_tensor(l_rank[:, :], logits, l_max[:, 0:1], rank[:, :], ALU.is_equal,
                                            ALU.mult).then_inc(s["l_read"], 1)
                if live(b):
                    at(dve, s["l_read"], b)
                    ve.tensor_reduce(l_best[:, :], l_rank[:, :], AX.X, ALU.max).then_inc(s["l_best_made"], 1)
                tri = triu[:, :].unsqueeze(1).to_broadcast([P, PAIRS, P])
                if live(c):
                    at(dve, s["o_made"], c - 1)
                    at(dve, s["a1_made"], c)
                    for j, masked in ((0, s["a1e_masked"]), (1, s["a1o_masked"])):
                        ve.tensor_tensor(att1[:, j, :, :], bank[3 + j][:, :].rearrange("p (a t) -> p a t", a=PAIRS),
                                         tri, ALU.mult).then_inc(masked, 1)
                if live(b):
                    at(dve, s["l_best_made"], b)
                    at(dve, s["v_copied"], b - 1)
                    at(dve, s["hot_turned"], b - 1)
                    ve.tensor_scalar(onehot_late[:, pb, :], l_rank[:, :], l_best[:, 0:1], None, ALU.is_equal)
                    ve.tensor_scalar(onehot[:, :], l_rank[:, :], l_best[:, 0:1], None, ALU.is_equal).then_inc(s["onehot_made"], 1)
                if live(a):
                    at(dve, s["cum_made"], a)
                    at(dve, s["carry_made"], a - 1)
                    at(dve, s["past_made"], a - 1)
                    ve.tensor_scalar(dist[:, :], bank[1][:, 0:P], unstarted[:, bass.ds(a, 1)], row_no[:, 0:1], ALU.max,
                                     ALU.subtract).then_inc(s["dist_made"], 1)
                if live(c):
                    same = mask2[:, pc, :].unsqueeze(1).to_broadcast([P, PAIRS, P])
                    at(dve, s["a2_made"], c)
                    for j, masked in ((0, s["a2e_masked"]), (1, s["a2o_masked"])):
                        ve.tensor_tensor(att2[:, j, :, :], bank[5 + j][:, :].rearrange("p (a t) -> p a t", a=PAIRS),
                                         same, ALU.mult).then_inc(masked, 1)
                if live(a):
                    at(dve, s["dist_made"], a)
                    at(dve, s["decay_made"], a - 1)
                    ve.tensor_scalar(dist_p[:, :], dist[:, :], 0.0, None, ALU.max).then_inc(s["dist_pos"], 1)
                    at(dve, s["dep_w_made"], a - 1)
                    at(dve, s["a_rs"], a)
                    ve.tensor_scalar(in_past[:, :], dist[:, :], 0.0, rs_a[:, 1:2], ALU.is_ge,
                                     ALU.mult).then_inc(s["past_made"], 1)
                if live(b):
                    at(dve, s["l_exp_made"], b)
                    at(dve, s["kt2_made"], b - 1)
                    ve.reciprocal(fac[:, :], l_sum[:, :]).then_inc(s["fac_made"], 1)
                    at(dve, s["hot_turned"], b)
                    at(dve, s["same_made"], b - 1)
                    ve.tensor_copy(onehot_t[:, :], bank[1][0:NE, P:2 * P]).then_inc(s["hot_t_made"], 1)
                    at(dve, s["fac_made"], b)
                    at(dve, s["q2_copied"], b - 1)
                    ve.tensor_scalar(fac_q[:, :], fac[:, :], SCALE, None, ALU.mult).then_inc(s["facq_made"], 1)
                    for j in (0, 2):
                        at(dve, z_made[j], b)
                        at(dve, (s["dec_made"], s["dec_made"], s["sig_made"])[j], b - 1)
                        ve.tensor_scalar(gate_l[:, j, :], bank[j][:, :], -1.0, 40.0, ALU.mult, ALU.min).then_inc(z_min[j], 1)
                if live(b):
                    at(dve, s["same_made"], b)
                    at(dve, s["a2o_masked"], b - 2)
                    at(dve, s["gt2_made"], b - 1)
                    ve.tensor_tensor(mask2[:, pb, :], bank[1][:, 2 * P:3 * P], triu[:, :], ALU.mult)
                    ve.tensor_tensor(cum_mat2[:, :], bank[1][:, 2 * P:3 * P], cum_mat[:, :], ALU.mult).then_inc(s["same_used"], 1)
                    at(dve, s["dec_made"], b - 1)
                    at(dve, s["onehot_made"], b)
                    ve.tensor_tensor(z2_half[:, :, :], onehot[:, :].unsqueeze(1).to_broadcast([P, 2, NE]),
                                     half_z[:, :].unsqueeze(2).to_broadcast([P, 2, NE]), ALU.mult)
                if live(a):
                    at(dve, s["past_made"], a)
                    at(dve, s["decay_made"], a)
                    at(dve, s["dep_made"], a - 1)
                    ve.tensor_tensor(w_depool[:, :], decay_w[:, :], in_past[:, :], ALU.mult)
                    at(dve, s["carry_made"], a)
                    ve.tensor_scalar(w_carry[96:P, :], carry_y[96:P, :], started[96:P, bass.ds(a, 1)], last_row[96:P, 0:1],
                                     ALU.mult, ALU.mult).then_inc(s["dep_w_made"], 1)
                if live(b):
                    at(dve, s["k2_made"], b)
                    at(dve, s["k2d_made"], b - 1)
                    at(dve, s["k2_summed"], b - 1)
                    ve.tensor_reduce(k2_max[:, :], heads(bank[5][:, :]), AX.X, ALU.max).then_inc(s["k2_maxed"], 1)
                    at(dve, z_made[1], b)
                    at(dve, s["dec_made"], b - 1)
                    ve.tensor_scalar(gate_l[:, 1, :], bank[1][:, :], -1.0, 40.0, ALU.mult, ALU.min).then_inc(z_min[1], 1)
                    at(dve, s["k2_maxed"], b)
                    ve.tensor_tensor(heads(k2_exp[:, :]), heads(bank[5][:, :]), over_heads(k2_max[:, :]),
                                     ALU.subtract).then_inc(s["k2_subbed"], 1)
                    for j in (0, 2, 1):
                        at(dve, z_ln[j], b)
                        ve.scalar_tensor_tensor(gate_l[:, j, :], bank[j][:, :], -1.0, gate_l[:, j, :], ALU.mult,
                                                ALU.max).then_inc(l_made[j], 1)
                for half, banks, made in ((0, (7, 3), s["o_half_made"]), (1, (4, 5), s["o_made"])):
                    if live(c):
                        at(dve, s["o_n_made"], c - 1)
                        at(dve, made, c)
                        for e in range(NE):
                            if e > 0:
                                summed(dve, c, NE * half + e)
                            for j, bk in enumerate(banks):
                                part = o[:, :].rearrange("p (a j d) -> p a j d", a=PAIRS, j=2)[
                                    :, 2 * half:2 * half + 2, j, :]
                                one = bank[bk][:, :].rearrange("p (a e d) -> p a e d", a=2, e=NE)[:, :, e, :]
                                if e == 0:
                                    last = ve.tensor_scalar(part, one, onehot_late[:, pc, e:e + 1], None, ALU.mult)
                                else:
                                    last = ve.scalar_tensor_tensor(part, one, onehot_late[:, pc, e:e + 1], part,
                                                                   ALU.mult, ALU.add)
                            last.then_inc(s["o_sum"], 1)
                    if half == 0 and live(b):
                        at(dve, s["silu_made"], b - 1)
                        ve.tensor_tensor(heads(g_norm[:, :]), heads(bank[2][:, :]),
                                         norm_s[:, :].unsqueeze(1).to_broadcast([P, H, DK]), ALU.mult).then_inc(s["g_normed"], 1)
                if live(c):
                    at(dve, s["o_base_made"], c)
                    summed(dve, c, 2 * NE)
                    ve.tensor_tensor(o[:, :], o[:, :], bank[6][:, :], ALU.add).then_inc(s["o_sum"], 1)
                if live(b):
                    at(dve, s["k2_exped"], b)
                    ve.tensor_reduce(k2_sum[:, :], heads(k2_exp[:, :]), AX.X, ALU.add).then_inc(s["k2_summed"], 1)
                    at(dve, s["k2_summed"], b)
                    ve.reciprocal(k2_rec[:, :], k2_sum[:, :]).then_inc(s["k2_reced"], 1)
                    at(dve, s["k2_reced"], b)
                    at(dve, s["kt2_made"], b - 1)
                    ve.tensor_scalar(k2_fac[:, :], k2_rec[:, :], fac[:, 0:1], None, ALU.mult).then_inc(s["k2_faced"], 1)
                    at(dve, s["gt1_exped"], b)
                    at(dve, s["q1_copied"], b)
                    ve.tensor_tensor(e1p[:, :], q1[:, :], e1p[:, :], ALU.mult).then_inc(s["qt1_made"], 1)
                    at(dve, s["gt2_exped"], b)
                    at(dve, s["q2_copied"], b)
                    at(dve, s["q2_turned"], b - 1)
                    ve.tensor_tensor(e2p[:, :], q2[:, :], e2p[:, :], ALU.mult).then_inc(s["qt2_made"], 1)
                if live(c):
                    at(dve, s["o_sq_made"], c)
                    at(dve, s["o_var_made"], c - 1)
                    ve.tensor_reduce(o_ss[:, :], heads(o_sq[:, :]), AX.X, ALU.add).then_inc(s["o_summed"], 1)
                    at(dve, s["o_summed"], c)
                    at(dve, s["o_rs_made"], c - 1)
                    ve.tensor_scalar(o_var[:, :], o_ss[:, :], 1.0 / DK, LN_EPS, ALU.mult, ALU.add).then_inc(s["o_var_made"], 1)
                    at(dve, s["kv0_made"], c)
                    kept = state[:, 0:2, 1:SLOTS, :]
                    ve.tensor_tensor(kept, kept, bank[4][:, :].rearrange("p (a e d) -> p a e d", a=2, e=NE),
                                     ALU.add).then_inc(s["kv0_added"], 1)
                    at(dve, s["kv1_made"], c)
                    kept = state[:, 2:4, 1:SLOTS, :]
                    ve.tensor_tensor(kept, kept, bank[5][:, :].rearrange("p (a e d) -> p a e d", a=2, e=NE),
                                     ALU.add).then_inc(s["kv1_added"], 1)
                    at(dve, s["o_gated_made"], c)
                    at(dve, s["o_rs_made"], c)
                    at(dve, s["o_turned"], c - 1)
                    ve.tensor_tensor(heads(o_n[:, :]), heads(o[:, :]), over_heads(o_rs[:, :]),
                                     ALU.mult).then_inc(s["o_n_made"], 1)
                    at(dve, s["kvd_made"], c)
                    kept = state[:, :, 0, :]
                    ve.tensor_tensor(kept, kept, bank[6][:, 0:PAIRS * DK].rearrange("p (a d) -> p a d", a=PAIRS),
                                     ALU.add).then_inc(s["state_added"], 1)
                if live(b):
                    at(dve, s["dec_exped"], b)
                    at(dve, s["state_first"], b - 2)
                    ve.tensor_scalar(dec_first[:, pb, :, :], dec[:, pb, 0, :, :], keep[:, bass.ds(b, 1)], None,
                                     ALU.mult).then_inc(s["dec_kept"], 1)
                    at(dve, s["k2d_made"], b)
                    at(dve, s["k2_faced"], b)
                    at(dve, s["kv1_made"], b - 2)
                    ve.tensor_tensor(heads(kt2[:, pb, :]), heads(e2m[:, :]), over_heads(k2_fac[:, :]),
                                     ALU.mult).then_inc(s["kt2_made"], 1)
                if live(a):
                    at(dve, s["w_made"], a)
                    at(dve, s["resid_made"], a)
                    at(dve, s["x1_moved"], a - 2)
                    ve.tensor_tensor(x1[:, pa, :], bank[7][:, :], resid[:, :], ALU.add).then_inc(s["x1_made"], 1)
                    at(dve, s["x1_made"], a)
                    ve.bn_stats(stat2[:, :], x1[:, pa, :]).then_inc(s["x1_stats"], 1)
                    at(dve, s["x1_stats"], a)
                    at(dve, s["xn_made"], a - 1)
                    ve.memset(idle[:, :], 0.0)
                    ve.bn_aggr(mv2[:, :], stat2[:, :]).then_inc(s["x1_mean"], 1)
                    at(dve, s["x1_mean"], a)
                    at(dve, s["x1_rs"], a - 1)
                    ve.tensor_scalar(var2[:, :], mv2[:, 1:2], LN_EPS, None, ALU.add).then_inc(s["x1_var"], 1)
                    at(dve, s["x1_rs"], a)
                    at(dve, s["xn_turned"], a - 1)
                    ve.tensor_scalar(xn[:, :], x1[:, pa, :], mv2[:, 0:1], rs2[:, 0:1], ALU.subtract,
                                     ALU.mult).then_inc(s["xn_made"], 1)
                if live(c):
                    at(dve, s["y_made"], c)
                    at(dve, s["x1_moved"], c)
                    moved(dve, res_out, c - 2, pc)
                    ve.tensor_tensor(res[:, pc, :], bank[2][:, :], x1_late[:, pc, :], ALU.add).then_inc(s["res_made"], 1)

            run(dve, step)


_INS = ['x', 'ctx_2048', 'mask_BxS2_if0', 'L0_xattn_W_in', 'L0_xattn_b_in', 'L0_xattn_g_res', 'L0_xattn_g_init',
        'L0_ffn_Wq', 'L0_ffn_Wk', 'L0_ffn_Wv', 'L0_ffn_Wqa', 'L0_ffn_Wqb', 'L0_ffn_Wka', 'L0_ffn_Wkb',
        'L0_ffn_Wg1a', 'L0_ffn_Wg1b', 'L0_ffn_bg1', 'L0_ffn_Wg2a', 'L0_ffn_Wg2b', 'L0_ffn_bg2', 'L0_ffn_We',
        'L0_ffn_Wga', 'L0_ffn_Wgb', 'L0_ffn_norm_w', 'L0_ffn_Wo']


def kernel(**inputs):
    import numpy as np
    import concourse.bacc as bacc
    from concourse.bass_utils import run_bass_kernel_spmd

    nc = bacc.Bacc("TRN2", target_bir_lowering=False, num_devices=1)
    arrays, args = {}, []
    for name in _INS:
        a = np.ascontiguousarray(inputs[name])
        arrays[f"in_{name}"] = a
        args.append(nc.dram_tensor(f"in_{name}", a.shape, mybir.dt.from_np(a.dtype), kind="ExternalInput").ap())
    out = nc.dram_tensor("out", inputs["x"].shape, F32, kind="ExternalOutput").ap()
    xattn_ffn(nc, *args, out)
    r = run_bass_kernel_spmd(nc, [arrays], core_ids=[0])
    return r.results[0]["out"]
```

```python
import math
from contextlib import ExitStack

import concourse.bass as bass
from concourse import mybir

ALU = mybir.AluOpType
ACT = mybir.ActivationFunctionType
AX = mybir.AxisListType
F32 = mybir.dt.float32
BF16 = mybir.dt.bfloat16
I32 = mybir.dt.int32
F32R = mybir.dt.float32r

LOOP_FROM, UNROLL = 4, 2
P = 128
D = 512
KC = D // P
H, DK = 8, 64
PAIRS = H // 2
NE = 4
SLOTS = 1 + NE
LORA, GLR = 64, 16
LN_EPS = 1e-5
RMS_EPS = 1e-5
NORMALIZER = 16.0
SCALE = DK ** -0.5
LOGP = -0.001
B_COEF = math.exp(LOGP)
WEIGHTS = 2 + 3 * KC
SELECTED = 12
SMALL = 5 + 5 + 5 + 2
LN_A = math.log(-math.expm1(LOGP))


def xattn_ffn(nc, x, ctx_in, lens, w_in, b_in, g_res, g_init, wq, wk, wv, wqa, wqb, wka, wkb,
              wg1a, wg1b, bg1, wg2a, wg2b, bg2, we, wga, wgb, norm_w, wo, out):
    B, S, _ = x.shape
    PLEN, DG = ctx_in.shape[1], ctx_in.shape[2]
    TB = S // P
    NT = B * TB
    LC = -(-PLEN // P)
    LCF = PLEN // P
    TAIL = PLEN - LCF * P
    NCOL = B * LC
    x_rows = x.rearrange("b s d -> (b s) d")
    out_rows = out.rearrange("b s d -> (b s) d")
    ctx_rows = ctx_in.rearrange("b p d -> (b p) d")

    stack = ExitStack()
    with stack:
        def sb(name, shape, dt=F32):
            return stack.enter_context(nc.sbuf_tensor(name, shape, dt))

        def sem(name):
            return stack.enter_context(nc.semaphore(name))

        bank = [stack.enter_context(nc.psum_tensor(f"bank{i}", [P, D], F32)) for i in range(8)]

        ident = sb("ident", [P, P])
        triu = sb("triu", [P, P])
        triu_b = sb("triu_b", [P, P], BF16)
        ones = sb("ones", [P, P])
        ones_b = sb("ones_b", [P, P], BF16)
        cum_mat = sb("cum_mat", [P, P])
        half_z = sb("half_z", [P, 2])
        rank = sb("rank", [P, NE])
        minus_half = sb("minus_half", [P, H])
        row_no = sb("row_no", [P, 1])
        carry_bias = sb("carry_bias", [P, 1])
        last_row = sb("last_row", [P, 1])
        bias_rows = sb("bias_rows", [P, 1])
        keep = sb("keep", [P, NT + UNROLL])
        wq_hi, wk_hi, wv_hi, w_in_hi = (sb(n, [P, KC, D], F32R) for n in ("wq_hi", "wk_hi", "wv_hi", "w_in_hi"))
        wq_lo, wk_lo, wv_lo, w_in_lo = (sb(n, [P, KC, D], F32R) for n in ("wq_lo", "wk_lo", "wv_lo", "w_in_lo"))
        wo_s = sb("wo_s", [P, KC, D])
        low_hi, low_lo = (sb(n, [P, KC, 2 * P + NE], F32R) for n in ("low_hi", "low_lo"))
        we_s = sb("we_s", [P, KC, NE])
        w_up = sb("w_up", [P, 2, D])
        g_res_s = sb("g_res_s", [P, KC])
        b_in_s = sb("b_in_s", [P, D])
        g_init_s = sb("g_init_s", [P, D])
        norm_s = sb("norm_s", [P, DK])
        bound = sb("bound", [P, NT + UNROLL])
        started = sb("started", [P, NT + UNROLL])
        unstarted = sb("unstarted", [P, NT + UNROLL])
        first_row = sb("first_row", [1, NT], I32)

        lens_rows = sb("lens_rows", [P, P], I32)

        xs = sb("xs", [P, 2, D])
        ctx = sb("ctx", [P, 2, DG])
        stat = sb("stat", [P, 6])
        stat2 = sb("stat2", [P, 6])
        mv = sb("mv", [P, 2])
        mv2 = sb("mv2", [P, 2])
        var_a = sb("var_a", [P, 2])
        rs_a = sb("rs_a", [P, 2])
        ctx_ss = sb("ctx_ss", [P, 1])
        var2 = sb("var2", [P, 1])
        idle = sb("idle", [P, 1])
        rs2 = sb("rs2", [P, 1])
        xhat = sb("xhat", [P, D])
        xhat_hi = sb("xhat_hi", [P, KC, P], F32R)
        xhat_lo = sb("xhat_lo", [P, KC, P], F32R)
        tri_bound = sb("tri_bound", [P, P], BF16)
        dist = sb("dist", [P, P])
        dist_p = sb("dist_p", [P, P])
        decay_w = sb("decay_w", [P, P])
        carry_y = sb("carry_y", [P, P])
        in_past = sb("in_past", [P, P])
        w_depool = sb("w_depool", [P, P])
        w_carry = sb("w_carry", [P, P])
        depool = sb("depool", [P, 2, D])
        resid = sb("resid", [P, D])
        x1 = sb("x1", [P, D])
        xn = xhat
        xn_hi = sb("xn_hi", [P, KC, P], F32R)
        xn_lo = sb("xn_lo", [P, KC, P], F32R)
        x1_late = sb("x1_late", [P, 2, D])
        low_tok = sb("low_tok", [P, 2 * P])
        low = sb("low", [P, 2 * P])
        l_max = sb("l_max", [P, 1])
        l_sub = sb("l_sub", [P, NE])
        l_exp = sb("l_exp", [P, NE])
        l_sum = sb("l_sum", [P, 1])
        l_rank = sb("l_rank", [P, NE])
        l_best = sb("l_best", [P, 1])
        onehot = sb("onehot", [P, NE])
        onehot_late = sb("onehot_late", [P, 2, NE])
        fac = sb("fac", [P, 1])
        fac_q = sb("fac_q", [P, 1])
        onehot_t = sb("onehot_t", [NE, P], BF16)
        mask2 = sb("mask2", [P, 2, P])
        cum_mat2 = sb("cum_mat2", [P, P])
        z2_half = sb("z2_half", [P, 2, NE])
        q1 = sb("q1", [P, D])
        k1 = sb("k1", [P, D])
        q2 = sb("q2", [P, D])
        v = sb("v", [P, 2, D])
        v_e = sb("v_e", [P, NE, D])
        gate_l = sb("gate_l", [P, 3, D])
        g_norm = sb("g_norm", [P, D])
        sig = gate_l[:, 2, :]
        g_silu = sb("g_silu", [P, D])
        k2_max = sb("k2_max", [P, H])
        k2_exp = sb("k2_exp", [P, D])
        k2_sum = sb("k2_sum", [P, H])
        k2_rec = sb("k2_rec", [P, H])
        k2_fac = sb("k2_fac", [P, H])
        e1p = sb("e1p", [P, D])
        e1m = sb("e1m", [P, D])
        e2p = sb("e2p", [P, D])
        e2m = sb("e2m", [P, D])
        dec = sb("dec", [P, 2, 2, PAIRS, SLOTS])
        dec_first = sb("dec_first", [P, 2, PAIRS, SLOTS])
        kt1 = sb("kt1", [P, 2, D])
        kt2 = sb("kt2", [P, D])
        q1_t = sb("q1_t", [P, PAIRS, P])
        k1_t = sb("k1_t", [P, PAIRS, P])
        q2_t = sb("q2_t", [P, PAIRS, P])
        k2_t = sb("k2_t", [P, PAIRS, P])
        att1 = sb("att1", [P, 2, PAIRS, P])
        att2 = sb("att2", [P, 2, PAIRS, P])
        state = sb("state", [P, PAIRS, SLOTS, DK])
        o = sb("o", [P, D])
        o_ss = sb("o_ss", [P, H])
        o_var = sb("o_var", [P, H])
        o_rs = sb("o_rs", [P, H])
        o_n = sb("o_n", [P, D])
        o_sq = o_n
        o_t = sb("o_t", [P, KC, P])
        ctx_bin = o_n[:, :].bitcast(BF16)
        scratch = [v[:, n, :].rearrange("p (c n) -> p c n", n=P) for n in range(2)] + [att2[:, n, :, :] for n in range(2)]
        lens_i = lens_rows[0:NCOL, :]
        lens_f = scratch[0][0:NCOL, 1, :]
        lens_t = scratch[0][:, 2, 0:NCOL]
        totals = scratch[0][:, 3, 0:NCOL].rearrange("p (b c) -> p b c", b=B)
        offs = scratch[1][:, 0, 0:NCOL].rearrange("p (b c) -> p b c", b=B)
        ends = scratch[1][:, 1, 0:NCOL].rearrange("p (b c) -> p b c", b=B)
        wrapped = scratch[1][:, 2, 0:NCOL]
        hi_no = scratch[1][:, 3, 0:NCOL]
        w_stage = [[g_norm, q2, q1, k1], [xhat, e1p, e1m, e2p], [o, resid, q1_t[:, :, :].rearrange("p a t -> p (a t)"), k2_exp]]
        w_low = kt1[:, :, :].rearrange("p a n -> p (a n)").rearrange("p (c n) -> p c n", c=KC)
        w_in_rows = ctx[:, :, :].rearrange("p a n -> p (a n)").rearrange("p (c n) -> p c n", c=KC)
        lo_no = scratch[2][:, 0, 0:NCOL]
        thr = scratch[2][:, 1, 0:TB + 1]
        col_no = scratch[2][:, 2, :]
        row_start = scratch[2][:, 3, 0:NT].rearrange("p (b t) -> p b t", b=B)
        before = scratch[3][:, 0, 0:NT].rearrange("p (b t) -> p b t", b=B)
        tile_tot = scratch[3][:, 1, 0:NT].rearrange("p (b t) -> p b t", b=B)
        row_first = scratch[3][:, 2, 0:NT].rearrange("p (b t) -> p b t", b=B)
        reached = v_e[:, 0:2, :].bitcast(BF16).rearrange("p a n -> p (a n)")[:, 0:NCOL * (TB + 1)]\
            .rearrange("p (c j) -> p c j", j=TB + 1)
        hi_hot = v_e[:, 2:4, :].bitcast(BF16).rearrange("p a n -> p (a n)")[:, 0:NCOL * TB]\
            .rearrange("p (c j) -> p c j", j=TB)
        lo_hot = [att1[:, :, :, :].bitcast(BF16).rearrange("p j a n -> p (j a n)")[:, 0:LC * P],
                  gate_l[:, :, :].bitcast(BF16).rearrange("p a n -> p (a n)")[:, 0:LC * P]]
        lo_hot = [h.rearrange("p (c n) -> p c n", n=P) for h in lo_hot]

        s = {n: sem(n) for n in """
            consts_made consts_selected weights_in weights_rounded lens_in small_in lens_float lens_turned lens_summed
            prologue_step g_scaled counts_ready w_in_turned hot_ready hot_used totals_ready tables_ready
            x_stats x_mean x_var a_rs xhat_made xhat_turned xhat_t_made xhat_lo_made
            ctx_sq ctx_var tri_made cum_made dist_made dist_pos decay_made carry_made past_made dep_w_made
            dep_made dep_copied xb_made dep_scaled resid_made w_made x1_made x1_stats x1_mean x1_var x1_rs
            xn_made xn_turned xn_hi_made xn_lo_made x1_moved
            low_made low_out low_turned low_copied l_max_made l_read l_sub_made l_best_made onehot_made l_exp_made fac_made facq_made
            q1_made k1_made v_made q1_copied k1_copied v_copied
            q2_made k2_made q2_copied k2_maxed k2_subbed k2_exped k2_summed k2_reced k2_faced
            g_normed sig_made silu_made
            hot_turned hot_t_made same_made same_used z2_made
            gt1_made gt2_made dec_made gt1_exped gt2_exped dec_exped dec_kept
            qt1_made qt2_made k2d_made kt1_made kt2_made
            q1_turned k1_turned q2_turned k2_turned q1_t_made k1_t_made q2_t_made k2_t_made 
            a1_made a2_made a1e_masked a1o_masked a2e_masked a2o_masked att_summed state_first o_even_made o_base_made o_half_made o_made o_sum o_sq_made kv0_made kv1_made kvd_made kv0_added kv1_added
            state_added state_made o_summed o_var_made o_rs_made o_gated_made o_n_made
            o_turned o_t_made y_made res_made
            """.split()}

        z_made = [sem(f"z_made{j}") for j in range(3)]
        z_min = [sem(f"z_min{j}") for j in range(3)]
        z_exp = [sem(f"z_exp{j}") for j in range(3)]
        z_ln = [sem(f"z_ln{j}") for j in range(3)]
        l_made = [sem(f"l_made{j}") for j in range(3)]

        x_in = [sem(f"x_in{j}") for j in range(2)]
        ctx_loaded = [sem(f"ctx_loaded{j}") for j in range(2)]
        res_out = [sem(f"res_out{j}") for j in range(2)]

        def moved(eng, semaphores, tile, par):
            if not isinstance(tile, int) or tile >= 0:
                eng.wait_ge(semaphores[par], (tile - par) * 8 + 16)

        def at(eng, semaphore, tile):
            if isinstance(tile, int):
                if tile < 0:
                    return
                tile = min(tile, NT - 1)
            eng.wait_ge(semaphore, tile + 1)

        def summed(eng, tile, parts=2 * NE + 1):
            eng.wait_ge(s["o_sum"], (2 * NE + 1) * tile + parts)

        def heads(a):
            return a.rearrange("p (h d) -> p h d", h=H)

        def over_heads(col):
            return col.unsqueeze(2).to_broadcast([P, H, DK])


        def run(eng, step):
            for i in range(LOOP_FROM):
                step(i, i % UNROLL)
            with eng.Fori(LOOP_FROM, NT, UNROLL) as i:
                for u in range(UNROLL):
                    step(i + u, u)
            for i in range(NT, NT + 2):
                step(i, i % UNROLL)

        def live(tile):
            return not isinstance(tile, int) or 0 <= tile < NT

        block = stack.enter_context(nc.Block())

        @block.sync
        def _(sp):
            sp.wait_ge(s["consts_made"], 1)
            for b in range(B):
                sp.dma_start(lens_i[b * LCF:(b + 1) * LCF, :],
                             lens[b, 0:LCF * P].rearrange("(c k) -> c k", k=P)).then_inc(s["lens_in"], 16)
            sp.dma_start(lens_i[B * LCF:NCOL, 0:TAIL], lens[:, LCF * P:PLEN]).then_inc(s["lens_in"], 16)
            for dst, src in ((w_in_rows, w_in), (wo_s, wo)):
                sp.dma_start(dst[:, :, :], src.rearrange("(c p) n -> p c n", p=P)).then_inc(s["weights_in"], 16)
            for stage, src in zip(w_stage, (wq, wk, wv)):
                for k in range(KC):
                    sp.dma_start(stage[k][:, :], src[k * P:(k + 1) * P, :]).then_inc(s["weights_in"], 16)

            def load_x(t, par):
                at(sp, s["resid_made"], t - 2)
                sp.dma_start(xs[:, par, :], x_rows[bass.ds(t * P, P), :]).then_inc(x_in[par], 16)

            def load_ctx(t, par):
                at(sp, s["dep_made"], t - 2)
                at(sp, s["ctx_sq"], t - 2)
                row = sp.value_load(first_row[0:1, bass.ds(t, 1)], min_val=0, max_val=B * PLEN - P)
                sp.dma_start(ctx[:, par, :], ctx_rows[bass.ds(row, P), :]).then_inc(ctx_loaded[par], 16)

            load_x(0, 0)
            sp.wait_ge(s["tables_ready"], 1)
            sp.wait_ge(s["w_in_turned"], 1)

            load_ctx(0, 0)

            def step(i, u):
                if not isinstance(i, int) or i + 1 < NT:
                    load_ctx(i + 1, 1 - u)
                    load_x(i + 1, 1 - u)
                if live(i - 2):
                    at(sp, s["res_made"], i - 2)
                    sp.dma_start(out_rows[bass.ds((i - 2) * P, P), :], x1_late[:, u, :]).then_inc(res_out[u], 16)

            for i in range(LOOP_FROM):
                step(i, i % 2)
            with sp.Fori(LOOP_FROM, NT - 2, 2) as i:
                for u in range(2):
                    step(i + u, u)
            for i in range(NT - 2, NT + 2):
                step(i, i % 2)
            for par in range(2):
                moved(sp, res_out, NT - 2 + par, par)

        @block.gpsimd
        def _(pool):
            g = nc.gpsimd
            g.memset(lens_rows[:, :], 0)
            g.memset(ones[:, :], 1.0)
            g.memset(ones_b[:, :], 1.0)
            g.memset(ident[:, :], 0.0)
            g.memset(cum_mat[:, :], 0.0)
            g.memset(half_z[:, :], -1.0 / NORMALIZER)
            g.memset(minus_half[:, :], -0.5)
            g.memset(last_row[:, :], 0.0)
            g.memset(bias_rows[:, :], 0.0)
            g.memset(keep[:, :], 1.0)
            g.memset(w_low[:, :, :], 0.0)
            g.memset(state[:, :, :, :], 0.0)
            g.memset(depool[:, 1, :], 0.0)
            g.iota(row_no[:, :], pattern=[[0, 1]], base=1, channel_multiplier=1,
                   allow_small_or_imprecise_dtypes=True)
            g.iota(rank[:, :], pattern=[[-1, NE]], base=NE, channel_multiplier=0,
                   allow_small_or_imprecise_dtypes=True)
            g.iota(thr, pattern=[[P, TB + 1]], base=0, channel_multiplier=0,
                   allow_small_or_imprecise_dtypes=True)
            g.iota(col_no, pattern=[[1, P]], base=0, channel_multiplier=0,
                   allow_small_or_imprecise_dtypes=True)
            g.iota(row_start, pattern=[[PLEN, B], [0, TB]], base=0, channel_multiplier=0,
                   allow_small_or_imprecise_dtypes=True).then_inc(s["consts_made"], 1)
            pool.wait_ge(s["consts_made"], 1)
            done = 0

            def then(ins):
                nonlocal done
                done += 1
                ins.then_inc(s["consts_selected"], 1)
                pool.wait_ge(s["consts_selected"], done)

            then(g.affine_select(out=ident[:, :], in_=ident[:, :], compare_op=ALU.not_equal, fill=1.0, base=0,
                            pattern=[[-1, P]], channel_multiplier=1))
            then(g.affine_select(out=triu[:, :], in_=ones[:, :], compare_op=ALU.is_ge, fill=0.0, base=0,
                            pattern=[[1, P]], channel_multiplier=-1))
            then(g.affine_select(out=triu_b[:, :], in_=ones_b[:, :], compare_op=ALU.is_ge, fill=0.0, base=0,
                            pattern=[[1, P]], channel_multiplier=-1))
            then(g.affine_select(out=cum_mat[0:64, :], in_=cum_mat[0:64, :], compare_op=ALU.is_ge,
                            fill=1.0 / NORMALIZER, base=0, pattern=[[1, P]], channel_multiplier=-1))
            then(g.affine_select(out=cum_mat[64:P, :], in_=cum_mat[64:P, :], compare_op=ALU.is_gt,
                            fill=-1.0 / NORMALIZER, base=64, pattern=[[-1, P]], channel_multiplier=1))
            then(g.memset(half_z[64:P, 0:1], 0.0))
            then(g.memset(half_z[0:64, 1:2], 0.0))
            then(g.affine_select(out=last_row[:, :], in_=last_row[:, :], compare_op=ALU.not_equal, fill=1.0,
                            base=-(P - 1), pattern=[[0, 1]], channel_multiplier=1))
            then(g.affine_select(out=bias_rows[:, :], in_=bias_rows[:, :], compare_op=ALU.not_equal, fill=1.0,
                            base=-(LORA + GLR), pattern=[[0, 1]], channel_multiplier=1))
            then(g.affine_select(out=bias_rows[:, :], in_=bias_rows[:, :], compare_op=ALU.not_equal, fill=1.0,
                            base=-(96 + GLR), pattern=[[0, 1]], channel_multiplier=1))
            then(g.memset(keep[:, 0:NT].rearrange("p (b t) -> p b t", t=TB)[:, :, 0:1], 0.0))
            then(g.tensor_scalar(carry_bias[:, :], row_no[:, :], LN_A, 0.0, ALU.mult, ALU.add))

            def step(i, u):
                a, b, c = i, i - 1, i - 2
                pa, pb, pc = u, 1 - u, u
                if live(a):
                    at(pool, s["x_var"], a)
                    at(pool, s["ctx_var"], a)
                    at(pool, s["past_made"], a - 1)
                    at(pool, s["xhat_made"], a - 1)
                    g.tensor_tensor(rs_a[:, :], var_a[:, :], minus_half[:, 0:2], ALU.pow).then_inc(s["a_rs"], 1)
                if live(c):
                    at(pool, s["dec_kept"], c)
                    at(pool, s["state_made"], c - 1)
                    g.tensor_tensor(state[:, :, :, :], state[:, :, :, :],
                                    dec_first[:, pc, :, :].unsqueeze(3).to_broadcast([P, PAIRS, SLOTS, DK]),
                                    ALU.mult).then_inc(s["state_first"], 1)
                if live(a):
                    at(pool, s["xhat_made"], a)
                    at(pool, s["x1_made"], b)
                    moved(pool, res_out, b - 2, pb)
                    g.tensor_tensor(xs[:, pa, :], xs[:, pa, :], b_in_s[:, :], ALU.add).then_inc(s["xb_made"], 1)
                if live(c):
                    at(pool, s["sig_made"], c)
                    at(pool, s["g_normed"], c)
                    at(pool, s["o_gated_made"], c - 1)
                    g.tensor_tensor(g_silu[:, :], g_norm[:, :], sig, ALU.mult).then_inc(s["silu_made"], 1)
                if live(c):
                    for j, one, two in ((0, s["a1e_masked"], s["a2e_masked"]), (1, s["a1o_masked"], s["a2o_masked"])):
                        at(pool, one, c)
                        at(pool, two, c)
                        g.tensor_tensor(att1[:, j, :, :], att1[:, j, :, :], att2[:, j, :, :],
                                        ALU.add).then_inc(s["att_summed"], 1)
                if live(b):
                    if not live(a):
                        at(pool, s["x1_made"], b)
                        moved(pool, res_out, b - 2, pb)
                    g.tensor_copy(x1_late[:, pb, :], x1[:, :]).then_inc(s["x1_moved"], 1)
                if live(c):
                    at(pool, s["o_sq_made"], c)
                    at(pool, s["silu_made"], c)
                    g.tensor_tensor(o[:, :], o[:, :], g_silu[:, :], ALU.mult).then_inc(s["o_gated_made"], 1)
                    at(pool, s["o_var_made"], c)
                    g.tensor_tensor(o_rs[:, :], o_var[:, :], minus_half[:, :], ALU.pow).then_inc(s["o_rs_made"], 1)
                if live(b):
                    at(pool, s["gt1_exped"], b)
                    at(pool, s["k1_copied"], b)
                    at(pool, s["kvd_made"], b - 2)
                    at(pool, s["k1_turned"], b - 1)
                    g.tensor_tensor(kt1[:, pb, :], k1[:, :], e1m[:, :], ALU.mult).then_inc(s["kt1_made"], 1)
                    at(pool, s["gt2_exped"], b)
                    at(pool, s["k2_exped"], b)
                    at(pool, s["kt2_made"], b - 1)
                    g.tensor_tensor(e2m[:, :], k2_exp[:, :], e2m[:, :], ALU.mult).then_inc(s["k2d_made"], 1)
                if live(a):
                    at(pool, s["dep_copied"], a)
                    at(pool, s["x1_made"], a - 1)
                    g.tensor_tensor(resid[:, :], depool[:, pa, :], g_init_s[:, :], ALU.mult).then_inc(s["dep_scaled"], 1)
                    at(pool, s["dep_scaled"], a)
                    at(pool, s["xb_made"], a)
                    g.tensor_tensor(resid[:, :], resid[:, :], xs[:, pa, :], ALU.add).then_inc(s["resid_made"], 1)
                    at(pool, s["x1_var"], a)
                    at(pool, s["xn_made"], a - 1)
                    g.tensor_tensor(rs2[:, :], var2[:, :], minus_half[:, 0:1], ALU.pow).then_inc(s["x1_rs"], 1)
                if live(c):
                    at(pool, s["state_added"], c)
                    g.tensor_tensor(state[:, :, :, :], state[:, :, :, :],
                                    dec[:, pc, 1, :, :].unsqueeze(3).to_broadcast([P, PAIRS, SLOTS, DK]),
                                    ALU.mult).then_inc(s["state_made"], 1)

            run(pool, step)

        @block.scalar
        def _(act):
            sc = nc.scalar
            sc.preload_act_table_set("natural_log_exp_and_others")
            sc.dma_start(g_res_s[:, :], g_res.rearrange("(c p) -> p c", p=P),
                         allow_slow_non_contiguous=True).then_inc(s["small_in"], 16)
            sc.dma_start(b_in_s[:, :], b_in.unsqueeze(0).to_broadcast([P, D])).then_inc(s["small_in"], 16)
            sc.dma_start(g_init_s[:, :], g_init[0:D].unsqueeze(0).to_broadcast([P, D])).then_inc(s["small_in"], 16)
            sc.dma_start(norm_s[:, :], norm_w.unsqueeze(0).to_broadcast([P, DK])).then_inc(s["small_in"], 16)
            sc.dma_start(we_s[:, :, :], we.rearrange("(c p) n -> p c n", p=P)).then_inc(s["small_in"], 16)
            act.wait_ge(s["consts_made"], 1)
            for c0, w, src in ((0, LORA, wqa), (LORA, LORA, wka), (P, LORA, wga), (P + 64, GLR, wg1a),
                               (P + 96, GLR, wg2a)):
                sc.dma_start(w_low[:, :, c0:c0 + w], src.rearrange("(c p) n -> p c n", p=P)).then_inc(s["small_in"], 16)
            for r0, h, src in ((0, 0, wqb), (64, 0, wkb), (0, 1, wgb), (64, 1, wg1b), (96, 1, wg2b)):
                sc.dma_start(w_up[r0:r0 + src.shape[0], h, :], src).then_inc(s["small_in"], 16)
            for r0, src in ((64 + GLR, bg1), (96 + GLR, bg2)):
                sc.dma_start(w_up[r0:r0 + 1, 1, :], src.unsqueeze(0)).then_inc(s["small_in"], 16)

            act.wait_ge(s["weights_in"], 16 * WEIGHTS)
            for stage, hi in zip(w_stage, (wq_hi, wk_hi, wv_hi)):
                for k in range(KC):
                    sc.copy(hi[:, k, :], stage[k][:, :]).then_inc(s["weights_rounded"], 1)

            act.wait_ge(s["small_in"], 16 * SMALL)
            sc.copy(low_hi[:, :, 0:2 * P], w_low)
            sc.copy(low_hi[:, :, 2 * P:2 * P + NE], we_s[:, :, :]).then_inc(s["weights_rounded"], 1)

            def step(i, u):
                a, b, c = i, i - 1, i - 2
                pa, pb, pc = u, 1 - u, u
                if live(a):
                    moved(act, ctx_loaded, a, pa)
                    at(act, s["ctx_var"], a - 1)
                    at(act, s["o_turned"], a - 3)
                    sc.activation(ctx_bin, ctx[:, pa, :], ACT.Square, accum_out=ctx_ss[:, :]).then_inc(s["ctx_sq"], 1)
                if live(b):
                    at(act, s["l_sub_made"], b)
                    at(act, s["fac_made"], b - 1)
                    sc.activation(l_exp[:, :], l_sub[:, :], ACT.Exp, accum_out=l_sum[:, :]).then_inc(s["l_exp_made"], 1)
                if live(a):
                    at(act, s["xhat_turned"], a)
                    at(act, s["w_made"], a - 1)
                    sc.copy(xhat_hi[:, :, :], bank[0][:, :].rearrange("p (c t) -> p c t", c=KC)).then_inc(s["xhat_t_made"], 1)
                    at(act, s["dist_pos"], a)
                    at(act, s["dep_w_made"], a - 1)
                    sc.activation(decay_w[:, :], dist_p[:, :], ACT.Exp, scale=LN_A).then_inc(s["decay_made"], 1)
                    sc.activation(carry_y[96:P, :], dist[96:P, :], ACT.Exp, scale=LN_A,
                                  bias=carry_bias[96:P, :]).then_inc(s["carry_made"], 1)
                if live(b):
                    at(act, s["q1_made"], b)
                    at(act, s["qt1_made"], b - 1)
                    sc.mul(q1[:, :], bank[7][:, :], SCALE).then_inc(s["q1_copied"], 1)
                    at(act, z_min[0], b)
                    sc.activation(gate_l[:, 0, :], gate_l[:, 0, :], ACT.Exp).then_inc(z_exp[0], 1)
                    at(act, z_min[2], b)
                    sc.activation(gate_l[:, 2, :], gate_l[:, 2, :], ACT.Exp).then_inc(z_exp[2], 1)
                    at(act, z_exp[0], b)
                    sc.activation(gate_l[:, 0, :], gate_l[:, 0, :], ACT.Ln, bias=1.0).then_inc(z_ln[0], 1)
                    at(act, s["q2_made"], b)
                    at(act, s["facq_made"], b)
                    at(act, s["qt2_made"], b - 1)
                    sc.mul(q2[:, :], bank[4][:, :], fac_q[:, 0:1]).then_inc(s["q2_copied"], 1)
                    at(act, z_exp[2], b)
                    sc.activation(gate_l[:, 2, :], gate_l[:, 2, :], ACT.Ln, bias=1.0).then_inc(z_ln[2], 1)
                    at(act, s["k1_made"], b)
                    at(act, s["kt1_made"], b - 1)
                    sc.copy(k1[:, :], bank[3][:, :]).then_inc(s["k1_copied"], 1)
                    at(act, z_min[1], b)
                    sc.activation(gate_l[:, 1, :], gate_l[:, 1, :], ACT.Exp).then_inc(z_exp[1], 1)
                    at(act, z_exp[1], b)
                    sc.activation(gate_l[:, 1, :], gate_l[:, 1, :], ACT.Ln, bias=1.0).then_inc(z_ln[1], 1)
                    at(act, s["k2_subbed"], b)
                    sc.activation(k2_exp[:, :], k2_exp[:, :], ACT.Exp).then_inc(s["k2_exped"], 1)
                    at(act, l_made[2], b)
                    at(act, s["silu_made"], b - 1)
                    sc.activation(sig, gate_l[:, 2, :], ACT.Exp, scale=-1.0).then_inc(s["sig_made"], 1)
                if live(b):
                    at(act, s["gt1_made"], b)
                    at(act, s["q1_turned"], b - 1)
                    at(act, s["kt1_made"], b - 1)
                    sc.activation(e1p[:, :], bank[0][:, :], ACT.Exp)
                    sc.activation(e1m[:, :], bank[0][:, :], ACT.Exp, scale=-1.0).then_inc(s["gt1_exped"], 1)
                    at(act, s["gt2_made"], b)
                    at(act, s["q2_turned"], b - 1)
                    at(act, s["kt2_made"], b - 1)
                    sc.activation(e2p[:, :], bank[1][:, :], ACT.Exp)
                    sc.activation(e2m[:, :], bank[1][:, :], ACT.Exp, scale=-1.0).then_inc(s["gt2_exped"], 1)
                if live(c):
                    summed(act, c)
                    at(act, s["o_turned"], c - 1)
                    sc.activation(o_sq[:, :], o[:, :], ACT.Square).then_inc(s["o_sq_made"], 1)
                if live(a):
                    at(act, s["dep_made"], a)
                    at(act, s["dep_scaled"], a - 2)
                    sc.copy(depool[:, pa, :], bank[5][:, :]).then_inc(s["dep_copied"], 1)
                if live(b):
                    at(act, s["v_made"], b)
                    at(act, s["kvd_made"], b - 2)
                    at(act, s["onehot_made"], b)
                    sc.copy(v[:, pb, :], bank[3][:, :])
                    at(act, s["kv1_made"], b - 1)
                    for e in range(NE):
                        last = sc.mul(v_e[:, e, :], bank[3][:, :], onehot[:, e:e + 1])
                    last.then_inc(s["v_copied"], 1)
                    at(act, s["dec_made"], b)
                    at(act, s["state_made"], b - 2)
                    at(act, s["dec_kept"], b - 2)
                    dv = dec[:, pb, :, :, :].rearrange("p j a s -> p a j s")
                    sc.activation(dv[:, :, :, 0:1], bank[2][:, 0:2 * PAIRS].rearrange("p (a j s) -> p a j s", a=PAIRS, j=2),
                                  ACT.Exp)
                    for j in range(2):
                        last = sc.activation(dv[:, :, j, 1:SLOTS],
                                      bank[2][:, 8:8 + 2 * PAIRS * NE].rearrange("p (a j s) -> p a j s", a=PAIRS, j=2)[:, :, j, :],
                                      ACT.Exp)
                    last.then_inc(s["dec_exped"], 1)
                if live(c):
                    at(act, s["o_turned"], c)
                    at(act, s["y_made"], c - 1)
                    sc.copy(o_t[:, :, :], bank[4][:, :].rearrange("p (c t) -> p c t", c=KC)).then_inc(s["o_t_made"], 1)
                if live(b):
                    at(act, s["q1_turned"], b)
                    at(act, s["o_made"], b - 1)
                    sc.copy(q1_t[:, :, :], bank[3][:, :].rearrange("p (a t) -> p a t", a=PAIRS)).then_inc(s["q1_t_made"], 1)
                    at(act, s["k1_turned"], b)
                    sc.copy(k1_t[:, :, :], bank[6][:, :].rearrange("p (a t) -> p a t", a=PAIRS)).then_inc(s["k1_t_made"], 1)
                if live(b):
                    at(act, s["q2_turned"], b)
                    sc.copy(q2_t[:, :, :], bank[5][:, :].rearrange("p (a t) -> p a t", a=PAIRS)).then_inc(s["q2_t_made"], 1)
                if live(a):
                    at(act, s["xn_turned"], a)
                    at(act, s["v_made"], a - 1)
                    turned = bank[1][:, :].rearrange("p (c t) -> p c t", c=KC)
                    sc.copy(xn_hi[:, :, :], turned).then_inc(s["xn_hi_made"], 1)
                if live(b):
                    at(act, s["k2_turned"], b)
                    sc.copy(k2_t[:, :, :], bank[0][:, :].rearrange("p (a t) -> p a t", a=PAIRS)).then_inc(s["k2_t_made"], 1)

            run(act, step)

        @block.tensor
        def _(pe):
            te = nc.tensor
            mm = te.matmul
            pe.wait_ge(s["consts_selected"], SELECTED)
            pe.wait_ge(s["lens_float"], 1)
            te.transpose(bank[0][:, 0:NCOL], lens_f, ident[0:NCOL, 0:NCOL]).then_inc(s["lens_turned"], 1)
            pe.wait_ge(s["lens_turned"], 2)
            mm(bank[1][:, 0:NCOL], triu[:, :], lens_t, start=True, stop=True)
            mm(bank[2][:, 0:NCOL], ones[:, :], lens_t, start=True, stop=True).then_inc(s["lens_summed"], 1)
            for b in range(B):
                pe.wait_ge(s["hot_ready"], b + 1)
                for k in range(LC):
                    last = mm(bank[3][:, b * TB:(b + 1) * TB], lo_hot[b % 2][:, k, :], hi_hot[:, b * LC + k, :],
                              start=(k == 0), stop=(k == LC - 1))
                last.then_inc(s["hot_used"], 1)
            pe.wait_ge(s["counts_ready"], 1)
            mm(bank[4][:, 0:NT], ones[:, :], bound[:, 0:NT], start=True, stop=True).then_inc(s["totals_ready"], 1)
            pe.wait_ge(s["weights_in"], 16 * WEIGHTS)
            pe.wait_ge(s["tables_ready"], 2)
            for k in range(KC):
                for m in range(KC):
                    last = te.transpose(bank[4 + k][:, m * P:(m + 1) * P], w_in_rows[:, m, k * P:(k + 1) * P], ident[:, :])
            last.then_inc(s["w_in_turned"], 1)
            pe.wait_ge(s["small_in"], 16 * SMALL)
            pe.wait_ge(s["g_scaled"], 1)

            def rows(j):
                return slice(DK * j, DK * j + DK)

            def turn(bk, src):
                for k in range(KC):
                    last = te.transpose(bank[bk][:, k * P:(k + 1) * P], src[:, k * P:(k + 1) * P], ident[:, :])
                return last

            def product(bk, lhs_t, w):
                for k in range(KC):
                    last = mm(bank[bk][:, :], lhs_t[:, k, :], w[:, k, :], start=(k == 0), stop=(k == KC - 1))
                return last

            def times(dst, x_hi, x_lo, w_hi, w_lo, k):
                mm(dst, x_hi[:, k, :], w_hi[:, k, :], start=(k == 0), stop=False)
                mm(dst, x_hi[:, k, :], w_lo[:, k, :], start=False, stop=False)
                return mm(dst, x_lo[:, k, :], w_hi[:, k, :], start=False, stop=(k == KC - 1))

            def step(i, u):
                a, b, c = i, i - 1, i - 2
                pa, pb, pc = u, 1 - u, u
                def attention(kt, qt, bk, pr):
                    for j in range(2):
                        last = mm(bank[bk + j][:, pr * P:(pr + 1) * P], kt[rows(j), pr, :], qt[rows(j), pr, :],
                                  start=True, stop=True)
                    return last

                if live(c):
                    at(pe, s["q1_t_made"], c)
                    at(pe, s["k1_t_made"], c)
                    for pr in range(PAIRS):
                        last = attention(k1_t, q1_t, 3, pr)
                    last.then_inc(s["a1_made"], 1)
                if live(b):
                    at(pe, s["xn_lo_made"], b)
                    at(pe, s["res_made"], b - 2)
                    for k in range(KC):
                        last = times(bank[2][:, 0:2 * P + NE], xn_hi, xn_lo, low_hi, low_lo, k)
                    last.then_inc(s["low_made"], 1)
                if live(c):
                    at(pe, s["q2_t_made"], c)
                    at(pe, s["k2_t_made"], c)
                    at(pe, s["o_t_made"], c - 1)
                    for pr in range(PAIRS - 1):
                        attention(k2_t, q2_t, 5, pr)
                if live(b):
                    at(pe, s["x1_made"], b)
                    at(pe, s["low_out"], b)
                    for h in range(2):
                        last = te.transpose(bank[7][:, h * P:(h + 1) * P], low_tok[:, h * P:(h + 1) * P], ident[:, :])
                    last.then_inc(s["low_turned"], 1)
                if live(c):
                    attention(k2_t, q2_t, 5, PAIRS - 1).then_inc(s["a2_made"], 1)
                if live(a):
                    at(pe, s["xhat_made"], a)
                    at(pe, s["k2_t_made"], a - 2)
                    turn(0, xhat).then_inc(s["xhat_turned"], 1)
                    at(pe, s["tri_made"], a)
                    at(pe, s["xn_lo_made"], a - 1)
                    mm(bank[1][:, 0:P], ones_b[:, :], tri_bound[:, :], start=True, stop=True).then_inc(s["cum_made"], 1)
                if live(b):
                    at(pe, s["low_copied"], b)
                    for k in range(KC):
                        last = times(bank[7][:, :], xn_hi, xn_lo, wq_hi, wq_lo, k)
                    last.then_inc(s["q1_made"], 1)
                    at(pe, s["onehot_made"], b)
                    at(pe, s["dist_made"], b + 1)
                    te.transpose(bank[1][0:NE, P:2 * P], onehot[:, :], ident[:, :]).then_inc(s["hot_turned"], 1)
                def head_cols(pr, j):
                    return slice((2 * pr + j) * DK, (2 * pr + j + 1) * DK)

                def dense(j):
                    for pr in range(PAIRS):
                        last = mm(bank[6][:, head_cols(pr, j)], q1_t[rows(j), pr, :], state[rows(j), pr, 0, :],
                                  start=(j == 0 and pr == 0), stop=(j == 1), skip_group_check=True)
                    return last

                def own(pr, j):
                    mm(bank[6][:, head_cols(pr, j)], att1[:, j, pr, :], v[:, pc, head_cols(pr, j)],
                       start=False, stop=(j == 0), skip_group_check=True)

                def routed(half, banks):
                    for pr in (2 * half, 2 * half + 1):
                        for j in range(2):
                            last = mm(bank[banks[j]][:, (pr % 2) * NE * DK:(pr % 2 + 1) * NE * DK], q2_t[rows(j), pr, :],
                                      state[rows(j), pr, 1:SLOTS, :], start=True, stop=True)
                    return last

                if live(b):
                    at(pe, s["l_read"], b)
                    at(pe, s["xhat_lo_made"], b + 1)
                    mm(bank[0][:, :], low[64:64 + GLR + 1, P:2 * P], w_up[64:64 + GLR + 1, 1, :],
                       start=True, stop=True).then_inc(z_made[0], 1)
                if live(c):
                    at(pe, s["a2o_masked"], c)
                    at(pe, s["state_first"], c)
                    dense(0).then_inc(s["o_even_made"], 1)

                def keys_and_own(k):
                    if live(b):
                        last = times(bank[3][:, :], xn_hi, xn_lo, wk_hi, wk_lo, k)
                        if k == KC - 1:
                            last.then_inc(s["k1_made"], 1)
                    if live(c):
                        if k % 2 == 0:
                            pe.wait_ge(s["att_summed"], 2 * c + 1 + k // 2)
                        own(2 * (k % 2), k // 2)
                        own(2 * (k % 2) + 1, k // 2)

                if live(b):
                    at(pe, s["a1e_masked"], b - 1)
                keys_and_own(0)
                if live(b):
                    mm(bank[2][:, :], low[0:LORA, P:2 * P], w_up[0:LORA, 1, :],
                       start=True, stop=True).then_inc(z_made[2], 1)
                    at(pe, s["hot_t_made"], b)
                    mm(bank[1][:, 2 * P:3 * P], onehot_t[:, :], onehot_t[:, :], start=True, stop=True).then_inc(s["same_made"], 1)
                keys_and_own(1)
                if live(b):
                    at(pe, s["a2e_masked"], b - 1)
                    mm(bank[5][:, :], low[64:P, 0:P], w_up[64:P, 0, :], start=True, stop=True).then_inc(s["k2_made"], 1)
                    at(pe, s["a1o_masked"], b - 1)
                    mm(bank[4][:, :], low[0:LORA, 0:P], w_up[0:LORA, 0, :], start=True, stop=True).then_inc(s["q2_made"], 1)
                keys_and_own(2)
                if live(b):
                    at(pe, s["same_used"], b)
                    mm(bank[1][:, :], low[96:96 + GLR + 1, P:2 * P], w_up[96:96 + GLR + 1, 1, :],
                       start=True, stop=True).then_inc(z_made[1], 1)
                keys_and_own(3)
                if live(c):
                    at(pe, s["o_even_made"], c)
                    dense(1).then_inc(s["o_base_made"], 1)
                if live(c):
                    at(pe, s["q1_copied"], c + 1)
                    at(pe, s["k1_copied"], c + 1)
                    routed(0, (7, 3)).then_inc(s["o_half_made"], 1)
                if live(b):
                    at(pe, l_made[0], b)
                    mm(bank[0][:, :], cum_mat[:, :], gate_l[:, 0, :], start=True, stop=True).then_inc(s["gt1_made"], 1)
                if live(c):
                    at(pe, s["q2_copied"], c + 1)
                    at(pe, s["k2_subbed"], c + 1)
                    routed(1, (4, 5)).then_inc(s["o_made"], 1)
                if live(b):
                    at(pe, l_made[1], b)
                    mm(bank[1][:, :], cum_mat2[:, :], gate_l[:, 1, :], start=True, stop=True).then_inc(s["gt2_made"], 1)
                if live(b):
                    if live(c):
                        summed(pe, c, NE)
                    at(pe, s["k1_copied"], b)
                    at(pe, l_made[2], b)
                    at(pe, s["g_normed"], b)
                    for k in range(KC):
                        last = times(bank[3][:, :], xn_hi, xn_lo, wv_hi, wv_lo, k)
                        if k == KC - 1:
                            last.then_inc(s["v_made"], 1)
                        mm(bank[2][:, 2 * k:2 * k + 2], gate_l[:, 0, k * P:(k + 1) * P], half_z[:, :],
                           start=True, stop=True)
                        last = mm(bank[2][:, 8 + 8 * k:16 + 8 * k], gate_l[:, 1, k * P:(k + 1) * P],
                                  z2_half[:, :, :].rearrange("p j e -> p (j e)"), start=True, stop=True)
                    last.then_inc(s["dec_made"], 1)
                if live(c):
                    summed(pe, c)
                if live(a):
                    at(pe, s["dep_w_made"], a)
                    at(pe, s["dep_copied"], a - 1)
                    mm(bank[5][:, :], w_depool[:, :], ctx[:, pa, 0:D], start=True, stop=False)
                    mm(bank[5][:, :], w_carry[96:P, :], depool[96:P, 1 - pa, :], start=False, stop=True,
                       tile_position=(96, 0)).then_inc(s["dep_made"], 1)
                if live(c):
                    for bk, prs, made in ((4, (0, 1), s["kv0_made"]), (5, (2, 3), s["kv1_made"])):
                        if bk == 5:
                            at(pe, s["dep_copied"], c + 2)
                        for n, pr in enumerate(prs):
                            for j in range(2):
                                hd = slice((2 * pr + j) * DK, (2 * pr + j + 1) * DK)
                                last = mm(bank[bk][rows(j), n * NE * DK:(n + 1) * NE * DK], kt2[:, hd],
                                          v_e[:, :, hd], start=True, stop=True)
                        last.then_inc(made, 1)
                if live(a):
                    at(pe, s["xhat_lo_made"], a)
                    if not live(c):
                        at(pe, s["q1_copied"], a - 1)
                for k in range(KC):
                    if k == KC - 1 and live(c):
                        at(pe, s["o_n_made"], c)
                        at(pe, s["kv0_added"], c)
                        turn(4, o_n).then_inc(s["o_turned"], 1)
                    if live(a):
                        last = times(bank[7][:, :], xhat_hi, xhat_lo, w_in_hi, w_in_lo, k)
                        if k == KC - 1:
                            last.then_inc(s["w_made"], 1)
                    if live(c):
                        for j in range(2):
                            last = mm(bank[6][rows(j), k * DK:(k + 1) * DK], kt1[:, pc, head_cols(k, j)],
                                      v[:, pc, head_cols(k, j)], start=True, stop=True)
                        if k == KC - 1:
                            last.then_inc(s["kvd_made"], 1)
                if live(b):
                    at(pe, s["qt1_made"], b)
                    at(pe, s["v_copied"], b)
                    turn(3, e1p).then_inc(s["q1_turned"], 1)
                    at(pe, s["kt1_made"], b)
                    at(pe, s["state_added"], b - 1)
                    turn(6, kt1[:, pb]).then_inc(s["k1_turned"], 1)
                if live(b):
                    at(pe, s["qt2_made"], b)
                    at(pe, s["dep_copied"], b + 1)
                    at(pe, s["kv1_added"], b - 1)
                    turn(5, e2p).then_inc(s["q2_turned"], 1)
                if live(c):
                    at(pe, s["o_t_made"], c)
                    at(pe, s["dec_exped"], c + 1)
                    product(2, o_t, wo_s).then_inc(s["y_made"], 1)
                if live(a):
                    at(pe, s["xn_made"], a)
                    at(pe, s["gt2_exped"], a - 1)
                    turn(1, xn).then_inc(s["xn_turned"], 1)
                if live(b):
                    at(pe, s["kt2_made"], b)
                    at(pe, s["gt1_exped"], b)
                    turn(0, kt2).then_inc(s["k2_turned"], 1)

            run(pe, step)

        @block.vector
        def _(dve):
            ve = nc.vector
            n = 0

            def then(ins):
                nonlocal n
                n += 1
                ins.then_inc(s["prologue_step"], 1)
                dve.wait_ge(s["prologue_step"], n)

            dve.wait_ge(s["consts_made"], 1)
            dve.wait_ge(s["lens_in"], 16 * (B + 1))
            ve.tensor_copy(lens_f, lens_i).then_inc(s["lens_float"], 1)
            dve.wait_ge(s["lens_turned"], 1)
            ve.tensor_copy(lens_t, bank[0][:, 0:NCOL]).then_inc(s["lens_turned"], 1)
            dve.wait_ge(s["lens_summed"], 1)

            def by_batch(ap):
                return ap[:, 0:B * LCF].rearrange("p (b c) -> p b c", b=B), ap[:, B * LCF:NCOL].unsqueeze(2)

            for dst, bk in ((ends, 1), (totals, 2)):
                full, tail = by_batch(bank[bk])
                ve.tensor_copy(dst[:, :, 0:LCF], full)
                then(ve.tensor_copy(dst[:, :, LCF:LC], tail))
            then(ve.memset(offs[:, :, 0:1], -1.0))
            for k in range(1, LC):
                then(ve.tensor_tensor(offs[:, :, k:k + 1], offs[:, :, k - 1:k], totals[:, :, k - 1:k], ALU.add))
            flat_ends = ends.rearrange("p b c -> p (b c)")
            then(ve.tensor_tensor(flat_ends, flat_ends, offs.rearrange("p b c -> p (b c)"), ALU.add))
            then(ve.tensor_scalar(wrapped, flat_ends, 0.0, float(S), ALU.is_lt, ALU.mult))
            then(ve.tensor_tensor(flat_ends, flat_ends, wrapped, ALU.add))
            then(ve.tensor_tensor(reached, flat_ends.unsqueeze(2).to_broadcast([P, NCOL, TB + 1]),
                                  thr.unsqueeze(1).to_broadcast([P, NCOL, TB + 1]), ALU.is_ge))
            then(ve.tensor_tensor(hi_hot, reached[:, :, 0:TB], reached[:, :, 1:TB + 1], ALU.subtract))
            then(ve.tensor_reduce(hi_no.unsqueeze(2), reached[:, :, 1:TB + 1], AX.X, ALU.add))
            then(ve.scalar_tensor_tensor(lo_no, hi_no, float(-P), flat_ends, ALU.mult, ALU.add))
            for b in range(B):
                if b >= 2:
                    dve.wait_ge(s["hot_used"], b - 1)
                ve.tensor_tensor(lo_hot[b % 2], lo_no[:, b * LC:(b + 1) * LC].unsqueeze(2).to_broadcast([P, LC, P]),
                                 col_no.unsqueeze(1).to_broadcast([P, LC, P]), ALU.is_equal).then_inc(s["hot_ready"], 1)
            dve.wait_ge(s["hot_used"], B)
            ve.tensor_scalar(bound[:, 0:NT], bank[3][:, 0:NT], 1.0, None, ALU.min).then_inc(s["counts_ready"], 1)
            dve.wait_ge(s["totals_ready"], 1)
            then(ve.tensor_copy(tile_tot, bank[4][:, 0:NT].rearrange("p (b t) -> p b t", b=B)))
            then(ve.memset(before[:, :, 0:1], 0.0))
            for t in range(1, TB):
                then(ve.tensor_tensor(before[:, :, t:t + 1], before[:, :, t - 1:t], tile_tot[:, :, t - 1:t], ALU.add))
            flat_before = before.rearrange("p b t -> p (b t)")
            then(ve.tensor_tensor(row_first, before, row_start, ALU.add))
            ve.tensor_copy(first_row[:, :], row_first[0:1].rearrange("p b t -> p (b t)")).then_inc(s["tables_ready"], 1)
            then(ve.tensor_scalar(started[:, 0:NT], flat_before, 1.0, None, ALU.min))
            then(ve.tensor_scalar(unstarted[:, 0:NT], started[:, 0:NT], -1.0, 1.0, ALU.mult, ALU.add))
            dve.wait_ge(s["consts_selected"], SELECTED)
            ve.memset(onehot[:, :], 0.0).then_inc(s["tables_ready"], 1)
            dve.wait_ge(s["weights_rounded"], 3 * KC)
            for stage, hi, lo in zip(w_stage, (wq_hi, wk_hi, wv_hi), (wq_lo, wk_lo, wv_lo)):
                for k in range(KC):
                    ve.tensor_tensor(lo[:, k, :], stage[k][:, :], hi[:, k, :].bitcast(F32), ALU.subtract)
            dve.wait_ge(s["weights_rounded"], 3 * KC + 1)
            ve.tensor_tensor(low_lo[:, :, 0:2 * P], w_low, low_hi[:, :, 0:2 * P].bitcast(F32), ALU.subtract)
            then(ve.tensor_tensor(low_lo[:, :, 2 * P:2 * P + NE], we_s[:, :, :],
                                  low_hi[:, :, 2 * P:2 * P + NE].bitcast(F32), ALU.subtract))
            dve.wait_ge(s["small_in"], 16 * SMALL)
            ve.tensor_scalar(g_init_s[:, :], g_init_s[:, :], B_COEF, None, ALU.mult)
            dve.wait_ge(s["w_in_turned"], 1)
            for k in range(KC):
                last = ve.tensor_scalar(w_stage[1][k][:, :], bank[4 + k][:, :], g_res_s[:, k:k + 1], None, ALU.mult)
            then(last)
            for k in range(KC):
                last = ve.tensor_copy(w_in_hi[:, k, :], w_stage[1][k][:, :])
            then(last)
            for k in range(KC):
                last = ve.tensor_tensor(w_in_lo[:, k, :], w_stage[1][k][:, :], w_in_hi[:, k, :].bitcast(F32), ALU.subtract)
            last.then_inc(s["g_scaled"], 1)

            def step(i, u):
                a, b, c = i, i - 1, i - 2
                pa, pb, pc = u, 1 - u, u
                if live(a):
                    moved(dve, x_in, a, pa)
                    ve.bn_stats(stat[:, :], xs[:, pa, :]).then_inc(s["x_stats"], 1)
                    at(dve, s["cum_made"], a - 1)
                    ve.tensor_scalar(tri_bound[:, :], triu_b[:, :], bound[:, bass.ds(a, 1)], None,
                                     ALU.mult).then_inc(s["tri_made"], 1)
                    at(dve, s["ctx_sq"], a)
                    at(dve, s["a_rs"], a - 1)
                    at(dve, s["x_stats"], a)
                    ve.tensor_scalar(var_a[:, 1:2], ctx_ss[:, :], 1.0 / DG, RMS_EPS, ALU.mult,
                                     ALU.add).then_inc(s["ctx_var"], 1)
                    ve.bn_aggr(mv[:, :], stat[:, :]).then_inc(s["x_mean"], 1)
                    at(dve, s["x_mean"], a)
                    ve.tensor_scalar(var_a[:, 0:1], mv[:, 1:2], 1.0 + RMS_EPS, RMS_EPS * LN_EPS, ALU.mult,
                                     ALU.add).then_inc(s["x_var"], 1)
                if live(b):
                    at(dve, s["low_made"], b)
                    at(dve, s["low_turned"], b - 1)
                    ve.tensor_copy(low_tok[:, :], bank[2][:, 0:2 * P]).then_inc(s["low_out"], 1)
                    logits = bank[2][:, 2 * P:2 * P + NE]
                    ve.tensor_reduce(l_max[:, :], logits, AX.X, ALU.max).then_inc(s["l_max_made"], 1)
                    at(dve, s["l_max_made"], b)
                    at(dve, s["l_exp_made"], b - 1)
                    ve.tensor_scalar(l_sub[:, :], logits, l_max[:, 0:1], None, ALU.subtract).then_inc(s["l_sub_made"], 1)
                    ve.scalar_tensor_tensor(l_rank[:, :], logits, l_max[:, 0:1], rank[:, :], ALU.is_equal,
                                            ALU.mult).then_inc(s["l_read"], 1)
                if live(a):
                    at(dve, s["a_rs"], a)
                    at(dve, s["xn_turned"], a - 1)
                    ve.tensor_scalar(xhat[:, :], xs[:, pa, :], mv[:, 0:1], rs_a[:, 0:1], ALU.subtract,
                                     ALU.mult).then_inc(s["xhat_made"], 1)
                if live(b):
                    at(dve, s["l_read"], b)
                    ve.tensor_reduce(l_best[:, :], l_rank[:, :], AX.X, ALU.max).then_inc(s["l_best_made"], 1)
                    at(dve, s["low_turned"], b)
                    at(dve, s["q2_made"], b - 1)
                    at(dve, s["k2_made"], b - 1)
                    ve.tensor_copy(low[:, 0:P], bank[7][:, 0:P])
                    ve.tensor_scalar(low[:, P:2 * P], bank[7][:, P:2 * P], bias_rows[:, 0:1], None,
                                     ALU.add).then_inc(s["low_copied"], 1)
                tri = triu[:, :].unsqueeze(1).to_broadcast([P, PAIRS, P])
                if live(c):
                    at(dve, s["o_made"], c - 1)
                    at(dve, s["a1_made"], c)
                    for j, masked in ((0, s["a1e_masked"]), (1, s["a1o_masked"])):
                        ve.tensor_tensor(att1[:, j, :, :], bank[3 + j][:, :].rearrange("p (a t) -> p a t", a=PAIRS),
                                         tri, ALU.mult).then_inc(masked, 1)
                if live(b):
                    at(dve, s["l_best_made"], b)
                    at(dve, s["v_copied"], b - 1)
                    at(dve, s["hot_turned"], b - 1)
                    ve.tensor_scalar(onehot_late[:, pb, :], l_rank[:, :], l_best[:, 0:1], None, ALU.is_equal)
                    ve.tensor_scalar(onehot[:, :], l_rank[:, :], l_best[:, 0:1], None, ALU.is_equal).then_inc(s["onehot_made"], 1)
                if live(a):
                    at(dve, s["cum_made"], a)
                    at(dve, s["carry_made"], a - 1)
                    at(dve, s["past_made"], a - 1)
                    ve.tensor_scalar(dist[:, :], bank[1][:, 0:P], unstarted[:, bass.ds(a, 1)], row_no[:, 0:1], ALU.max,
                                     ALU.subtract).then_inc(s["dist_made"], 1)
                if live(a):
                    at(dve, s["xhat_t_made"], a)
                    ve.tensor_tensor(xhat_lo[:, :, :], bank[0][:, :].rearrange("p (c t) -> p c t", c=KC),
                                     xhat_hi[:, :, :].bitcast(F32), ALU.subtract).then_inc(s["xhat_lo_made"], 1)
                if live(c):
                    same = mask2[:, pc, :].unsqueeze(1).to_broadcast([P, PAIRS, P])
                    at(dve, s["a2_made"], c)
                    for j, masked in ((0, s["a2e_masked"]), (1, s["a2o_masked"])):
                        ve.tensor_tensor(att2[:, j, :, :], bank[5 + j][:, :].rearrange("p (a t) -> p a t", a=PAIRS),
                                         same, ALU.mult).then_inc(masked, 1)
                if live(a):
                    at(dve, s["dist_made"], a)
                    at(dve, s["decay_made"], a - 1)
                    ve.tensor_scalar(dist_p[:, :], dist[:, :], 0.0, None, ALU.max).then_inc(s["dist_pos"], 1)
                    at(dve, s["dep_w_made"], a - 1)
                    at(dve, s["a_rs"], a)
                    ve.tensor_scalar(in_past[:, :], dist[:, :], 0.0, rs_a[:, 1:2], ALU.is_ge,
                                     ALU.mult).then_inc(s["past_made"], 1)
                if live(b):
                    at(dve, s["l_exp_made"], b)
                    at(dve, s["kt2_made"], b - 1)
                    ve.reciprocal(fac[:, :], l_sum[:, :]).then_inc(s["fac_made"], 1)
                    at(dve, s["hot_turned"], b)
                    at(dve, s["same_made"], b - 1)
                    ve.tensor_copy(onehot_t[:, :], bank[1][0:NE, P:2 * P]).then_inc(s["hot_t_made"], 1)
                    at(dve, s["fac_made"], b)
                    at(dve, s["q2_copied"], b - 1)
                    ve.tensor_scalar(fac_q[:, :], fac[:, :], SCALE, None, ALU.mult).then_inc(s["facq_made"], 1)
                    for j in (0, 2):
                        at(dve, z_made[j], b)
                        at(dve, (s["dec_made"], s["dec_made"], s["silu_made"])[j], b - 1)
                        ve.tensor_scalar(gate_l[:, j, :], bank[j][:, :], -1.0, 40.0, ALU.mult, ALU.min).then_inc(z_min[j], 1)
                if live(b):
                    at(dve, s["same_made"], b)
                    at(dve, s["a2o_masked"], b - 2)
                    at(dve, s["gt2_made"], b - 1)
                    ve.tensor_tensor(mask2[:, pb, :], bank[1][:, 2 * P:3 * P], triu[:, :], ALU.mult)
                    ve.tensor_tensor(cum_mat2[:, :], bank[1][:, 2 * P:3 * P], cum_mat[:, :], ALU.mult).then_inc(s["same_used"], 1)
                    at(dve, s["dec_made"], b - 1)
                    at(dve, s["onehot_made"], b)
                    ve.tensor_tensor(z2_half[:, :, :], onehot[:, :].unsqueeze(1).to_broadcast([P, 2, NE]),
                                     half_z[:, :].unsqueeze(2).to_broadcast([P, 2, NE]), ALU.mult)
                if live(a):
                    at(dve, s["past_made"], a)
                    at(dve, s["decay_made"], a)
                    at(dve, s["dep_made"], a - 1)
                    ve.tensor_tensor(w_depool[:, :], decay_w[:, :], in_past[:, :], ALU.mult)
                    at(dve, s["carry_made"], a)
                    ve.tensor_scalar(w_carry[96:P, :], carry_y[96:P, :], started[96:P, bass.ds(a, 1)], last_row[96:P, 0:1],
                                     ALU.mult, ALU.mult).then_inc(s["dep_w_made"], 1)
                if live(b):
                    at(dve, s["k2_made"], b)
                    at(dve, s["k2d_made"], b - 1)
                    at(dve, s["k2_summed"], b - 1)
                    ve.tensor_reduce(k2_max[:, :], heads(bank[5][:, :]), AX.X, ALU.max).then_inc(s["k2_maxed"], 1)
                    at(dve, z_made[1], b)
                    at(dve, s["dec_made"], b - 1)
                    ve.tensor_scalar(gate_l[:, 1, :], bank[1][:, :], -1.0, 40.0, ALU.mult, ALU.min).then_inc(z_min[1], 1)
                    at(dve, s["k2_maxed"], b)
                    ve.tensor_tensor(heads(k2_exp[:, :]), heads(bank[5][:, :]), over_heads(k2_max[:, :]),
                                     ALU.subtract).then_inc(s["k2_subbed"], 1)
                    for j in (0, 2, 1):
                        at(dve, z_ln[j], b)
                        ve.scalar_tensor_tensor(gate_l[:, j, :], bank[j][:, :], -1.0, gate_l[:, j, :], ALU.mult,
                                                ALU.max).then_inc(l_made[j], 1)
                for half, banks, made in ((0, (7, 3), s["o_half_made"]), (1, (4, 5), s["o_made"])):
                    if live(c):
                        at(dve, s["o_n_made"], c - 1)
                        at(dve, made, c)
                        for e in range(NE):
                            if e > 0:
                                summed(dve, c, NE * half + e)
                            for j, bk in enumerate(banks):
                                part = o[:, :].rearrange("p (a j d) -> p a j d", a=PAIRS, j=2)[
                                    :, 2 * half:2 * half + 2, j, :]
                                one = bank[bk][:, :].rearrange("p (a e d) -> p a e d", a=2, e=NE)[:, :, e, :]
                                if e == 0:
                                    last = ve.tensor_scalar(part, one, onehot_late[:, pc, e:e + 1], None, ALU.mult)
                                else:
                                    last = ve.scalar_tensor_tensor(part, one, onehot_late[:, pc, e:e + 1], part,
                                                                   ALU.mult, ALU.add)
                            last.then_inc(s["o_sum"], 1)
                    if half == 0 and live(b):
                        at(dve, s["silu_made"], b - 1)
                        ve.tensor_tensor(heads(g_norm[:, :]), heads(bank[2][:, :]),
                                         norm_s[:, :].unsqueeze(1).to_broadcast([P, H, DK]), ALU.mult).then_inc(s["g_normed"], 1)
                if live(c):
                    at(dve, s["o_base_made"], c)
                    summed(dve, c, 2 * NE)
                    ve.tensor_tensor(o[:, :], o[:, :], bank[6][:, :], ALU.add).then_inc(s["o_sum"], 1)
                if live(b):
                    at(dve, s["k2_exped"], b)
                    ve.tensor_reduce(k2_sum[:, :], heads(k2_exp[:, :]), AX.X, ALU.add).then_inc(s["k2_summed"], 1)
                    at(dve, s["k2_summed"], b)
                    ve.reciprocal(k2_rec[:, :], k2_sum[:, :]).then_inc(s["k2_reced"], 1)
                    at(dve, s["k2_reced"], b)
                    at(dve, s["kt2_made"], b - 1)
                    ve.tensor_scalar(k2_fac[:, :], k2_rec[:, :], fac[:, 0:1], None, ALU.mult).then_inc(s["k2_faced"], 1)
                    at(dve, s["gt1_exped"], b)
                    at(dve, s["q1_copied"], b)
                    ve.tensor_tensor(e1p[:, :], q1[:, :], e1p[:, :], ALU.mult).then_inc(s["qt1_made"], 1)
                    at(dve, s["gt2_exped"], b)
                    at(dve, s["q2_copied"], b)
                    at(dve, s["q2_turned"], b - 1)
                    ve.tensor_tensor(e2p[:, :], q2[:, :], e2p[:, :], ALU.mult).then_inc(s["qt2_made"], 1)
                if live(c):
                    at(dve, s["o_sq_made"], c)
                    at(dve, s["o_var_made"], c - 1)
                    ve.tensor_reduce(o_ss[:, :], heads(o_sq[:, :]), AX.X, ALU.add).then_inc(s["o_summed"], 1)
                    at(dve, s["o_summed"], c)
                    at(dve, s["o_rs_made"], c - 1)
                    ve.tensor_scalar(o_var[:, :], o_ss[:, :], 1.0 / DK, LN_EPS, ALU.mult, ALU.add).then_inc(s["o_var_made"], 1)
                    at(dve, s["kv0_made"], c)
                    kept = state[:, 0:2, 1:SLOTS, :]
                    ve.tensor_tensor(kept, kept, bank[4][:, :].rearrange("p (a e d) -> p a e d", a=2, e=NE),
                                     ALU.add).then_inc(s["kv0_added"], 1)
                    at(dve, s["kv1_made"], c)
                    kept = state[:, 2:4, 1:SLOTS, :]
                    ve.tensor_tensor(kept, kept, bank[5][:, :].rearrange("p (a e d) -> p a e d", a=2, e=NE),
                                     ALU.add).then_inc(s["kv1_added"], 1)
                    at(dve, s["o_gated_made"], c)
                    at(dve, s["o_rs_made"], c)
                    at(dve, s["o_turned"], c - 1)
                    at(dve, s["o_summed"], c)
                    ve.tensor_tensor(heads(o_n[:, :]), heads(o[:, :]), over_heads(o_rs[:, :]),
                                     ALU.mult).then_inc(s["o_n_made"], 1)
                    at(dve, s["kvd_made"], c)
                    kept = state[:, :, 0, :]
                    ve.tensor_tensor(kept, kept, bank[6][:, 0:PAIRS * DK].rearrange("p (a d) -> p a d", a=PAIRS),
                                     ALU.add).then_inc(s["state_added"], 1)
                if live(b):
                    at(dve, s["dec_exped"], b)
                    at(dve, s["state_first"], b - 2)
                    ve.tensor_scalar(dec_first[:, pb, :, :], dec[:, pb, 0, :, :], keep[:, bass.ds(b, 1)], None,
                                     ALU.mult).then_inc(s["dec_kept"], 1)
                    at(dve, s["k2d_made"], b)
                    at(dve, s["k2_faced"], b)
                    at(dve, s["kv1_made"], b - 1)
                    ve.tensor_tensor(heads(kt2[:, :]), heads(e2m[:, :]), over_heads(k2_fac[:, :]),
                                     ALU.mult).then_inc(s["kt2_made"], 1)
                if live(a):
                    at(dve, s["w_made"], a)
                    at(dve, s["resid_made"], a)
                    at(dve, s["x1_moved"], a - 1)
                    ve.tensor_tensor(x1[:, :], bank[7][:, :], resid[:, :], ALU.add).then_inc(s["x1_made"], 1)
                    at(dve, s["x1_made"], a)
                    ve.bn_stats(stat2[:, :], x1[:, :]).then_inc(s["x1_stats"], 1)
                    at(dve, s["x1_stats"], a)
                    at(dve, s["xn_made"], a - 1)
                    ve.memset(idle[:, :], 0.0)
                    ve.bn_aggr(mv2[:, :], stat2[:, :]).then_inc(s["x1_mean"], 1)
                    at(dve, s["x1_mean"], a)
                    at(dve, s["x1_rs"], a - 1)
                    ve.tensor_scalar(var2[:, :], mv2[:, 1:2], LN_EPS, None, ALU.add).then_inc(s["x1_var"], 1)
                    at(dve, s["x1_rs"], a)
                    at(dve, s["xhat_turned"], a)
                    ve.tensor_scalar(xn[:, :], x1[:, :], mv2[:, 0:1], rs2[:, 0:1], ALU.subtract,
                                     ALU.mult).then_inc(s["xn_made"], 1)
                if live(c):
                    at(dve, s["y_made"], c)
                    at(dve, s["x1_moved"], c)
                    ve.tensor_tensor(x1_late[:, pc, :], bank[2][:, :], x1_late[:, pc, :], ALU.add).then_inc(s["res_made"], 1)
                if live(a):
                    at(dve, s["xn_hi_made"], a)
                    ve.tensor_tensor(xn_lo[:, :, :], bank[1][:, :].rearrange("p (c t) -> p c t", c=KC),
                                     xn_hi[:, :, :].bitcast(F32), ALU.subtract).then_inc(s["xn_lo_made"], 1)

            run(dve, step)


_INS = ['x', 'ctx_2048', 'mask_BxS2_if0', 'L0_xattn_W_in', 'L0_xattn_b_in', 'L0_xattn_g_res', 'L0_xattn_g_init',
        'L0_ffn_Wq', 'L0_ffn_Wk', 'L0_ffn_Wv', 'L0_ffn_Wqa', 'L0_ffn_Wqb', 'L0_ffn_Wka', 'L0_ffn_Wkb',
        'L0_ffn_Wg1a', 'L0_ffn_Wg1b', 'L0_ffn_bg1', 'L0_ffn_Wg2a', 'L0_ffn_Wg2b', 'L0_ffn_bg2', 'L0_ffn_We',
        'L0_ffn_Wga', 'L0_ffn_Wgb', 'L0_ffn_norm_w', 'L0_ffn_Wo']


def kernel(**inputs):
    import numpy as np
    import concourse.bacc as bacc
    from concourse.bass_utils import run_bass_kernel_spmd

    nc = bacc.Bacc("TRN2", target_bir_lowering=False, num_devices=1)
    arrays, args = {}, []
    for name in _INS:
        a = np.ascontiguousarray(inputs[name])
        arrays[f"in_{name}"] = a
        args.append(nc.dram_tensor(f"in_{name}", a.shape, mybir.dt.from_np(a.dtype), kind="ExternalInput").ap())
    out = nc.dram_tensor("out", inputs["x"].shape, F32, kind="ExternalOutput").ap()
    xattn_ffn(nc, *args, out)
    r = run_bass_kernel_spmd(nc, [arrays], core_ids=[0])
    return r.results[0]["out"]
```
